# Optimizing a Trainium2 kernel written in Bass

```python
import numpy as np
import jax
import jax.numpy as jnp

def _softmax(x, axis=-1):
    return jax.nn.softmax(x, axis=axis)

def _gelu(x):
    return jax.nn.gelu(x, approximate=True)

def _silu(x):
    return jax.nn.silu(x)

def _sigmoid(x):
    return jax.nn.sigmoid(x)

def _layernorm(x, axis=-1, eps=1e-05):
    m = jnp.mean(x, axis=axis, keepdims=True)
    v = jnp.var(x, axis=axis, keepdims=True)
    return (x - m) / jnp.sqrt(v + eps)

def _scatter_add(tgt, idx, src, axis=0):
    return tgt.at[idx].add(src)

def _segment_sum(src, seg, n):
    return jax.ops.segment_sum(src, seg, n)
kernel_name = 'mk_prb_d2_jaxref_r8_e65a12'

def setup_inputs(seed: int=0):
    np.random.seed(seed)
    _w = jnp.asarray

    def _L0_attn_setup():
        import jax, jax.numpy as jnp
        import numpy as np
        import math
        D_MODEL = 256
        N_HEADS = 16
        Q_LORA = 192
        KV_LORA = 64
        D_NOPE = 128
        D_ROPE = 64
        D_V = 128
        EPS = 1e-05

        def _layernorm(x, w, b):
            mu = jnp.mean(x, axis=-1, keepdims=True)
            var = jnp.mean(jnp.square(x - mu), axis=-1, keepdims=True)
            return (x - mu) * jax.lax.rsqrt(var + EPS) * w + b

        def _rope_tables(seq_len, dim, dtype):
            inv_freq = 1.0 / 10000.0 ** (np.arange(0, dim, 2, dtype=np.float32) / dim)
            t = np.arange(seq_len, dtype=np.float32)
            freqs = np.outer(t, inv_freq)
            emb = np.concatenate([freqs, freqs], -1)
            return (jnp.asarray(np.cos(emb), dtype), jnp.asarray(np.sin(emb), dtype))

        def _rotate_half(x):
            x1, x2 = jnp.split(x, 2, axis=-1)
            return jnp.concatenate([-x2, x1], axis=-1)

        def _apply_rope(x, cos, sin):
            c = cos[None, :, None, :]
            s = sin[None, :, None, :]
            return x * c + _rotate_half(x) * s
        key = jax.random.key(seed)
        ks = jax.random.split(key, 8)

        def lin(k, out_d, in_d):
            return jax.random.normal(k, (out_d, in_d), jnp.float32) * (1.0 / math.sqrt(in_d))
        B, S = (2, 256)
        return {'hidden_states': jax.random.normal(ks[0], (B, S, D_MODEL), jnp.float32), 'q_a_w': lin(ks[1], Q_LORA, D_MODEL), 'q_a_ln_w': jnp.ones((Q_LORA,), jnp.float32), 'q_a_ln_b': jnp.zeros((Q_LORA,), jnp.float32), 'q_b_w': lin(ks[2], N_HEADS * D_NOPE, Q_LORA), 'q_rope_w': lin(ks[3], N_HEADS * D_ROPE, Q_LORA), 'kv_a_w': lin(ks[4], KV_LORA + D_ROPE, D_MODEL), 'kv_a_ln_w': jnp.ones((KV_LORA,), jnp.float32), 'kv_a_ln_b': jnp.zeros((KV_LORA,), jnp.float32), 'kv_b_w': lin(ks[5], N_HEADS * (D_NOPE + D_V), KV_LORA), 'o_w': lin(ks[6], D_MODEL, N_HEADS * D_V)}
    _L0_attn_in = _L0_attn_setup()

    def _L0_ffn_setup():
        import jax, jax.numpy as jnp
        import numpy as np
        B, S, H = (2, 256, 256)
        E, K, F = (32, 4, 176)
        FS = 704
        EPS = 1e-06
        CAP = 128
        key = jax.random.key(seed)
        ks = jax.random.split(key, 10)
        s = 0.02
        return {'hidden_states': jax.random.normal(ks[0], (B, S, H), jnp.float32), 'w_norm': 1.0 + 0.02 * jax.random.normal(ks[1], (H,), jnp.float32), 'w_router': s * jax.random.normal(ks[2], (H, E), jnp.float32), 'w_gate': s * jax.random.normal(ks[3], (E, H, F), jnp.float32), 'w_up': s * jax.random.normal(ks[4], (E, H, F), jnp.float32), 'w_down': s * jax.random.normal(ks[5], (E, F, H), jnp.float32), 'sw_gate': s * jax.random.normal(ks[6], (H, FS), jnp.float32), 'sw_up': s * jax.random.normal(ks[7], (H, FS), jnp.float32), 'sw_down': s * jax.random.normal(ks[8], (FS, H), jnp.float32), 'w_shared_gate': s * jax.random.normal(ks[9], (H, 1), jnp.float32)}
    _L0_ffn_in = _L0_ffn_setup()

    def _L1_attn_setup():
        import jax, jax.numpy as jnp
        import numpy as np
        H = 16
        CHUNK = 32
        TOPK = 4
        THETA = 10000.0
        EPS = 1e-06
        NEG = -1e+30
        POS = 1e+30

        def _rope(x, cos, sin):
            d2 = x.shape[-1] // 2
            x1, x2 = (x[..., :d2], x[..., d2:])
            return jnp.concatenate([x1 * cos - x2 * sin, x2 * cos + x1 * sin], axis=-1)
        key = jax.random.key(seed)
        ks = jax.random.split(key, 6)
        B, S, D = (1, 256, 256)
        scale = 0.02
        return {'hidden_states': jax.random.normal(ks[0], (B, S, D), jnp.float32), 'Wq': jax.random.normal(ks[1], (D, D), jnp.float32) * scale, 'Wk': jax.random.normal(ks[2], (D, D), jnp.float32) * scale, 'Wv': jax.random.normal(ks[3], (D, D), jnp.float32) * scale, 'Wo': jax.random.normal(ks[4], (D, D), jnp.float32) * scale, 'o_norm_w': jnp.ones((D // H,), jnp.float32)}
    _L1_attn_in = _L1_attn_setup()

    def _L1_ffn_setup():
        import jax, jax.numpy as jnp
        import numpy as np
        B, S, H, F, E, R, K = (2, 128, 256, 896, 8, 32, 2)

        def _gather_slot(a_all, e):
            return jnp.take_along_axis(a_all, e[:, None, None], axis=1)[:, 0]
        key = jax.random.key(seed)
        ks = jax.random.split(key, 12)
        sc = 0.02
        n = lambda k, shape, s: jax.random.normal(k, shape, dtype=jnp.float32) * s
        return {'hidden_states': n(ks[0], (B, S, H), 1.0), 'Wg': n(ks[1], (E, H), sc), 'W1': n(ks[2], (F, H), sc), 'W2': n(ks[3], (H, F), sc), 'W3': n(ks[4], (F, H), sc), 'A1': n(ks[5], (E, R, H), sc), 'B1': n(ks[6], (E, F, R), sc), 'A2': n(ks[7], (E, R, F), sc), 'B2': n(ks[8], (E, H, R), sc), 'A3': n(ks[9], (E, R, H), sc), 'B3': n(ks[10], (E, F, R), sc)}
    _L1_ffn_in = _L1_ffn_setup()
    _d = {'L0_attn_hidden_states': _L0_attn_in['hidden_states'], 'L0_attn_q_a_w': _L0_attn_in['q_a_w'], 'L0_attn_q_a_ln_w': _L0_attn_in['q_a_ln_w'], 'L0_attn_q_a_ln_b': _L0_attn_in['q_a_ln_b'], 'L0_attn_q_b_w': _L0_attn_in['q_b_w'], 'L0_attn_q_rope_w': _L0_attn_in['q_rope_w'], 'L0_attn_kv_a_w': _L0_attn_in['kv_a_w'], 'L0_attn_kv_a_ln_w': _L0_attn_in['kv_a_ln_w'], 'L0_attn_kv_a_ln_b': _L0_attn_in['kv_a_ln_b'], 'L0_attn_kv_b_w': _L0_attn_in['kv_b_w'], 'L0_attn_o_w': _L0_attn_in['o_w'], 'L0_ffn_w_norm': _L0_ffn_in['w_norm'], 'L0_ffn_w_router': _L0_ffn_in['w_router'], 'L0_ffn_w_gate': _L0_ffn_in['w_gate'], 'L0_ffn_w_up': _L0_ffn_in['w_up'], 'L0_ffn_w_down': _L0_ffn_in['w_down'], 'L0_ffn_sw_gate': _L0_ffn_in['sw_gate'], 'L0_ffn_sw_up': _L0_ffn_in['sw_up'], 'L0_ffn_sw_down': _L0_ffn_in['sw_down'], 'L0_ffn_w_shared_gate': _L0_ffn_in['w_shared_gate'], 'L1_attn_Wq': _L1_attn_in['Wq'], 'L1_attn_Wk': _L1_attn_in['Wk'], 'L1_attn_Wv': _L1_attn_in['Wv'], 'L1_attn_Wo': _L1_attn_in['Wo'], 'L1_attn_o_norm_w': _L1_attn_in['o_norm_w'], 'L1_ffn_Wg': _L1_ffn_in['Wg'], 'L1_ffn_W1': _L1_ffn_in['W1'], 'L1_ffn_W2': _L1_ffn_in['W2'], 'L1_ffn_W3': _L1_ffn_in['W3'], 'L1_ffn_A1': _L1_ffn_in['A1'], 'L1_ffn_B1': _L1_ffn_in['B1'], 'L1_ffn_A2': _L1_ffn_in['A2'], 'L1_ffn_B2': _L1_ffn_in['B2'], 'L1_ffn_A3': _L1_ffn_in['A3'], 'L1_ffn_B3': _L1_ffn_in['B3']}
    _x0 = _d['L0_attn_hidden_states']
    _d['L0_attn_hidden_states'] = jax.random.normal(jax.random.fold_in(jax.random.key(seed), 1), (4, 256, 256), dtype=_x0.dtype)
    del _x0
    return _d

def reference(L0_attn_hidden_states, L0_attn_q_a_w, L0_attn_q_a_ln_w, L0_attn_q_a_ln_b, L0_attn_q_b_w, L0_attn_q_rope_w, L0_attn_kv_a_w, L0_attn_kv_a_ln_w, L0_attn_kv_a_ln_b, L0_attn_kv_b_w, L0_attn_o_w, L0_ffn_w_norm, L0_ffn_w_router, L0_ffn_w_gate, L0_ffn_w_up, L0_ffn_w_down, L0_ffn_sw_gate, L0_ffn_sw_up, L0_ffn_sw_down, L0_ffn_w_shared_gate, L1_attn_Wq, L1_attn_Wk, L1_attn_Wv, L1_attn_Wo, L1_attn_o_norm_w, L1_ffn_Wg, L1_ffn_W1, L1_ffn_W2, L1_ffn_W3, L1_ffn_A1, L1_ffn_B1, L1_ffn_A2, L1_ffn_B2, L1_ffn_A3, L1_ffn_B3):

    def _L0_attn_ref(hidden_states, q_a_w, q_a_ln_w, q_a_ln_b, q_b_w, q_rope_w, kv_a_w, kv_a_ln_w, kv_a_ln_b, kv_b_w, o_w):
        import jax, jax.numpy as jnp
        import numpy as np
        import math
        D_MODEL = 256
        N_HEADS = 16
        Q_LORA = 192
        KV_LORA = 64
        D_NOPE = 128
        D_ROPE = 64
        D_V = 128
        EPS = 1e-05

        def _layernorm(x, w, b):
            mu = jnp.mean(x, axis=-1, keepdims=True)
            var = jnp.mean(jnp.square(x - mu), axis=-1, keepdims=True)
            return (x - mu) * jax.lax.rsqrt(var + EPS) * w + b

        def _rope_tables(seq_len, dim, dtype):
            inv_freq = 1.0 / 10000.0 ** (np.arange(0, dim, 2, dtype=np.float32) / dim)
            t = np.arange(seq_len, dtype=np.float32)
            freqs = np.outer(t, inv_freq)
            emb = np.concatenate([freqs, freqs], -1)
            return (jnp.asarray(np.cos(emb), dtype), jnp.asarray(np.sin(emb), dtype))

        def _rotate_half(x):
            x1, x2 = jnp.split(x, 2, axis=-1)
            return jnp.concatenate([-x2, x1], axis=-1)

        def _apply_rope(x, cos, sin):
            c = cos[None, :, None, :]
            s = sin[None, :, None, :]
            return x * c + _rotate_half(x) * s
        B, S, _ = hidden_states.shape
        cos, sin = _rope_tables(S, D_ROPE, hidden_states.dtype)
        q_latent = _layernorm(hidden_states @ q_a_w.T, q_a_ln_w, q_a_ln_b)
        q_nope = (q_latent @ q_b_w.T).reshape(B, S, N_HEADS, D_NOPE)
        q_rope = (q_latent @ q_rope_w.T).reshape(B, S, N_HEADS, D_ROPE)
        kv_mixed = hidden_states @ kv_a_w.T
        kv_latent, k_rope = (kv_mixed[..., :KV_LORA], kv_mixed[..., KV_LORA:])
        kv_latent = _layernorm(kv_latent, kv_a_ln_w, kv_a_ln_b)
        kv_dec = (kv_latent @ kv_b_w.T).reshape(B, S, N_HEADS, D_NOPE + D_V)
        k_nope, v = (kv_dec[..., :D_NOPE], kv_dec[..., D_NOPE:])
        k_rope = k_rope[:, :, None, :]
        q_rope = _apply_rope(q_rope, cos, sin)
        k_rope = _apply_rope(k_rope, cos, sin)
        q = jnp.concatenate([q_nope, q_rope], axis=-1)
        k = jnp.concatenate([k_nope, jnp.broadcast_to(k_rope, (B, S, N_HEADS, D_ROPE))], axis=-1)
        scale = 1.0 / math.sqrt(D_NOPE + D_ROPE)
        scores = jnp.einsum('bqhd,bkhd->bhqk', q, k) * scale
        probs = jax.nn.softmax(scores, axis=-1)
        attn = jnp.einsum('bhqk,bkhd->bqhd', probs, v)
        attn = attn.reshape(B, S, N_HEADS * D_V)
        return attn @ o_w.T

    def _L0_ffn_ref(hidden_states, w_norm, w_router, w_gate, w_up, w_down, sw_gate, sw_up, sw_down, w_shared_gate):
        import jax, jax.numpy as jnp
        import numpy as np
        B, S, H = (2, 256, 256)
        E, K, F = (32, 4, 176)
        FS = 704
        EPS = 1e-06
        CAP = 128
        inp = hidden_states
        xf = inp.astype(jnp.float32)
        var = jnp.mean(xf * xf, axis=-1, keepdims=True)
        x = (w_norm * (xf * jax.lax.rsqrt(var + EPS))).astype(inp.dtype)
        Bq, Sq, Hq = x.shape
        x = x.reshape(-1, Hq)
        T = Bq * Sq
        logits = x @ w_router
        probs = jax.nn.softmax(logits.astype(jnp.float32), axis=-1)
        w_topk, sel = jax.lax.top_k(probs, K)
        w_topk = w_topk.astype(x.dtype)
        flat_e = sel.reshape(-1)
        order = jnp.argsort(flat_e)
        sorted_e = flat_e[order]
        counts = jnp.zeros((E,), jnp.int32).at[flat_e].add(1)
        starts = jnp.cumsum(counts) - counts
        pos = jnp.arange(T * K) - starts[sorted_e]
        tok = order // K
        valid = pos < CAP
        dest = jnp.where(valid, pos, CAP)
        buf = jnp.zeros((E, CAP + 1, Hq), x.dtype).at[sorted_e, dest].set(x[tok])
        buf = buf[:, :CAP]
        g = jnp.einsum('ech,ehf->ecf', buf, w_gate)
        u = jnp.einsum('ech,ehf->ecf', buf, w_up)
        y = jnp.einsum('ecf,efh->ech', jax.nn.silu(g) * u, w_down)
        wv = w_topk.reshape(-1)[order] * valid.astype(x.dtype)
        gath = y[sorted_e, jnp.minimum(pos, CAP - 1)]
        out = jnp.zeros((T, Hq), x.dtype).at[tok].add(gath * wv[:, None])
        sh = jax.nn.silu(x @ sw_gate) * (x @ sw_up) @ sw_down
        sh = jax.nn.sigmoid(x @ w_shared_gate) * sh
        out = out + sh
        return inp + out.reshape(Bq, Sq, Hq)

    def _L1_attn_ref(hidden_states, Wq, Wk, Wv, Wo, o_norm_w):
        import jax, jax.numpy as jnp
        import numpy as np
        H = 16
        CHUNK = 32
        TOPK = 4
        THETA = 10000.0
        EPS = 1e-06
        NEG = -1e+30
        POS = 1e+30

        def _rope(x, cos, sin):
            d2 = x.shape[-1] // 2
            x1, x2 = (x[..., :d2], x[..., d2:])
            return jnp.concatenate([x1 * cos - x2 * sin, x2 * cos + x1 * sin], axis=-1)
        B, S, D = hidden_states.shape
        d = D // H
        nblk = S // CHUNK
        q = (hidden_states @ Wq.T).reshape(B, S, H, d)
        k = (hidden_states @ Wk.T).reshape(B, S, H, d)
        v = (hidden_states @ Wv.T).reshape(B, S, H, d)
        pos = jnp.arange(S)
        inv_freq = 1.0 / THETA ** (jnp.arange(0, d, 2).astype(jnp.float32) / d)
        freqs = pos[:, None].astype(jnp.float32) * inv_freq
        cos = jnp.cos(freqs)[None, :, None, :]
        sin = jnp.sin(freqs)[None, :, None, :]
        q = _rope(q, cos, sin)
        k = _rope(k, cos, sin)
        km = k.reshape(B, nblk, CHUNK, H, d).mean(axis=2)
        gate = jnp.einsum('bshd,bnhd->bhsn', q, km)
        blk_q = pos // CHUNK
        blk_ids = jnp.arange(nblk)
        future = blk_ids[None, :] > blk_q[:, None]
        selfb = blk_ids[None, :] == blk_q[:, None]
        gate = jnp.where(future, NEG, gate)
        gate = jnp.where(selfb, POS, gate)
        vals, idx = jax.lax.top_k(gate, TOPK)
        valid = (vals > NEG / 2).astype(jnp.float32)
        sel = (jax.nn.one_hot(idx, nblk, dtype=jnp.float32) * valid[..., None]).sum(axis=-2) > 0
        sel_tok = jnp.repeat(sel, CHUNK, axis=-1)
        causal = pos[None, :] <= pos[:, None]
        mask = sel_tok & causal
        scores = jnp.einsum('bihd,bjhd->bhij', q, k) * d ** (-0.5)
        scores = jnp.where(mask, scores, NEG)
        p = jax.nn.softmax(scores, axis=-1)
        o = jnp.einsum('bhij,bjhd->bihd', p, v)
        o = o * jax.lax.rsqrt(jnp.mean(o * o, axis=-1, keepdims=True) + EPS) * o_norm_w
        return o.reshape(B, S, D) @ Wo.T

    def _L1_ffn_ref(hidden_states, Wg, W1, W2, W3, A1, B1, A2, B2, A3, B3):
        import jax, jax.numpy as jnp
        import numpy as np
        B, S, H, F, E, R, K = (2, 128, 256, 896, 8, 32, 2)

        def _gather_slot(a_all, e):
            return jnp.take_along_axis(a_all, e[:, None, None], axis=1)[:, 0]
        b, s, h = hidden_states.shape
        x = hidden_states.reshape(-1, h)
        nE = Wg.shape[0]
        logits = x @ Wg.T
        probs = jax.nn.softmax(logits.astype(jnp.float32), axis=-1)
        rw, sel = jax.lax.top_k(probs, K)
        rw = (rw / rw.sum(axis=-1, keepdims=True)).astype(x.dtype)
        base1 = x @ W1.T
        base3 = x @ W3.T
        a1_all = jnp.einsum('th,erh->ter', x, A1)
        a3_all = jnp.einsum('th,erh->ter', x, A3)
        out = jnp.zeros_like(x)
        for k in range(K):
            e = sel[:, k]
            mask = jax.nn.one_hot(e, nE, dtype=x.dtype)
            a1 = _gather_slot(a1_all, e)
            a3 = _gather_slot(a3_all, e)
            lora1 = jnp.einsum('ter,efr->tf', mask[:, :, None] * a1[:, None, :], B1)
            lora3 = jnp.einsum('ter,efr->tf', mask[:, :, None] * a3[:, None, :], B3)
            x1 = base1 + lora1
            x3 = base3 + lora3
            x2 = jax.nn.silu(x1) * x3
            down = x2 @ W2.T
            a2_all = jnp.einsum('tf,erf->ter', x2, A2)
            a2 = _gather_slot(a2_all, e)
            lora2 = jnp.einsum('ter,ehr->th', mask[:, :, None] * a2[:, None, :], B2)
            out = out + (down + lora2) * rw[:, k:k + 1]
        return out.reshape(b, s, h)
    x = L0_attn_hidden_states
    xn = _layernorm(x, axis=-1)
    x = x + _L0_attn_ref(xn, L0_attn_q_a_w, L0_attn_q_a_ln_w, L0_attn_q_a_ln_b, L0_attn_q_b_w, L0_attn_q_rope_w, L0_attn_kv_a_w, L0_attn_kv_a_ln_w, L0_attn_kv_a_ln_b, L0_attn_kv_b_w, L0_attn_o_w) + _L0_ffn_ref(xn, L0_ffn_w_norm, L0_ffn_w_router, L0_ffn_w_gate, L0_ffn_w_up, L0_ffn_w_down, L0_ffn_sw_gate, L0_ffn_sw_up, L0_ffn_sw_down, L0_ffn_w_shared_gate)
    xn = _layernorm(x, axis=-1)
    x = x + _L1_attn_ref(xn, L1_attn_Wq, L1_attn_Wk, L1_attn_Wv, L1_attn_Wo, L1_attn_o_norm_w) + _L1_ffn_ref(xn, L1_ffn_Wg, L1_ffn_W1, L1_ffn_W2, L1_ffn_W3, L1_ffn_A1, L1_ffn_B1, L1_ffn_A2, L1_ffn_B2, L1_ffn_A3, L1_ffn_B3)
    return x

_drawn_inputs = setup_inputs


def setup_inputs(seed=0):
    import zlib

    import numpy as np

    out = dict(_drawn_inputs(seed))
    spreads = {'L0_attn_q_a_ln_w': (1.0, 0.6),
     'L0_attn_q_a_ln_b': (0.0, 2.0),
     'L0_attn_kv_a_ln_w': (1.0, 0.6),
     'L0_attn_kv_a_ln_b': (0.0, 0.8),
     'L1_attn_o_norm_w': (1.0, 0.6)}
    factors = {'L0_ffn_w_norm': 8.0,
     'L0_ffn_w_router': 8.0,
     'L0_ffn_w_gate': 8.0,
     'L0_ffn_w_up': 8.0,
     'L0_ffn_w_down': 8.0,
     'L0_ffn_sw_gate': 5.986,
     'L0_ffn_sw_up': 5.862,
     'L0_ffn_sw_down': 6.033,
     'L0_ffn_w_shared_gate': 8.0,
     'L1_ffn_Wg': 8.0,
     'L1_ffn_W1': 17.433,
     'L1_ffn_W2': 16.608,
     'L1_ffn_W3': 16.564,
     'L1_ffn_A1': 8.0,
     'L1_ffn_B1': 8.0,
     'L1_ffn_A2': 8.0,
     'L1_ffn_B2': 8.0,
     'L1_ffn_A3': 8.0,
     'L1_ffn_B3': 8.0,
     'L0_attn_q_a_w': 8.0,
     'L0_attn_q_b_w': 8.0,
     'L0_attn_q_rope_w': 8.0,
     'L0_attn_kv_a_w': 8.0,
     'L0_attn_kv_b_w': 8.0,
     'L0_attn_o_w': 8.0,
     'L1_attn_Wq': 64.0,
     'L1_attn_Wk': 64.0,
     'L1_attn_Wv': 64.0,
     'L1_attn_Wo': 64.0}
    for name, (base, spread) in spreads.items():
        noise = np.random.default_rng([zlib.crc32(name.encode()), seed]).standard_normal(out[name].shape)
        drawn = base * np.exp(spread * noise) if base else spread * noise
        out[name] = jnp.asarray(drawn.astype(out[name].dtype))
    for name, factor in factors.items():
        out[name] = (out[name] * factor).astype(out[name].dtype)
    return out
```

```python
from contextlib import ExitStack

import numpy as np

import concourse.bass as bass
from concourse import mybir

F32 = mybir.dt.float32
BF16 = mybir.dt.bfloat16
U32 = mybir.dt.uint32
ALU = mybir.AluOpType
ACT = mybir.ActivationFunctionType
AX = mybir.AxisListType

P = 128
B, S, D = 4, 256, 256
TOK = B * S
NT = TOK // P
QT = S // P
KD = D // P
H0, QL, KVL, DN, DR, DV = 16, 192, 64, 128, 64, 128
PAIRS = H0 // 2
UNITS = 2 * B
LATW = QL + KVL + 2 * DR
E0, TOPK0, F0, FS, CAP = 32, 4, 176, 704, 128
FH = F0 // 2
NF = -(-FS // P)
SETS = 4
H1, CHUNK, TOPK1 = 16, 32, 4
D1 = D // H1
NB = S // CHUNK
GROUPS = 8
HG = H1 // 2
F1, E1, R1 = 896, 8, 32
ER = E1 * R1
NF1 = F1 // P
CH = 512
BIG = 1e30
HUGE = 3e38


def columns(spec):
    at, out = 0, {}
    for name, n in spec:
        out[name] = (at, n)
        at += n
    return out, at


CF, CF_N = columns([("ident", P), ("q_even", S), ("q_odd", S), ("q_sin", S), ("k_cos", QT * DR), ("k_sin", QT * DR),
                    ("iota", E0), ("cos1", QT * D1), ("sin1", QT * D1), ("keep", QT * H1 * NB),
                    ("force", QT * H1 * NB), ("future", QT * H1 * NB), ("later", NB), ("head_mean", HG),
                    ("head_scale", HG), ("slot_expert", ER), ("ones", P), ("eps_norm", 1)])
CB, CB_N = columns([("ident", P), ("before", P), ("ones", P), ("causal", P)])
BC, BC_N = columns([("lat_w", QL + KVL), ("lat_b", QL + KVL), ("w_norm", D), ("o_norm", D1)])

SMALL = 2304
REGIONS = (SMALL, 4 * NT * D, 17920, 8448, 9728)
SB_COLS = CF_N + BC_N + NT * D + sum(REGIONS)


def tables():
    cf = np.zeros((P, CF_N), np.float32)
    cb = np.zeros((P, CB_N), np.float32)

    def put(name, a):
        at, n = CF[name]
        cf[:, at:at + n] = np.asarray(a, np.float32).reshape(P, n)

    def putb(name, a):
        at, n = CB[name]
        cb[:, at:at + n] = a

    i = np.arange(P)
    put("ident", np.eye(P))
    inv = 1.0 / 10000.0 ** (np.arange(0, DR, 2, dtype=np.float32) / DR)
    fr = np.outer(np.arange(S, dtype=np.float32), inv)
    emb = np.concatenate([fr, fr], -1)
    cos, sin = np.cos(emb), np.sin(emb)
    signed = np.concatenate([-sin[:, :DR // 2], sin[:, DR // 2:]], -1)
    sc = np.float32(-1.0 / np.sqrt(DN + DR))
    one = np.full((DR, S), sc, np.float32)
    put("q_even", np.concatenate([one, sc * cos.T]))
    put("q_odd", np.concatenate([sc * cos.T, one]))
    put("q_sin", np.concatenate([sc * signed.T, sc * signed.T]))
    put("k_cos", cos.reshape(QT, P, DR).transpose(1, 0, 2))
    put("k_sin", signed.reshape(QT, P, DR).transpose(1, 0, 2))
    put("iota", np.tile(np.arange(E0), (P, 1)))
    inv1 = (1.0 / np.float32(10000.0) ** (np.arange(0, D1, 2).astype(np.float32) / np.float32(D1))).astype(np.float32)
    f1 = np.arange(S, dtype=np.float32)[:, None] * inv1
    c1, s1 = np.cos(f1), np.sin(f1)
    put("cos1", np.concatenate([c1, c1], -1).reshape(QT, P, D1).transpose(1, 0, 2))
    put("sin1", np.concatenate([-s1, s1], -1).reshape(QT, P, D1).transpose(1, 0, 2))
    own = np.arange(S)[:, None] // CHUNK
    n = np.arange(NB)[None, :]

    def rows(a):
        return np.repeat(a.reshape(QT, P, 1, NB), H1, 2).transpose(1, 0, 2, 3)

    put("keep", rows((n < own).astype(np.float32)))
    put("force", rows(np.where(n > own, -BIG, np.where(n == own, BIG, 0.0))))
    put("future", rows(np.where(n > own, BIG, 0.0)))
    put("later", np.tile(NB - 1 - np.arange(NB), (P, 1)))
    mine = (i[:, None] // D1 == np.arange(HG)[None, :]).astype(np.float32)
    put("head_mean", mine / CHUNK)
    put("head_scale", -mine * D1 ** -0.5)
    put("slot_expert", np.tile(np.arange(ER) // R1, (P, 1)))
    put("ones", np.ones((P, P)))
    put("eps_norm", np.full((P, 1), 1e-5))
    putb("ident", np.eye(P))
    putb("before", i[:, None] < i[None, :])
    putb("ones", 1.0)
    putb("causal", np.where(i[None, :] > i[:, None], BIG, 0.0))
    return cf, cb.astype(mybir.dt.np(BF16))


def lay_out(a):
    f = {k: np.asarray(v) for k, v in a.items()}

    def tiles(w):
        return w.reshape(-1, P, w.shape[1]).transpose(1, 0, 2)

    def rep(*v):
        return np.tile(np.concatenate(v)[None, :], (P, 1))

    def swap(w):
        return np.concatenate([w[..., DR // 2:, :], w[..., :DR // 2, :]], -2)

    out = {"x": f["L0_attn_hidden_states"].reshape(TOK, D)}
    out["consts"], out["consts_b"] = tables()
    out["rows"] = rep(f["L0_attn_q_a_ln_w"], f["L0_attn_kv_a_ln_w"], f["L0_attn_q_a_ln_b"], f["L0_attn_kv_a_ln_b"],
                      f["L0_ffn_w_norm"], f["L1_attn_o_norm_w"])
    kva = f["L0_attn_kv_a_w"]
    out["w_lat"] = tiles(np.concatenate([f["L0_attn_q_a_w"], kva[:KVL], kva[KVL:], swap(kva[KVL:])]).T)
    wq = f["L0_attn_q_b_w"].reshape(PAIRS, 2, DN, QL).transpose(0, 2, 1, 3)
    kvb = f["L0_attn_kv_b_w"].reshape(PAIRS, 2, 2, DN, KVL)
    vkv = np.concatenate([kvb[:, :, 1], kvb[:, :, 0], kvb[:, :, 1]], -1).transpose(0, 2, 1, 3)
    wo = f["L0_attn_o_w"].T.reshape(PAIRS, 2, DV, D).transpose(0, 2, 1, 3)
    out["w_pair"] = np.concatenate([w.reshape(PAIRS, P, -1) for w in (wq, vkv, wo)], -1)
    qr = f["L0_attn_q_rope_w"].reshape(PAIRS, 2, DR, QL)
    qs = swap(qr)
    out["w_rope"] = np.stack([np.concatenate([qr[:, 0], qr[:, 1]], 1), np.concatenate([qs[:, 1], qs[:, 0]], 1)],
                             1).transpose(0, 3, 1, 2)
    out["w_route"] = tiles(np.concatenate([f["L0_ffn_w_router"], f["L0_ffn_w_shared_gate"],
                                           np.zeros((D, P - E0 - 1), np.float32)], 1))
    pad = np.zeros((D, NF * P - FS), np.float32)
    out["sw_up"] = tiles(np.concatenate([f["L0_ffn_sw_gate"], pad, f["L0_ffn_sw_up"], pad], 1))
    out["sw_down"] = tiles(np.concatenate([f["L0_ffn_sw_down"], np.zeros((NF * P - FS, D), np.float32)]))
    gu = np.stack([f["L0_ffn_w_gate"], f["L0_ffn_w_up"]], 2)
    out["w_gate_up"] = gu.reshape(E0, KD, P, 2 * F0).transpose(0, 2, 1, 3)
    out["w_down"] = f["L0_ffn_w_down"].reshape(E0, 2, FH, D).transpose(0, 2, 1, 3)
    out["w_qkvg"] = tiles(np.concatenate([f["L1_attn_Wq"], f["L1_attn_Wk"], f["L1_attn_Wv"], f["L1_ffn_Wg"]]).T)
    out["w_o1"] = tiles(f["L1_attn_Wo"].T)
    out["w13"] = tiles(np.concatenate([f["L1_ffn_W1"], f["L1_ffn_W3"]]).T)
    out["a13"] = tiles(np.concatenate([f["L1_ffn_A1"].reshape(ER, D), f["L1_ffn_A3"].reshape(ER, D)]).T)
    out["b13"] = tiles(np.concatenate([f["L1_ffn_B1"].transpose(0, 2, 1).reshape(ER, F1),
                                       f["L1_ffn_B3"].transpose(0, 2, 1).reshape(ER, F1)], 1))
    out["w2"] = tiles(f["L1_ffn_W2"].T)
    out["a2"] = tiles(f["L1_ffn_A2"].reshape(ER, F1).T)
    out["b2"] = tiles(f["L1_ffn_B2"].transpose(0, 2, 1).reshape(ER, D))
    return {k: np.ascontiguousarray(v) for k, v in out.items()}


class Strip:

    def __init__(self, whole, at, n):
        self.whole, self.at, self.end = whole, at, at + n

    def take(self, *shape):
        n = int(np.prod(shape))
        assert self.at + n <= self.end, "the strip is full"
        ap = self.whole[:, self.at:self.at + n]
        self.at += n
        if len(shape) == 2:
            return ap.rearrange("p (a b) -> p a b", b=shape[1])
        if len(shape) == 3:
            return ap.rearrange("p (a b c) -> p a b c", b=shape[1], c=shape[2])
        return ap

    def take_b(self, *shape):
        n = int(np.prod(shape))
        ap = self.take(n // 2).bitcast(BF16)
        if len(shape) == 2:
            return ap.rearrange("p (a b) -> p a b", b=shape[1])
        if len(shape) == 3:
            return ap.rearrange("p (a b c) -> p a b c", b=shape[1], c=shape[2])
        return ap


def along(ap, *dims):
    for at, n in dims:
        ap = ap.unsqueeze(at)
        shape = list(ap.shape)
        shape[at] = n
        ap = ap.broadcast_to(shape)
    return ap


def at_least(eng, sem, n):
    if not isinstance(n, int) or n > 0:
        eng.wait_ge(sem, n)


def program(nc, t, y):
    ctx = ExitStack()
    with ctx:
        def sem(name):
            return ctx.enter_context(nc.semaphore(name))

        sb = ctx.enter_context(nc.sbuf_tensor("sb", [P, SB_COLS], F32))
        cb = ctx.enter_context(nc.sbuf_tensor("cb", [P, CB_N], BF16))
        bank = [ctx.enter_context(nc.psum_tensor(f"bank{i}", [P, 512], F32)) for i in range(8)]
        whole = Strip(sb, 0, SB_COLS)
        cf = whole.take(CF_N)
        rows = whole.take(BC_N)
        acc = whole.take(NT, D)
        small = whole.take(SMALL)
        region1 = whole.take(4 * NT * D)
        region2 = whole.take(17920)
        region3 = whole.take(8448)
        region4 = whole.take(9728)

        def strip(region):
            return Strip(region, 0, region.shape[1])

        def table(name, *shape):
            at, n = CF[name]
            ap = cf[:, at:at + n]
            if len(shape) == 2:
                return ap.rearrange("p (a b) -> p a b", b=shape[1])
            return ap

        def row(name):
            at, n = BC[name]
            return rows[:, at:at + n]

        def tableb(name):
            at, n = CB[name]
            return cb[:, at:at + n]

        ident, identb = table("ident"), tableb("ident")

        sm = Strip(small, 0, SMALL)
        stats = sm.take(NT, 6)
        mv = sm.take(NT, 2)
        var, sd, rstd = sm.take(NT), sm.take(NT), sm.take(NT)
        ms, sd2, rrms = sm.take(NT), sm.take(NT), sm.take(NT)
        lat_stats, lat_mv = sm.take(2 * NT, 6), sm.take(2 * NT, 2)
        lat_var, lat_sd, lat_rstd = sm.take(2 * NT), sm.take(2 * NT), sm.take(2 * NT)
        gate_z, gate_e, gate1, gate = sm.take(NT), sm.take(NT), sm.take(NT), sm.take(NT)
        weight4 = sm.take(NT * TOPK0)
        dest = sm.take(NT * TOPK0).bitcast(U32)
        source = sm.take(NT * TOPK0).bitcast(U32)
        row_min = sm.take(4, QT)
        row_sum = sm.take(4, QT)
        row_inv = sm.take(4, QT)

        r1 = strip(region1)
        xn, xnT = r1.take(NT, D), r1.take(KD, TOK)
        x2, x2T = r1.take(NT, D), r1.take(KD, TOK)
        picked = strip(region1).take(NT * TOPK0, D)

        r2 = strip(region2)
        lat = r2.take(NT, LATW)
        w_lat = r2.take(KD, LATW)
        w_route = r2.take(KD, P)
        sw_up = r2.take(KD, 2 * NF * P)
        sw_down = r2.take(NF, D)
        hT = r2.take(NF, TOK)
        sgate, sup = r2.take(2, CH), r2.take(2, CH)
        zeros = small[:, SMALL - D:SMALL]
        r2 = strip(region2)
        qb = [r2.take(2, TOK) for _ in range(2)]
        q_tmp = r2.take(CH)
        probs = r2.take(4, QT, S)
        probsT = r2.take(2, QT, S)
        ctxT = r2.take(PAIRS, TOK)
        w_vo = r2.take(PAIRS, D)

        r3 = strip(region3)
        xe = r3.take(SETS, D)
        w_gu = [r3.take(KD, 2 * F0) for _ in range(SETS)]
        w_dn = [r3.take(2, D) for _ in range(SETS)]
        xeT = [r3.take(KD, P) for _ in range(2)]
        e_act, e_hid = r3.take(2, 2, P), r3.take(2, 2, P)
        ye = r3.take(SETS, D)

        r4 = strip(region4)
        w_pair = [r4.take(2 * QL + 2 * 3 * KVL + 2 * D) for _ in range(2)]
        w_q = [w[:, 0:2 * QL].rearrange("p (h n) -> p h n", h=2) for w in w_pair]
        w_vk = [w[:, 2 * QL:2 * QL + 6 * KVL].rearrange("p (h n) -> p h n", h=2) for w in w_pair]
        w_o = [w[:, 2 * QL + 6 * KVL:].rearrange("p (h n) -> p h n", h=2) for w in w_pair]
        w_eff = [r4.take(2, 6 * DR) for _ in range(2)]
        qk = r4.take(4, TOK)
        kv_tok = r4.take(NT, 3 * KVL)
        r4 = strip(region4)
        logit, expo, prob = r4.take(NT, E0), r4.take(NT, E0), r4.take(NT, E0)
        route_max, route_sum, route_inv = r4.take(NT), r4.take(NT), r4.take(NT)
        top, top_at = r4.take(NT, 8), r4.take(NT, 8).bitcast(U32)
        chosen = r4.take(NT, TOPK0)
        onehot = r4.take(NT, TOPK0, E0)
        mask = r4.take(NT, E0)
        maskb = r4.take_b(NT, E0)
        place4, over, clipped = r4.take(NT * TOPK0), r4.take(NT * TOPK0), r4.take(NT * TOPK0)
        dest_f, source_f = r4.take(NT * TOPK0), r4.take(NT * TOPK0)
        assert r4.at <= 2 * 1280 + 2 * 768

        logit1, expo1, prob1 = sm.take(NT, E1), sm.take(NT, E1), sm.take(NT, E1)
        max1, sum1, inv1 = sm.take(NT), sm.take(NT), sm.take(NT)
        top1, top1_at, chosen1 = sm.take(NT, 8), sm.take(NT, 8).bitcast(U32), sm.take(NT, 2)
        share = sm.take(NT, 2)
        bias_g = sm.take(2, QT, HG * NB)
        o_var, o_sd, o_inv = sm.take(NT, H1), sm.take(NT, H1), sm.take(NT, H1)
        assert sm.at <= SMALL - D
        r1 = strip(region1)
        x1T = r1.take(KD, TOK)
        qkT = r1.take(4, TOK)
        v_tok = r1.take(NT, D)
        r1 = Strip(region1, KD * TOK, 4 * TOK + NT * D)
        w2, a2, b2 = r1.take(NF1, D), r1.take(NF1, ER), r1.take(2, D)
        oT = r1.take(KD, TOK)
        xn1 = Strip(region1, KD * TOK, NT * D).take(NT, D)
        r2 = strip(region2)
        am_first = [r2.take(2, TOK) for _ in range(2)]
        am_step = [r2.take(2, TOK) for _ in range(2)]
        phase = r2.at
        r2.take(NT * D)
        qk_tok = r2.take(NT, 2 * D)
        rope_tmp = r2.take(2, 2, 2 * D)
        kmean = r2.take(KD, B, H1 * NB)
        kblock = r2.take(KD, B * NB)
        r2 = Strip(region2, phase, NT * D)
        expert_of = [r2.take_b(NT, ER) for _ in range(2)]
        first_maskT = Strip(region2, phase + 7936, TOK).take_b(2, TOK)
        r2 = Strip(region2, phase, region2.shape[1] - phase)
        q_head = [r2.take(HG, S) for _ in range(2)]
        masked = r2.take(4, 3 * P)
        probs1 = r2.take(4, 3 * P)
        probs1T = r2.take(2, 3 * P)
        r2 = Strip(region2, phase, region2.shape[1] - phase)
        h_first = r2.take(NF1, CH)
        h_both = r2.take(NF1, CH)
        f_act, f_hid = r2.take(2, CH), r2.take(2, CH)
        squares = h_both.rearrange("p f n -> p (f n)")[:, 0:NT * D].rearrange("p (t h d) -> p (t h) d", h=H1, d=D1)
        r3 = strip(region3)
        w_qkvg = r3.take(KD, 3 * D + E1)
        w_o1, a13, w13 = r3.take(KD, D), r3.take(KD, 2 * ER), r3.take(KD, 2 * F1)
        rank = r3.take(NT, H1 * NB)
        share_rep = r3.take(4, P)
        r3 = strip(region3)
        am2, am2_tmp = r3.take(2, CH), r3.take(CH)
        r4 = strip(region4)
        b13 = r4.take(2, 2 * F1)
        second_maskT, step_maskT = r4.take_b(2, TOK), r4.take_b(2, TOK)
        shareT = r4.take(2, TOK)
        o_tok = r4.take(NT, D)
        r4 = strip(region4)
        score_blk = r4.take(NT * H1, NB)
        beats_first = [r4.take_b(QT * H1, NB - d) for d in range(1, NB)]
        beats_rest = [r4.take_b((NT - QT) * H1, NB - d) for d in range(1, NB)]
        assert r4.at <= 2 * 2 * F1

        buf = nc.dram_tensor("expert_in", [E0 * CAP, D], F32).ap()
        res = nc.dram_tensor("expert_out", [E0 * CAP, D], F32).ap()

        x_in = [sem(f"x_in{i}") for i in range(4)]
        cf_in, cb_in, rows_in, lat_in, route_in = (sem(n) for n in ("cf_in", "cb_in", "rows_in", "lat_in", "route_in"))
        up_in, down_in, zero_set, zero_in = (sem(n) for n in ("up_in", "down_in", "zero_set", "zero_in"))
        ln_stats, ln_mv, ln_var, ln_sd, ln_rstd = (sem(n) for n in ("ln_stats", "ln_mv", "ln_var", "ln_sd", "ln_rstd"))
        xn_done, ms_step, ms_var, ms_sd, ms_inv, x2_done = (
            sem(n) for n in ("xn_done", "ms_step", "ms_var", "ms_sd", "ms_inv", "x2_done"))
        acc_done = sem("acc_done")
        turned, turned_out = sem("turned"), sem("turned_out")
        lat_mm, lat_out, logit_mm = sem("lat_mm"), sem("lat_out"), sem("logit_mm")
        lat_st, lat_ag, lat_vr, lat_sdev, lat_rs, lat_norm, lat_scaled, lat_rope, lat_done = (
            sem(n) for n in ("lat_st", "lat_ag", "lat_vr", "lat_sdev", "lat_rs", "lat_norm", "lat_scaled", "lat_rope",
                             "lat_done"))
        pad_set, latT_mm, latT_out = sem("pad_set"), sem("latT_mm"), sem("latT_out")
        rt_max, rt_sub, rt_exp, rt_step, rt_mask, rt_pos, rt_dest = (
            sem(n) for n in ("rt_max", "rt_sub", "rt_exp", "rt_step", "rt_mask", "rt_pos", "rt_dest"))
        sh_mm, sh_act, sh_h, sh_down, sh_add = (sem(n) for n in ("sh_mm", "sh_act", "sh_h", "sh_down", "sh_add"))
        eff_pad = sem("eff_pad")
        scattered, gathered, weighted, combined = (sem(n) for n in ("scattered", "gathered", "weighted", "combined"))
        ew_in = [sem(f"ew_in{s}") for s in range(SETS)]
        eb_in = [sem(f"eb_in{s}") for s in range(SETS)]
        y_stored = [sem(f"y_stored{s}") for s in range(SETS)]
        ex_t, ex_tout, ex_g, ex_act, ex_h, ex_done, ex_y = (
            sem(n) for n in ("ex_t", "ex_tout", "ex_g", "ex_act", "ex_h", "ex_done", "ex_y"))
        pair_in = [sem(f"pair_in{i}") for i in range(2)]
        at_m, at_eff, at_q, at_qrope, at_qe = (sem(n) for n in ("at_m", "at_eff", "at_q", "at_qrope", "at_qe"))
        at_s, at_min, at_exp, at_inv, at_norm, at_t, at_tout, at_pv, at_ctx = (
            sem(n) for n in ("at_s", "at_min", "at_exp", "at_inv", "at_norm", "at_t", "at_tout", "at_pv", "at_ctx"))
        op_mm, op_add = sem("op_mm"), sem("op_add")
        l1_sd = sem("l1_sd")
        w3_in, b13_in, w2_in = sem("w3_in"), sem("b13_in"), sem("w2_in")
        qkv_mm, rope_mul, rope_add, v_out, qkT_mm, qkT_out = (
            sem(n) for n in ("qkv_mm", "rope_mul", "rope_add", "v_out", "qkT_mm", "qkT_out"))
        kmean_set, kmean_done, blk_mm, blk_step = (sem(n) for n in ("kmean_set", "kmean_done", "blk_mm", "blk_step"))
        blk_beats, blk_count, rest_beats, rest_count = (
            sem(n) for n in ("blk_beats", "blk_count", "rest_beats", "rest_count"))
        r1_step, r1_sub, r1_exp, r1_own, r1_share = (sem(n) for n in ("r1_step", "r1_sub", "r1_exp", "r1_own", "r1_share"))
        fill_mm, fill_out, step_mask, low_rank = (sem(n) for n in ("fill_mm", "fill_out", "step_mask", "low_rank"))
        bl_q, bl_bias, bl_s, bl_min, bl_exp, bl_inv, bl_t, bl_tout, bl_v, bl_o = (
            sem(n) for n in ("bl_q", "bl_bias", "bl_s", "bl_min", "bl_exp", "bl_inv", "bl_t", "bl_tout", "bl_v", "bl_o"))
        on_sq, on_step, on_sd, on_done = (sem(n) for n in ("on_sq", "on_step", "on_sd", "on_done"))
        f_mm, f_silu, f_h, f_x, f_x2, f_a2, f_am2, f_down = (
            sem(n) for n in ("f_mm", "f_silu", "f_h", "f_x", "f_x2", "f_a2", "f_am2", "f_down"))
        y_done, stored = sem("y_done"), sem("stored")

        def fills():
            out = [("low", j, h, c) for j in range(2) for h in range(2) for c in range(TOK // CH)]
            out += [("mask", k, h, c) for k in range(2) for h in range(2) for c in range(TOK // CH)]
            return out + [("share", k, 0, c) for k in range(2) for c in range(TOK // CH)]

        def turn_bank(g):
            return g % 4 if g < 8 else (2 if g < 12 else 6) + g % 2

        def uses():
            out = [(0, 0)]
            for f in range(1, NF1):
                out += [(f, 0), (f - 1, 1)]
            return out + [(NF1 - 1, 1)]

        first_heads, rest_heads = slice(0, QT * H1), slice(QT * H1, NT * H1)

        def compare(eng, heads, beats, step):
            for d in range(1, NB):
                eng.tensor_tensor(beats[d - 1], score_blk[:, heads, 0:NB - d], score_blk[:, heads, d:NB], ALU.is_ge)\
                    .then_inc(step, 1)

        def count(eng, heads, beats, step, n):
            ranks = rank.rearrange("p t (h n) -> p (t h) n", n=NB)[:, heads, :]
            for d in range(1, NB):
                eng.tensor_tensor(ranks[:, :, d:NB], ranks[:, :, d:NB], beats[d - 1], ALU.add).then_inc(step, 1)
                eng.wait_ge(step, n + 2 * d - 1)
                eng.tensor_tensor(ranks[:, :, 0:NB - d], ranks[:, :, 0:NB - d], beats[d - 1], ALU.subtract)\
                    .then_inc(step, 1)
                eng.wait_ge(step, n + 2 * d)

        block = ctx.enter_context(nc.Block())

        @block.sync
        def _(sp):
            x_t = t["x"].rearrange("(t p) d -> p t d", p=P)
            for i in range(4):
                sp.dma_start(acc[:, 2 * i:2 * i + 2, :], x_t[:, 2 * i:2 * i + 2, :]).then_inc(x_in[i], 16)
            sp.dma_start(cf, t["consts"]).then_inc(cf_in, 16)
            sp.dma_start(rows, t["rows"]).then_inc(rows_in, 16)
            sp.dma_start(w_lat, t["w_lat"]).then_inc(lat_in, 16)
            sp.dma_start(w_route, t["w_route"]).then_inc(route_in, 16)
            sp.dma_start(cb[:, :], t["consts_b"]).then_inc(cb_in, 16)
            sp.dma_start(sw_up, t["sw_up"]).then_inc(up_in, 16)
            sp.dma_start(sw_down, t["sw_down"]).then_inc(down_in, 16)

            def expert_weights(e, s):
                sp.dma_start(w_gu[s], t["w_gate_up"][bass.ds(e, 1)].rearrange("o p k n -> p (o k) n"))\
                    .then_inc(ew_in[s], 16)
                sp.dma_start(w_dn[s][0:FH], t["w_down"][bass.ds(e, 1)].rearrange("o p k n -> p (o k) n"))\
                    .then_inc(ew_in[s], 16)

            def expert_rows(e, s):
                sp.dma_start(xe[:, s, :], buf[bass.ds(e * CAP, CAP), :]).then_inc(eb_in[s], 16)

            for s in range(SETS):
                expert_weights(s, s)
            sp.wait_ge(zero_set, 1)
            sp.dma_start(buf.rearrange("(r p) d -> p r d", p=P), along(zeros, (1, E0))).then_inc(zero_in, 16)

            def pair_weights(p, i):
                half = [w_eff[i][:, k, :].rearrange("p (g c) -> p g c", g=2)[:, :, DR:3 * DR] for k in range(2)]
                rope = t["w_rope"][bass.ds(p, 1)].rearrange("o l g c -> l (o g) c")
                sp.dma_start(w_pair[i], t["w_pair"][bass.ds(p, 1)].rearrange("o p n -> p (o n)")).then_inc(pair_in[i], 16)
                sp.dma_start(half[0], rope[0:P]).then_inc(pair_in[i], 16)
                sp.dma_start(half[1][0:QL - P], rope[P:QL]).then_inc(pair_in[i], 16)

            sp.wait_ge(rt_dest, 2)
            sp.wait_ge(eff_pad, 2)
            for i in range(2):
                pair_weights(i, i)
            sp.wait_ge(scattered, 16 * NT * TOPK0)
            for s in range(SETS):
                expert_rows(s, s)
            with sp.Fori(0, E0 // SETS - 1) as i:
                for s in range(SETS):
                    sp.wait_ge(ex_done, SETS * i + s + 1)
                    expert_weights(SETS * i + SETS + s, s)
                    expert_rows(SETS * i + SETS + s, s)
            sp.wait_ge(ex_y, E0)
            for s in range(SETS):
                sp.wait_ge(y_stored[s], 16 * E0 // SETS)
            for dst, name in ((w_qkvg, "w_qkvg"), (w_o1, "w_o1"), (a13, "a13"), (w13, "w13")):
                sp.dma_start(dst, t[name]).then_inc(w3_in, 16)
            with sp.Fori(0, PAIRS // 2 - 1) as i:
                for s in range(2):
                    sp.wait_ge(at_q, 12 * i + 6 * s + 6)
                    pair_weights(2 * i + 2 + s, s)
            sp.wait_ge(blk_count, 2 * (NB - 1))
            sp.wait_ge(rest_count, 2 * (NB - 1))
            sp.dma_start(b13, t["b13"]).then_inc(b13_in, 16)
            sp.wait_ge(bl_q, GROUPS * HG)
            sp.wait_ge(bl_s, GROUPS * HG)
            for dst, name in ((w2, "w2"), (a2, "a2"), (b2, "b2")):
                sp.dma_start(dst, t[name]).then_inc(w2_in, 16)
            for i in range(NT):
                sp.wait_ge(y_done, i + 1)
                sp.dma_start(y[i * P:(i + 1) * P, :], acc[:, i, :]).then_inc(stored, 16)
            sp.wait_ge(stored, 16 * NT)

        @block.gpsimd
        def _(pool):
            pool.memset(zeros, 0.0).then_inc(zero_set, 1)
            for i in range(NT):
                pool.wait_ge(xn_done, i + 1)
                pool.tensor_tensor(acc[:, i, :], acc[:, i, :], xn[:, i, :], ALU.add).then_inc(acc_done, 1)
            for u in range(2 * NF):
                pool.wait_ge(sh_act, 2 * u + 2)
                pool.tensor_tensor(hT[:, u // 2, (u % 2) * CH:(u % 2 + 1) * CH], sgate[:, u % 2, :], sup[:, u % 2, :],
                                   ALU.mult).then_inc(sh_h, 1)
            pool.wait_ge(rt_dest, 2)
            pool.wait_ge(zero_in, 16)
            for j in range(NT * TOPK0):
                pool.indirect_dma_start(buf[:, :], bass.IndirectOffsetOnAxis(ap=dest[:, j:j + 1], axis=0),
                                        x2[:, j // TOPK0, :], None, bounds_check=E0 * CAP - 1, oob_is_err=False)\
                    .then_inc(scattered, 16)
            with pool.Fori(0, E0 // SETS) as i:
                for s in range(SETS):
                    pool.wait_ge(ex_y, SETS * i + s + 1)
                    pool.dma_start(res[bass.ds((SETS * i + s) * CAP, CAP), :], ye[:, s, :]).then_inc(y_stored[s], 16)
            for s in range(SETS):
                pool.wait_ge(y_stored[s], 16 * E0 // SETS)
            for k in range(TOPK0):
                for i in range(NT):
                    j = i * TOPK0 + k
                    pool.indirect_dma_start(picked[:, k * NT + i, :], None, res[:, :],
                                            bass.IndirectOffsetOnAxis(ap=source[:, j:j + 1], axis=0),
                                            bounds_check=E0 * CAP - 1, oob_is_err=False).then_inc(gathered, 16)

            pool.wait_ge(gathered, 16 * NT * TOPK0)
            pool.wait_ge(sh_add, NT)
            for k in range(TOPK0):
                rows_k = picked[:, k * NT:(k + 1) * NT, :]
                weight_k = along(weight4.rearrange("p (t k) -> p t k", k=TOPK0)[:, :, k], (2, D))
                pool.tensor_tensor(rows_k, rows_k, weight_k, ALU.mult).then_inc(weighted, 1)
            for k in range(TOPK0):
                pool.wait_ge(weighted, k + 1)
                at_least(pool, combined, k)
                pool.tensor_tensor(acc, acc, picked[:, k * NT:(k + 1) * NT, :], ALU.add).then_inc(combined, 1)

            pool.wait_ge(op_mm, NT)
            pool.memset(kmean, 0.0).then_inc(kmean_set, 1)
            for i in range(NT):
                pool.wait_ge(rope_mul, 3 * i + 3)
                pool.tensor_tensor(qk_tok[:, i, :], rope_tmp[:, i % 2, 0, :], rope_tmp[:, i % 2, 1, :], ALU.add)\
                    .then_inc(rope_add, 1)
            pool.wait_ge(rest_beats, NB - 1)
            count(pool, rest_heads, beats_rest, rest_count, 0)
            pool.wait_ge(fill_out, 16)
            pool.tensor_tensor(step_maskT, second_maskT, first_maskT, ALU.subtract).then_inc(step_mask, 1)
            for j in range(2):
                pool.tensor_tensor(am_first[j], am_step[j], first_maskT, ALU.mult).then_inc(low_rank, 1)
            pool.wait_ge(step_mask, 1)
            for j in range(2):
                pool.wait_ge(low_rank, j + 1)
                pool.tensor_tensor(am_step[j], am_step[j], step_maskT, ALU.mult).then_inc(low_rank, 1)

        @block.scalar
        def _(act):
            act.wait_ge(ln_var, 1)
            act.activation(sd, var, ACT.Sqrt).then_inc(ln_sd, 1)
            act.wait_ge(ms_var, 1)
            act.activation(sd2, ms, ACT.Sqrt).then_inc(ms_sd, 1)

            def turned_copy(g, dst):
                act.wait_ge(turned, g + 1)
                act.activation(dst[:, :, (g % 4) * 2 * P:(g % 4 + 1) * 2 * P],
                               bank[turn_bank(g)][:, :].rearrange("p (k n) -> p k n", k=KD), ACT.Copy)\
                    .then_inc(turned_out, 1)

            for g in range(4):
                turned_copy(g, xnT)
            for i in range(NT):
                act.wait_ge(lat_mm, i + 1)
                act.activation(lat[:, i, :], bank[4 + i % 2][:, 0:LATW], ACT.Copy).then_inc(lat_out, 1)
            for g in range(4, 8):
                turned_copy(g, x2T)
            act.wait_ge(lat_vr, 1)
            act.activation(lat_sd, lat_var, ACT.Sqrt).then_inc(lat_sdev, 1)
            act.wait_ge(rt_sub, 4)
            act.activation(expo, logit, ACT.Exp).then_inc(rt_exp, 1)
            act.activation(gate_e, gate_z, ACT.Exp, scale=-1.0).then_inc(rt_exp, 1)
            for u in range(2 * NF):
                act.wait_ge(sh_mm, u + 1)
                if u >= 2:
                    act.wait_ge(sh_h, u - 1)
                act.activation(sgate[:, u % 2, :], bank[2 * (u % 2)][:, :], ACT.Silu).then_inc(sh_act, 1)
                act.activation(sup[:, u % 2, :], bank[2 * (u % 2) + 1][:, :], ACT.Copy).then_inc(sh_act, 1)
            with act.Fori(0, E0 // SETS) as i:
                for s in range(SETS):
                    e = SETS * i + s
                    act.wait_ge(ex_g, e + 1)
                    if s >= 2:
                        act.wait_ge(ex_h, e - 1)
                    else:
                        act.wait_ge(ex_h, SETS * i)
                    act.activation(e_act[0:FH, s % 2], bank[2 + s % 2][0:FH, 0:2 * P].rearrange("p (f n) -> p f n", f=2),
                                   ACT.Silu).then_inc(ex_act, 1)

            def unit(p, u):
                g = UNITS * p + u
                copy_probsT(act, g - 3, (u - 3) % 4)
                act.wait_ge(at_min, g + 1)
                at_least(act, at_t, g - 3)
                for q in range(QT):
                    act.activation(probs[:, u % 4, q, :], bank[3 + u % 2][:, q * S:(q + 1) * S], ACT.Exp, scale=-1.0,
                                   bias=row_min[:, u % 4, q:q + 1], accum_out=row_sum[:, u % 4, q:q + 1])\
                        .then_inc(at_exp, 1)

            def copy_probsT(act, g, slot):
                if isinstance(g, int) and g < 0:
                    return
                act.wait_ge(at_t, g + 1)
                at_least(act, at_pv, g - 1)
                act.activation(probsT[:, slot % 2], bank[5 + slot % 2][:, :].rearrange("p (a b) -> p a b", a=QT), ACT.Copy)\
                    .then_inc(at_tout, 1)

            for u in range(UNITS):
                unit(0, u)
            with act.Fori(0, PAIRS // 2 - 1) as i:
                for p in range(2):
                    for u in range(UNITS):
                        unit(2 * i + 1 + p, u)
            for u in range(UNITS):
                unit(PAIRS - 1, u)
            for g in range(PAIRS * UNITS - 3, PAIRS * UNITS):
                copy_probsT(act, g, g % 4)

            act.wait_ge(cf_in, 16)
            for i in range(NT):
                act.wait_ge(ln_mv, NT + i + 1)
                act.activation(sd[:, i:i + 1], mv[:, i, 1:2], ACT.Sqrt, bias=table("eps_norm")).then_inc(l1_sd, 1)
                if i in (3, 5, 7):
                    turned_copy(8 + (i - 3) // 2, x1T)
            for i in range(NT):
                if i == 4:
                    turned_copy(11, x1T)
                act.wait_ge(qkv_mm, i + 1)
                src = bank[5 + 2 * (i % 2)]
                act.activation(v_tok[:, i, :], src[:, 0:D], ACT.Copy)
                act.activation(logit1[:, i, :], src[:, D:D + E1], ACT.Copy).then_inc(v_out, 1)
            for i in range(NT):
                act.wait_ge(qkT_mm, i + 1)
                act.activation(qkT[:, :, i * P:(i + 1) * P], bank[i % 4][:, :].rearrange("p (a n) -> p a n", a=4), ACT.Copy)\
                    .then_inc(qkT_out, 1)
            act.wait_ge(r1_sub, 1)
            act.activation(expo1, logit1, ACT.Exp).then_inc(r1_exp, 1)
            for n, (what, j, h, c) in enumerate(fills()):
                act.wait_ge(fill_mm, n + 1)
                cols = slice(c * CH, (c + 1) * CH)
                dst = {"low": am_step[j][:, h, cols], "mask": (first_maskT, second_maskT)[j][:, h, cols],
                       "share": shareT[:, j, cols]}[what]
                act.activation(dst, bank[4 + n % 4][:, :], ACT.Copy).then_inc(fill_out, 1)

            def unit1(g, u):
                copy_probs1T(g - 2, (u - 2) % HG)
                act.wait_ge(bl_min, 2 * g + 2)
                at_least(act, bl_t, g - 3)
                at_least(act, bl_inv, g - 3)
                for q, (a, b) in enumerate(((0, P), (P, 3 * P))):
                    act.activation(probs1[:, u % 4, a:b], masked[:, u % 4, a:b], ACT.Exp, scale=-1.0,
                                   bias=row_min[:, u % 4, q:q + 1], accum_out=row_sum[:, u % 4, q:q + 1])\
                        .then_inc(bl_exp, 1)

            def copy_probs1T(g, u):
                if isinstance(g, int) and g < 0:
                    return
                act.wait_ge(bl_t, g + 1)
                at_least(act, bl_v, g - 1)
                act.activation(probs1T[:, u % 2, :], bank[5 + u % 2][:, 0:3 * P], ACT.Copy).then_inc(bl_tout, 1)

            for u in range(HG):
                unit1(u, u)
            with act.Fori(0, GROUPS // 2 - 1) as i:
                for k in range(2):
                    for u in range(HG):
                        unit1(HG * (2 * i + 1 + k) + u, u)
            for u in range(HG):
                unit1(HG * (GROUPS - 1) + u, u)
            for g in range(GROUPS * HG - 2, GROUPS * HG):
                copy_probs1T(g, g % HG)
            act.wait_ge(bl_o, GROUPS * HG)
            act.activation(squares, o_tok.rearrange("p t (h d) -> p (t h) d", d=D1), ACT.Square).then_inc(on_sq, 1)
            act.wait_ge(on_step, 2)
            act.activation(o_sd, o_var, ACT.Sqrt).then_inc(on_sd, 1)
            m = 0
            for c in range(TOK // CH):
                for n, (f, k) in enumerate(uses()):
                    act.wait_ge(f_mm, m + 1)
                    at_least(act, f_h, m - 1)
                    act.activation(f_act[:, m % 2, :], bank[2 * (f % 3)][:, :], ACT.Silu).then_inc(f_silu, 1)
                    m += 1
                    if c == 0 and n == 4:
                        for g in range(12, 16):
                            turned_copy(g, oT)

        @block.vector
        def _(dve):
            for i in range(NT):
                dve.wait_ge(x_in[i // 2], 16)
                dve.bn_stats(stats[:, i, :], acc[:, i, :]).then_inc(ln_stats, 1)
            for i in range(NT):
                dve.wait_ge(ln_stats, i + 1)
                dve.bn_aggr(mv[:, i, :], stats[:, i, :]).then_inc(ln_mv, 1)
            dve.wait_ge(ln_mv, NT)
            dve.tensor_scalar(var, mv[:, :, 1], 1e-5, None, ALU.add).then_inc(ln_var, 1)
            dve.wait_ge(ln_sd, 1)
            dve.reciprocal(rstd, sd).then_inc(ln_rstd, 1)
            dve.wait_ge(ln_rstd, 1)
            dve.tensor_tensor(ms, mv[:, :, 1], rstd, ALU.mult).then_inc(ms_step, 1)
            for i in range(NT):
                dve.tensor_scalar(xn[:, i, :], acc[:, i, :], mv[:, i, 0:1], rstd[:, i:i + 1], ALU.subtract, ALU.mult)\
                    .then_inc(xn_done, 1)
                if i == 0:
                    dve.wait_ge(ms_step, 1)
                    dve.tensor_tensor(ms, ms, rstd, ALU.mult).then_inc(ms_step, 1)
                if i == 1:
                    dve.wait_ge(ms_step, 2)
                    dve.tensor_scalar(ms, ms, 1e-6, None, ALU.add).then_inc(ms_var, 1)
            dve.wait_ge(ms_sd, 1)
            dve.reciprocal(rrms, sd2).then_inc(ms_inv, 1)
            dve.wait_ge(ms_inv, 1)
            dve.wait_ge(rows_in, 16)
            for i in range(NT):
                dve.wait_ge(xn_done, i + 1)
                dve.scalar_tensor_tensor(x2[:, i, :], xn[:, i, :], rrms[:, i:i + 1], row("w_norm"), ALU.mult, ALU.mult)\
                    .then_inc(x2_done, 1)

            for i in range(NT):
                dve.wait_ge(lat_out, i + 1)
                dve.bn_stats(lat_stats[:, 2 * i, :], lat[:, i, 0:QL]).then_inc(lat_st, 1)
                dve.bn_stats(lat_stats[:, 2 * i + 1, :], lat[:, i, QL:QL + KVL]).then_inc(lat_st, 1)
            for i in range(2 * NT):
                dve.wait_ge(lat_st, i + 1)
                dve.bn_aggr(lat_mv[:, i, :], lat_stats[:, i, :]).then_inc(lat_ag, 1)
            dve.wait_ge(lat_ag, 2 * NT)
            dve.tensor_scalar(lat_var, lat_mv[:, :, 1], 1e-5, None, ALU.add).then_inc(lat_vr, 1)

            scores = [bank[6 + i][:, :].rearrange("p (t n) -> p t n", t=4) for i in range(2)]
            for i in range(2):
                dve.wait_ge(logit_mm, 4 * i + 4)
                dve.tensor_reduce(route_max[:, 4 * i:4 * i + 4], scores[i][:, :, 0:E0], AX.X, ALU.max).then_inc(rt_max, 1)
            for i in range(2):
                dve.wait_ge(rt_max, i + 1)
                dve.tensor_tensor(logit[:, 4 * i:4 * i + 4, :], scores[i][:, :, 0:E0],
                                  along(route_max[:, 4 * i:4 * i + 4], (2, E0)), ALU.subtract).then_inc(rt_sub, 1)
                dve.tensor_copy(gate_z[:, 4 * i:4 * i + 4], scores[i][:, :, E0]).then_inc(rt_sub, 1)

            dve.wait_ge(lat_sdev, 1)
            dve.reciprocal(lat_rstd, lat_sd).then_inc(lat_rs, 1)
            dve.wait_ge(lat_rs, 1)
            for i in range(NT):
                for j, a, b in ((2 * i, 0, QL), (2 * i + 1, QL, QL + KVL)):
                    dve.tensor_scalar(lat[:, i, a:b], lat[:, i, a:b], lat_mv[:, j, 0:1], lat_rstd[:, j:j + 1],
                                      ALU.subtract, ALU.mult).then_inc(lat_norm, 1)
            for q in range(QT):
                for name, a in (("k_cos", QL + KVL), ("k_sin", QL + KVL + DR)):
                    part = lat[:, q::QT, a:a + DR]
                    dve.tensor_tensor(part, part, along(table(name, QT, DR)[:, q, :], (1, B)), ALU.mult)\
                        .then_inc(lat_rope, 1)
            dve.wait_ge(lat_norm, 2 * NT)
            dve.tensor_tensor(lat[:, :, 0:QL + KVL], lat[:, :, 0:QL + KVL], along(row("lat_w"), (1, NT)), ALU.mult)\
                .then_inc(lat_scaled, 1)
            dve.wait_ge(lat_rope, 4)
            dve.tensor_tensor(kv_tok[:, :, KVL:2 * KVL], lat[:, :, QL + KVL:QL + KVL + DR], lat[:, :, QL + KVL + DR:LATW],
                              ALU.add).then_inc(lat_done, 1)
            dve.wait_ge(lat_scaled, 1)
            kv_b = along(row("lat_b")[:, QL:QL + KVL], (1, NT))
            for a in (0, 2 * KVL):
                dve.tensor_tensor(kv_tok[:, :, a:a + KVL], lat[:, :, QL:QL + KVL], kv_b, ALU.add).then_inc(lat_done, 1)
            dve.tensor_tensor(lat[:, :, 0:QL], lat[:, :, 0:QL], along(row("lat_b")[:, 0:QL], (1, NT)), ALU.add)\
                .then_inc(lat_done, 1)

            dve.wait_ge(rt_exp, 2)
            dve.tensor_reduce(route_sum, expo, AX.X, ALU.add).then_inc(rt_step, 1)
            dve.tensor_scalar(gate1, gate_e, 1.0, None, ALU.add).then_inc(rt_step, 1)
            dve.wait_ge(rt_step, 2)
            dve.reciprocal(route_inv, route_sum).then_inc(rt_step, 1)
            dve.reciprocal(gate, gate1).then_inc(rt_step, 1)
            dve.wait_ge(rt_step, 4)
            dve.tensor_tensor(prob, expo, along(route_inv, (2, E0)), ALU.mult).then_inc(rt_step, 1)
            dve.wait_ge(rt_step, 5)
            for i in range(NT):
                dve.max(top[:, i, :], prob[:, i, :]).then_inc(rt_step, 1)
            for i in range(NT):
                dve.wait_ge(rt_step, 6 + i)
                dve.max_index(top_at[:, i, :], top[:, i, :], prob[:, i, :]).then_inc(rt_step, 1)
            dve.wait_ge(rt_step, 5 + 2 * NT)
            dve.tensor_copy(chosen, top_at[:, :, 0:TOPK0]).then_inc(rt_step, 1)
            dve.wait_ge(rt_step, 6 + 2 * NT)
            flat = onehot.rearrange("p t k e -> p (t k) e")
            chosen_flat = chosen.rearrange("p t k -> p (t k)")
            dve.tensor_tensor(flat, along(table("iota"), (1, NT * TOPK0)), along(chosen_flat, (2, E0)), ALU.is_equal)\
                .then_inc(rt_step, 1)
            dve.wait_ge(rt_step, 7 + 2 * NT)
            dve.tensor_reduce(mask, onehot.rearrange("p t k e -> p t e k"), AX.X, ALU.add).then_inc(rt_step, 1)
            dve.wait_ge(rt_step, 8 + 2 * NT)
            dve.tensor_copy(maskb, mask).then_inc(rt_mask, 1)

            dve.memset(qk[QL - P:P, 3, :], 0.0).then_inc(pad_set, 1)
            for i in range(NT):
                dve.wait_ge(latT_mm, i + 1)
                src = bank[4 + i % 2][:, :].rearrange("p (a n) -> p a n", a=4)
                dve.tensor_copy(qk[:, 0:3, i * P:(i + 1) * P], src[:, 0:3, :]).then_inc(latT_out, 1)
                dve.tensor_copy(qk[0:QL - P, 3, i * P:(i + 1) * P], src[0:QL - P, 3, :]).then_inc(latT_out, 1)

            dve.wait_ge(rt_pos, 1)
            pos = bank[6][:, 0:NT * E0].rearrange("p (t e) -> p t e", e=E0)
            dve.tensor_tensor(onehot, onehot, along(pos, (2, TOPK0)), ALU.mult).then_inc(rt_step, 1)
            n = 9 + 2 * NT
            dve.wait_ge(rt_step, n)
            dve.tensor_reduce(place4, flat, AX.X, ALU.add).then_inc(rt_step, 1)
            dve.wait_ge(rt_step, n + 1)
            dve.tensor_scalar(over, place4, CAP - 0.5, None, ALU.is_gt).then_inc(rt_step, 1)
            dve.tensor_scalar(clipped, place4, CAP - 1.0, None, ALU.min).then_inc(rt_step, 1)
            dve.wait_ge(rt_step, n + 3)
            dve.scalar_tensor_tensor(source_f, chosen_flat, float(CAP), clipped, ALU.mult, ALU.add).then_inc(rt_step, 1)
            dve.scalar_tensor_tensor(weight4.rearrange("p (t k) -> p t k", k=TOPK0),
                                     over.rearrange("p (t k) -> p t k", k=TOPK0), 0.5, top[:, :, 0:TOPK0],
                                     ALU.is_lt, ALU.mult).then_inc(rt_step, 1)
            dve.wait_ge(rt_step, n + 5)
            dve.scalar_tensor_tensor(dest_f, over, 65536.0, source_f, ALU.mult, ALU.add).then_inc(rt_step, 1)
            dve.wait_ge(rt_step, n + 6)
            dve.tensor_copy(dest, dest_f).then_inc(rt_dest, 1)
            dve.tensor_copy(source, source_f).then_inc(rt_dest, 1)
            dve.wait_ge(rt_dest, 2)
            for i in range(2):
                dve.memset(w_eff[i][QL - P:P, 1, :], 0.0).then_inc(eff_pad, 1)

            for i in range(NT):
                dve.wait_ge(sh_down, i + 1)
                dve.wait_ge(acc_done, i + 1)
                dve.scalar_tensor_tensor(acc[:, i, :], bank[i % 4][:, 0:D], gate[:, i:i + 1], acc[:, i, :],
                                         ALU.mult, ALU.add).then_inc(sh_add, 1)

            def rows_out(e, s):
                dve.wait_ge(ex_t, e + 1)
                at_least(dve, ex_g, e - 1)
                dve.tensor_copy(xeT[s % 2], bank[s % 2][:, 0:KD * P].rearrange("p (k n) -> p k n", k=KD))\
                    .then_inc(ex_tout, 1)

            def hidden(e, s):
                dve.wait_ge(ex_act, e + 1)
                at_least(dve, ex_done, e - 1)
                dve.tensor_tensor(e_hid[0:FH, s % 2], e_act[0:FH, s % 2],
                                  bank[2 + s % 2][0:FH, 2 * P:4 * P].rearrange("p (f n) -> p f n", f=2), ALU.mult)\
                    .then_inc(ex_h, 1)

            def result(e, s, turn):
                dve.wait_ge(ex_done, e + 1)
                at_least(dve, y_stored[s], 16 * turn)
                dve.tensor_copy(ye[:, s, :], bank[4 + s % 2][:, 0:D]).then_inc(ex_y, 1)

            rows_out(0, 0)
            rows_out(1, 1)
            hidden(0, 0)
            with dve.Fori(0, E0 // SETS - 1) as i:
                for k in range(1, SETS + 1):
                    rows_out(SETS * i + k + 1, (k + 1) % SETS)
                    hidden(SETS * i + k, k % SETS)
                    result(SETS * i + k - 1, k - 1, i)
            for e in range(E0 - SETS + 1, E0):
                if e + 1 < E0:
                    rows_out(e + 1, (e + 1) % SETS)
                hidden(e, e % SETS)
                result(e - 1, (e - 1) % SETS, (e - 1) // SETS)
            result(E0 - 1, SETS - 1, E0 // SETS - 1)

            def effective(p, i):
                dve.wait_ge(at_m, p + 1)
                at_least(dve, at_q, 6 * (p - 1))
                m = bank[0][:, :].rearrange("p (h k n) -> p h k n", h=2, k=2)
                for h, a in ((0, 0), (1, 3 * DR)):
                    dve.tensor_copy(w_eff[i][:, 0, a:a + DR], m[:, h, 0, 0:KVL])
                    dve.tensor_copy(w_eff[i][0:QL - P, 1, a:a + DR], m[0:QL - P, h, 1, 0:KVL])
                for h in range(2):
                    rows_h = slice(h * KVL, (h + 1) * KVL)
                    ins = dve.tensor_copy(w_vo[rows_h, bass.ds(p, 1), :], bank[1][rows_h, h * D:(h + 1) * D].unsqueeze(1))
                ins.then_inc(at_eff, 1)

            def queries(p, m, i):
                c, j = m // 3, m % 3
                half = slice(c * CH, (c + 1) * CH)
                dve.wait_ge(at_q, 6 * p + m + 1)
                at_least(dve, at_s, UNITS * (p - 1))
                at_least(dve, at_qe, 4 * p + 2 * c)
                name, dst = (("q_sin", q_tmp), ("q_even", qb[i][:, 0, half]), ("q_odd", qb[i][:, 1, half]))[j]
                dve.tensor_tensor(dst.rearrange("p (b s) -> p b s", s=S),
                                  bank[m % 2][:, :].rearrange("p (b s) -> p b s", s=S),
                                  along(table(name), (1, CH // S)), ALU.mult).then_inc(at_qrope, 1)
                if j == 2:
                    dve.wait_ge(at_qrope, 6 * p + m + 1)
                    dve.tensor_tensor(qb[i][DR:P, 0, half], qb[i][DR:P, 0, half], q_tmp[DR:P], ALU.add)\
                        .then_inc(at_qe, 1)
                    dve.tensor_tensor(qb[i][0:DR, 1, half], qb[i][0:DR, 1, half], q_tmp[0:DR], ALU.add)\
                        .then_inc(at_qe, 1)

            def minimum(g, u):
                dve.wait_ge(at_s, g + 1)
                at_least(dve, at_exp, 2 * g - 6)
                dve.tensor_reduce(row_min[:, u % 4, :], bank[3 + u % 2][:, :].rearrange("p (q n) -> p q n", q=QT),
                                  AX.X, ALU.min).then_inc(at_min, 1)

            def normalise(g, u):
                dve.wait_ge(at_exp, 2 * g + 2)
                dve.reciprocal(row_inv[:, u % 4, :], row_sum[:, u % 4, :]).then_inc(at_inv, 1)
                dve.wait_ge(at_inv, g + 1)
                for q in range(QT):
                    ins = dve.tensor_scalar(probs[:, u % 4, q, :], probs[:, u % 4, q, :], row_inv[:, u % 4, q:q + 1], None,
                                            ALU.mult)
                ins.then_inc(at_norm, 1)

            def context(g, p, u):
                dve.wait_ge(at_pv, g + 1)
                b, h = u // 2, u % 2
                dve.tensor_copy(ctxT[h * KVL:(h + 1) * KVL, bass.ds(p, 1), b * S:(b + 1) * S],
                                bank[2 + 5 * h][0:KVL, 0:S].unsqueeze(1)).then_inc(at_ctx, 1)

            def pair(p, i, first, last):
                for u in range(UNITS):
                    g = UNITS * p + u
                    minimum(g, u)
                    if not (first and u < 4):
                        context(g - 4, p - 1 if u < 4 else p, (u - 4) % UNITS)
                    if not (first and u < 1):
                        normalise(g - 1, u - 1)
                    if not last:
                        if u == 1:
                            effective(p + 1, 1 - i)
                        if u >= 2:
                            queries(p + 1, u - 2, 1 - i)

            effective(0, 0)
            for m in range(6):
                queries(0, m, 0)
            pair(0, 0, True, False)
            with dve.Fori(0, PAIRS // 2 - 1) as i:
                for k in range(2):
                    pair(2 * i + 1 + k, 1 - k, False, False)
            pair(PAIRS - 1, 1, False, True)
            G = PAIRS * UNITS
            normalise(G - 1, UNITS - 1)
            for g in range(G - 4, G):
                context(g, PAIRS - 1, g % UNITS)

            dve.wait_ge(combined, TOPK0)

            def normal1(i):
                dve.wait_ge(l1_sd, i + 1)
                dve.reciprocal(rstd[:, i:i + 1], sd[:, i:i + 1]).then_inc(ln_rstd, 1)
                dve.wait_ge(ln_rstd, i + 2)
                dve.tensor_scalar(xn1[:, i, :], acc[:, i, :], mv[:, i, 0:1], rstd[:, i:i + 1], ALU.subtract, ALU.mult)\
                    .then_inc(xn_done, 1)

            for i in range(NT):
                dve.wait_ge(op_mm, i + 1)
                dve.tensor_tensor(acc[:, i, :], bank[i % 2][:, 0:D], acc[:, i, :], ALU.add).then_inc(op_add, 1)
                dve.wait_ge(op_add, i + 1)
                dve.bn_stats(stats[:, i, :], acc[:, i, :]).then_inc(ln_stats, 1)
                dve.wait_ge(ln_stats, NT + i + 1)
                dve.bn_aggr(mv[:, i, :], stats[:, i, :]).then_inc(ln_mv, 1)
                if i:
                    normal1(i - 1)
            normal1(NT - 1)

            for i in range(NT):
                dve.wait_ge(qkv_mm, i + 1)
                at_least(dve, rope_add, i - 1)
                src = bank[4 + 2 * (i % 2)][:, :].rearrange("p (h d) -> p h d", d=D1)
                cos_t = table("cos1", QT, D1)[:, i % QT, :]
                sin_t = table("sin1", QT, D1)[:, i % QT, :]
                by_cos = rope_tmp[:, i % 2, 0, :].rearrange("p (h d) -> p h d", d=D1)
                by_sin = rope_tmp[:, i % 2, 1, :].rearrange("p (h d) -> p h d", d=D1)
                half = D1 // 2
                dve.tensor_tensor(by_cos, src, along(cos_t, (1, 2 * H1)), ALU.mult).then_inc(rope_mul, 1)
                dve.tensor_tensor(by_sin[:, :, 0:half], src[:, :, half:D1], along(sin_t[:, 0:half], (1, 2 * H1)), ALU.mult)\
                    .then_inc(rope_mul, 1)
                dve.tensor_tensor(by_sin[:, :, half:D1], src[:, :, 0:half], along(sin_t[:, half:D1], (1, 2 * H1)), ALU.mult)\
                    .then_inc(rope_mul, 1)

            dve.wait_ge(v_out, NT)
            dve.tensor_reduce(max1, logit1, AX.X, ALU.max).then_inc(r1_step, 1)
            dve.wait_ge(r1_step, 1)
            dve.tensor_tensor(logit1, logit1, along(max1, (2, E1)), ALU.subtract).then_inc(r1_sub, 1)

            dve.wait_ge(qkT_out, NT)
            dve.tensor_reduce(kblock, qkT[:, 2:4, :].rearrange("p k (n c) -> p k n c", c=CHUNK), AX.X, ALU.add)\
                .then_inc(kmean_done, 1)
            dve.wait_ge(kmean_done, 1)
            dve.wait_ge(kmean_set, 1)
            for k in range(KD):
                for h in range(HG):
                    at = (k * HG + h) * NB
                    dve.tensor_scalar(kmean[:, k, :, at:at + NB], kblock[:, k, :].rearrange("p (b n) -> p b n", n=NB),
                                      table("head_mean")[:, h:h + 1], None, ALU.mult).then_inc(kmean_done, 1)

            dve.wait_ge(r1_exp, 1)
            dve.tensor_reduce(sum1, expo1, AX.X, ALU.add).then_inc(r1_step, 1)
            dve.wait_ge(r1_step, 2)
            dve.reciprocal(inv1, sum1).then_inc(r1_step, 1)
            dve.wait_ge(r1_step, 3)
            dve.tensor_tensor(prob1, expo1, along(inv1, (2, E1)), ALU.mult).then_inc(r1_step, 1)
            dve.wait_ge(r1_step, 4)
            for i in range(NT):
                dve.max(top1[:, i, :], prob1[:, i, :]).then_inc(r1_step, 1)
            for i in range(NT):
                dve.wait_ge(r1_step, 5 + i)
                dve.max_index(top1_at[:, i, :], top1[:, i, :], prob1[:, i, :]).then_inc(r1_step, 1)
            dve.wait_ge(r1_step, 4 + 2 * NT)
            dve.tensor_copy(chosen1, top1_at[:, :, 0:2]).then_inc(r1_step, 1)
            dve.tensor_tensor(sum1, top1[:, :, 0], top1[:, :, 1], ALU.add).then_inc(r1_step, 1)
            dve.wait_ge(r1_step, 6 + 2 * NT)
            dve.reciprocal(inv1, sum1).then_inc(r1_step, 1)

            g_b = score_blk.rearrange("p (b n) m -> p b (n m)", b=B)
            for i in range(2):
                dve.wait_ge(blk_mm, 4 * i + 4)
                dve.tensor_tensor(g_b[:, 2 * i:2 * i + 2, :], bank[i][:, :].rearrange("p (b n) -> p b n", b=2),
                                  along(table("keep"), (1, 2)), ALU.mult).then_inc(blk_step, 1)
            dve.tensor_copy(rank.rearrange("p t (h n) -> p (t h) n", n=NB), along(table("later"), (1, NT * H1))).then_inc(blk_step, 1)
            dve.wait_ge(blk_step, 2)
            dve.tensor_tensor(g_b, g_b, along(table("force"), (1, B)), ALU.add).then_inc(blk_step, 1)
            dve.wait_ge(blk_step, 4)
            compare(dve, rest_heads, beats_rest, rest_beats)
            compare(dve, first_heads, beats_first, blk_beats)

            for k in range(2):
                for i in range(NT):
                    dve.tensor_scalar(expert_of[k][:, i, :], table("slot_expert"), chosen1[:, i, k:k + 1], None,
                                      ALU.is_equal).then_inc(r1_own, 1)
            dve.wait_ge(r1_step, 7 + 2 * NT)
            dve.tensor_tensor(share, top1[:, :, 0:2], along(inv1, (2, 2)), ALU.mult).then_inc(r1_step, 1)
            dve.wait_ge(r1_step, 8 + 2 * NT)
            for n in range(2 * NT):
                k, i = n // NT, n % NT
                if n >= 4:
                    dve.wait_ge(fill_mm, 16 + n // 4)
                dve.tensor_scalar(share_rep[:, n % 4, :], table("ones"), share[:, i, k:k + 1], None, ALU.mult)\
                    .then_inc(r1_share, 1)

            dve.wait_ge(blk_beats, NB - 1)
            count(dve, first_heads, beats_first, blk_count, 0)

            def own_queries(G, b, k, u):
                at_least(dve, bl_s, HG * (G - 1))
                dve.tensor_scalar(q_head[k][:, u, :], qkT[:, k, bass.ds(b * S, S)], table("head_scale")[:, u:u + 1], None,
                                  ALU.mult).then_inc(bl_q, 1)

            def own_bias(G, b, k):
                at_least(dve, bl_min, 2 * HG * (G - 1))
                if not (isinstance(b, int) and b == 0):
                    dve.wait_ge(rest_count, 2 * (NB - 1))
                half = slice(k * HG * NB, (k + 1) * HG * NB)
                dve.tensor_scalar(bias_g[:, k], rank[:, bass.ds(QT * b, QT), half], TOPK1 - 0.5, BIG, ALU.is_gt, ALU.mult)\
                    .then_inc(bl_bias, 1)
                dve.wait_ge(bl_bias, 2 * G + 1)
                dve.tensor_tensor(bias_g[:, k], bias_g[:, k],
                                  table("future").rearrange("p (q n) -> p q n", q=QT)[:, :, half], ALU.max)\
                    .then_inc(bl_bias, 1)

            def masked_minimum(g, G, k, u, meanwhile):
                dve.wait_ge(bl_s, g + 1)
                dve.wait_ge(bl_bias, 2 * G + 2)
                at_least(dve, bl_exp, 2 * g - 6)
                meanwhile()
                for q, (a, b) in enumerate(((0, P), (P, 3 * P))):
                    n = (b - a) // CHUNK
                    dve.tensor_tensor_reduce(
                        masked[:, u % 4, a:b].rearrange("p (n c) -> p n c", c=CHUNK),
                        bank[3 + u % 2][:, a:b].rearrange("p (n c) -> p n c", c=CHUNK),
                        along(bias_g[:, k, q, u * NB:u * NB + n], (2, CHUNK)), 1.0, HUGE, ALU.add, ALU.min,
                        row_min[:, u % 4, q:q + 1]).then_inc(bl_min, 1)

            def inverse(g, u):
                dve.wait_ge(bl_exp, 2 * g + 2)
                at_least(dve, bl_o, g - 3)
                dve.reciprocal(row_inv[:, u % 4, :], row_sum[:, u % 4, :]).then_inc(bl_inv, 1)

            def head_out(g, b, k, u):
                dve.wait_ge(bl_v, g + 1)
                dve.wait_ge(bl_inv, g + 1)
                h = (k * HG + u) * D1
                dve.tensor_tensor(o_tok[:, bass.ds(QT * b, QT), h:h + D1],
                                  bank[2 + 5 * (u % 2)][:, 0:2 * P].rearrange("p (q n) -> p q n", q=QT)[:, :, u * D1:(u + 1) * D1],
                                  along(row_inv[:, u % 4, :], (2, D1)), ALU.mult).then_inc(bl_o, 1)

            def group(G, b, k, before, after):
                if after is not None:
                    own_bias(G + 1, after, 1 - k)
                for u in range(HG):
                    g = HG * G + u
                    masked_minimum(g, G, k, u, lambda: own_queries(G + 1, after, 1 - k, u) if after is not None else None)
                    if u >= 4:
                        head_out(g - 4, b, k, u - 4)
                    elif before is not None:
                        head_out(g - 4, before, 1 - k, u + 4)
                    if u >= 2 or before is not None:
                        inverse(g - 2, (u - 2) % HG)

            own_bias(0, 0, 0)
            for u in range(HG):
                own_queries(0, 0, 0, u)
            group(0, 0, 0, None, 0)
            with dve.Fori(0, GROUPS // 2 - 1) as i:
                group(2 * i + 1, i, 1, i, i + 1)
                group(2 * i + 2, i + 1, 0, i, i + 1)
            group(GROUPS - 1, B - 1, 1, B - 1, None)
            G = GROUPS * HG
            inverse(G - 2, HG - 2)
            inverse(G - 1, HG - 1)
            for g in range(G - 4, G):
                head_out(g, B - 1, 1, g % HG)

            o_heads = o_tok.rearrange("p t (h d) -> p (t h) d", d=D1)
            o_var_f, o_inv_f = o_var.rearrange("p t h -> p (t h)"), o_inv.rearrange("p t h -> p (t h)")
            dve.wait_ge(on_sq, 1)
            dve.tensor_reduce(o_var_f, squares, AX.X, ALU.add).then_inc(on_step, 1)
            dve.wait_ge(on_step, 1)
            dve.tensor_scalar(o_var, o_var, 1.0 / D1, 1e-6, ALU.mult, ALU.add).then_inc(on_step, 1)
            dve.wait_ge(on_sd, 1)
            dve.reciprocal(o_inv, o_sd).then_inc(on_step, 1)
            dve.wait_ge(on_step, 3)
            dve.tensor_tensor(o_heads, o_heads, along(o_inv_f, (2, D1)), ALU.mult).then_inc(on_step, 1)
            dve.wait_ge(on_step, 4)
            dve.tensor_tensor(o_heads, o_heads, along(row("o_norm"), (1, NT * H1)), ALU.mult).then_inc(on_done, 2)

            m = 0
            for c in range(TOK // CH):
                cols = slice(c * CH, (c + 1) * CH)
                for f, k in uses():
                    dve.wait_ge(f_silu, m + 1)
                    at_least(dve, f_x, m - 1)
                    dve.tensor_tensor(f_hid[:, m % 2, :], f_act[:, m % 2, :], bank[2 * (f % 3) + 1][:, :], ALU.mult)\
                        .then_inc(f_h, 1)
                    dve.wait_ge(f_h, m + 1)
                    if k == 0:
                        at_least(dve, f_a2, c)
                        dve.tensor_tensor(h_first[:, f, :], f_hid[:, m % 2, :], shareT[:, 0, cols], ALU.mult)\
                            .then_inc(f_x, 1)
                    else:
                        at_least(dve, f_down, 4 * c)
                        dve.tensor_tensor(h_both[:, f, :], f_hid[:, m % 2, :], shareT[:, 1, cols], ALU.mult)\
                            .then_inc(f_x, 1)
                        dve.wait_ge(f_x, m + 1)
                        dve.tensor_tensor(h_both[:, f, :], h_both[:, f, :], h_first[:, f, :], ALU.add).then_inc(f_x2, 1)
                    m += 1
                dve.wait_ge(f_a2, c + 1)
                at_least(dve, f_down, 4 * c)
                for h in range(2):
                    at_least(dve, f_am2, 3 * (2 * c + h))
                    dve.tensor_tensor(am2_tmp, bank[4 + h][:, :], step_maskT[:, h, cols], ALU.mult).then_inc(f_am2, 1)
                    dve.tensor_tensor(am2[:, h, :], bank[6 + h][:, :], second_maskT[:, h, cols], ALU.mult).then_inc(f_am2, 1)
                    dve.wait_ge(f_am2, 3 * (2 * c + h) + 2)
                    dve.tensor_tensor(am2[:, h, :], am2[:, h, :], am2_tmp, ALU.subtract).then_inc(f_am2, 1)
                for i in range(4):
                    dve.wait_ge(f_down, 4 * c + i + 1)
                    dve.tensor_tensor(acc[:, 4 * c + i, :], bank[i][:, 0:D], acc[:, 4 * c + i, :], ALU.add)\
                        .then_inc(y_done, 1)

        @block.tensor
        def _(pe):
            def turn(g, src, ready):
                pe.wait_ge(ready, 2 * (g % 4) + 2)
                at_least(pe, turned_out, g - 3)
                for k in range(KD):
                    for i in range(2):
                        mm = pe.transpose(bank[g % 4][:, (2 * k + i) * P:(2 * k + i + 1) * P],
                                          src[:, 2 * (g % 4) + i, k * P:(k + 1) * P], ident)
                mm.then_inc(turned, 1)

            pe.wait_ge(cf_in, 16)
            for g in range(4):
                turn(g, xn, xn_done)
            pe.wait_ge(lat_in, 16)
            for i in range(NT):
                pe.wait_ge(turned_out, i // 2 + 1)
                at_least(pe, lat_out, i - 1)
                for k in range(KD):
                    mm = pe.matmul(bank[4 + i % 2][:, 0:LATW], xnT[:, k, i * P:(i + 1) * P], w_lat[:, k, :],
                                   start=(k == 0), stop=(k == KD - 1))
                mm.then_inc(lat_mm, 1)
            for g in range(4, 8):
                turn(g, x2, x2_done)
            pe.wait_ge(route_in, 16)
            for i in range(NT):
                pe.wait_ge(turned_out, 5 + i // 2)
                for k in range(KD):
                    mm = pe.matmul(bank[6 + i // 4][:, (i % 4) * P:(i % 4 + 1) * P], x2T[:, k, i * P:(i + 1) * P],
                                   w_route[:, k, :], start=(k == 0), stop=(k == KD - 1))
                mm.then_inc(logit_mm, 1)

            def shared_up(u):
                f, c = u // 2, u % 2
                at_least(pe, sh_act, 2 * u - 2)
                for j in range(2):
                    for k in range(KD):
                        mm = pe.matmul(bank[2 * (u % 2) + j][:, :],
                                       sw_up[:, k, (j * NF + f) * P:(j * NF + f + 1) * P],
                                       x2T[:, k, c * CH:(c + 1) * CH], start=(k == 0), stop=(k == KD - 1))
                mm.then_inc(sh_mm, 1)

            def latents_turn(i):
                at_least(pe, latT_out, 2 * i - 2)
                dst = bank[4 + i % 2][:, :].rearrange("p (a n) -> p a n", a=4)
                pe.transpose(dst[:, 0, :], lat[:, i, 0:P], ident)
                pe.transpose(dst[:, 1, :], kv_tok[:, i, 0:2 * KVL], ident)
                pe.transpose(dst[:, 2, :], kv_tok[:, i, KVL:3 * KVL], ident)
                pe.transpose(dst[0:QL - P, 3, :], lat[:, i, P:QL], ident).then_inc(latT_mm, 1)

            pe.wait_ge(up_in, 16)
            for u in range(2 * NF):
                shared_up(u)
                if u == 6:
                    pe.wait_ge(lat_done, 4)
                    for i in range(NT):
                        latents_turn(i)
                if u == 7:
                    pe.wait_ge(rt_mask, 1)
                    pe.wait_ge(cb_in, 16)
                    pe.matmul(bank[6][:, 0:NT * E0], tableb("before"), maskb.rearrange("p t e -> p (t e)"),
                              start=True, stop=False, skip_group_check=True)
                    for i in range(NT - 1):
                        mm = pe.matmul(bank[6][:, (i + 1) * E0:NT * E0].rearrange("p (t e) -> p t e", e=E0),
                                       tableb("ones"), along(maskb[:, i, :], (1, NT - 1 - i)),
                                       start=False, stop=(i == NT - 2), skip_group_check=True)
                    mm.then_inc(rt_pos, 1)
            pe.wait_ge(down_in, 16)
            pe.wait_ge(sh_act, 4 * NF)
            pe.wait_ge(sh_h, 2 * NF)
            for i in range(NT):
                at_least(pe, sh_add, i - 3)
                for f in range(NF):
                    mm = pe.matmul(bank[i % 4][:, 0:D], hT[:, f, i * P:(i + 1) * P], sw_down[:, f, :],
                                   start=(f == 0), stop=(f == NF - 1))
                mm.then_inc(sh_down, 1)

            def rows_turn(e, s, turn_):
                pe.wait_ge(eb_in[s], 16 * turn_ + 16)
                at_least(pe, ex_tout, e - 1)
                for k in range(KD):
                    mm = pe.transpose(bank[s % 2][:, k * P:(k + 1) * P], xe[:, s, k * P:(k + 1) * P], ident)
                mm.then_inc(ex_t, 1)

            def gate_up(e, s, turn_):
                pe.wait_ge(ex_tout, e + 1)
                pe.wait_ge(ew_in[s], 32 * turn_ + 32)
                at_least(pe, ex_h, e - 1)
                for j in range(4):
                    for k in range(KD):
                        mm = pe.matmul(bank[2 + s % 2][0:FH, j * P:(j + 1) * P], w_gu[s][:, k, j * FH:(j + 1) * FH],
                                       xeT[s % 2][:, k, :], start=(k == 0), stop=(k == KD - 1))
                mm.then_inc(ex_g, 1)

            def down(e, s, read):
                pe.wait_ge(ex_h, e + 1)
                at_least(pe, ex_y, read)
                for f in range(2):
                    mm = pe.matmul(bank[4 + s % 2][:, 0:D], e_hid[0:FH, s % 2, f, :], w_dn[s][0:FH, f, :],
                                   start=(f == 0), stop=(f == 1))
                mm.then_inc(ex_done, 1)

            pe.wait_ge(sh_add, NT)
            pe.wait_ge(latT_out, 2 * NT)
            rows_turn(0, 0, 0)
            rows_turn(1, 1, 0)
            gate_up(0, 0, 0)
            with pe.Fori(0, E0 // SETS - 1) as i:
                for k in range(1, SETS + 1):
                    rows_turn(SETS * i + k + 1, (k + 1) % SETS, i + (k + 1) // SETS)
                    gate_up(SETS * i + k, k % SETS, i + k // SETS)
                    down(SETS * i + k - 1, k - 1, SETS * i + max(k - 2, 0))
            for e in range(E0 - SETS + 1, E0):
                if e + 1 < E0:
                    rows_turn(e + 1, (e + 1) % SETS, (e + 1) // SETS)
                gate_up(e, e % SETS, e // SETS)
                down(e - 1, (e - 1) % SETS, e - 2)
            down(E0 - 1, SETS - 1, E0 - 2)

            def merge(p, i, turn_):
                pe.wait_ge(pair_in[i], 48 * turn_ + 48)
                at_least(pe, at_qrope, 6 * p)
                for h in range(2):
                    for k, n in ((0, P), (1, QL - P)):
                        pe.matmul(bank[0][0:n, (2 * h + k) * P:(2 * h + k + 1) * P], w_q[i][:, h, k * P:k * P + n],
                                  w_vk[i][:, h, KVL:3 * KVL], start=True, stop=True)
                for h in range(2):
                    mm = pe.matmul(bank[1][:, h * D:(h + 1) * D], w_vk[i][:, h, h * KVL:h * KVL + 2 * KVL], w_o[i][:, h, :],
                                   start=True, stop=True)
                mm.then_inc(at_m, 1)

            def project(p, m, i):
                c, part = m // 3, (2, 0, 1)[m % 3]
                pe.wait_ge(at_eff, p + 1)
                at_least(pe, at_qrope, 6 * p + m - 1)
                for k in range(2):
                    mm = pe.matmul(bank[m % 2][:, :], w_eff[i][:, k, part * P:(part + 1) * P],
                                   qk[:, 3 * k, c * CH:(c + 1) * CH], start=(k == 0), stop=(k == 1))
                mm.then_inc(at_q, 1)

            def scores(g, p, u, i):
                b, h = u // 2, u % 2
                pe.wait_ge(at_qe, 4 * p + 2 * (b // 2) + 2)
                at_least(pe, at_exp, 2 * g - 2)
                for q in range(QT):
                    mm = pe.matmul(bank[3 + u % 2][:, q * S:(q + 1) * S],
                                   qb[i][:, h, b * S + q * P:b * S + (q + 1) * P], qk[:, 1 + h, b * S:(b + 1) * S],
                                   start=True, stop=True)
                mm.then_inc(at_s, 1)

            def probs_turn(g, u):
                pe.wait_ge(at_norm, g + 1)
                at_least(pe, at_tout, g - 1)
                dst = bank[5 + u % 2][:, :].rearrange("p (k n) -> p k n", k=QT)
                for k in range(QT):
                    for q in range(QT):
                        mm = pe.transpose(dst[:, k, q * P:(q + 1) * P], probs[:, u % 4, q, k * P:(k + 1) * P], ident)
                mm.then_inc(at_t, 1)

            def values(g, u):
                b, h = u // 2, u % 2
                pe.wait_ge(at_tout, g + 1)
                at_least(pe, at_ctx, g - 1)
                for k in range(QT):
                    mm = pe.matmul(bank[2 + 5 * h][0:KVL, 0:S], kv_tok[:, QT * b + k, 0:KVL],
                                   probsT[:, u % 2, k, :], start=(k == 0), stop=(k == QT - 1))
                mm.then_inc(at_pv, 1)

            def pair(p, i, turn_, first, last):
                for u in range(UNITS):
                    g = UNITS * p + u
                    scores(g, p, u, i)
                    if not (first and u < 2):
                        probs_turn(g - 2, (u - 2) % UNITS)
                    if not (first and u < 3):
                        values(g - 3, (u - 3) % UNITS)
                    if not last:
                        if u == 0:
                            merge(p + 1, 1 - i, turn_)
                        if u >= 2:
                            project(p + 1, u - 2, 1 - i)

            pe.wait_ge(ex_y, E0)
            merge(0, 0, 0)
            for m in range(6):
                project(0, m, 0)
            pair(0, 0, 0, True, False)
            with pe.Fori(0, PAIRS // 2 - 1) as i:
                for k in range(2):
                    pair(2 * i + 1 + k, 1 - k, i + 1 if k == 0 else i + 1, False, False)
            pair(PAIRS - 1, 1, 0, False, True)
            G = PAIRS * UNITS
            probs_turn(G - 2, UNITS - 2)
            values(G - 3, UNITS - 3)
            probs_turn(G - 1, UNITS - 1)
            values(G - 2, UNITS - 2)
            values(G - 1, UNITS - 1)

            def turn1(g, src, ready, n):
                pe.wait_ge(ready, n)
                at_least(pe, turned_out, g - 1)
                for k in range(KD):
                    for i in range(2):
                        mm = pe.transpose(bank[turn_bank(g)][:, (2 * k + i) * P:(2 * k + i + 1) * P],
                                          src[:, 2 * (g % 4) + i, k * P:(k + 1) * P], ident)
                mm.then_inc(turned, 1)

            for i in range(NT):
                pe.wait_ge(at_ctx, G - UNITS + 2 * (i // QT) + 2)
                at_least(pe, op_add, i - 1)
                for p in range(PAIRS):
                    mm = pe.matmul(bank[i % 2][:, 0:D], ctxT[:, p, i * P:(i + 1) * P], w_vo[:, p, :],
                                   start=(p == 0), stop=(p == PAIRS - 1))
                mm.then_inc(op_mm, 1)
                if i in (3, 5, 7):
                    g = 8 + (i - 3) // 2
                    turn1(g, xn1, xn_done, NT + 2 * (g % 4) + 2)

            pe.wait_ge(op_add, NT)
            pe.wait_ge(w3_in, 64)
            for i in range(NT):
                if i == 4:
                    turn1(11, xn1, xn_done, 2 * NT)
                pe.wait_ge(turned_out, 9 + i // 2)
                at_least(pe, rope_mul, 3 * (i - 1))
                at_least(pe, v_out, i - 1)
                for part, (a, b) in enumerate(((0, 2 * D), (2 * D, 3 * D + E1))):
                    for k in range(KD):
                        mm = pe.matmul(bank[4 + 2 * (i % 2) + part][:, 0:b - a], x1T[:, k, i * P:(i + 1) * P],
                                       w_qkvg[:, k, a:b], start=(k == 0), stop=(k == KD - 1))
                mm.then_inc(qkv_mm, 1)
            for i in range(NT):
                pe.wait_ge(rope_add, i + 1)
                at_least(pe, qkT_out, i - 3)
                for j in range(4):
                    mm = pe.transpose(bank[i % 4][:, j * P:(j + 1) * P], qk_tok[:, i, j * P:(j + 1) * P], ident)
                mm.then_inc(qkT_mm, 1)
            pe.wait_ge(rope_mul, 3 * NT)
            pe.wait_ge(v_out, NT)
            pe.wait_ge(kmean_done, 1 + KD * HG)
            for i in range(NT):
                for k in range(KD):
                    mm = pe.matmul(bank[i // 4][:, (i % 4) * P:(i % 4 + 1) * P], qkT[:, k, i * P:(i + 1) * P],
                                   kmean[:, k, i // QT, :], start=(k == 0), stop=(k == KD - 1))
                mm.then_inc(blk_mm, 1)
            for n, (what, j, h, c) in enumerate(fills()):
                at_least(pe, fill_out, n - 3)
                dst = bank[4 + n % 4]
                if what == "low":
                    for k in range(KD):
                        mm = pe.matmul(dst[:, :], a13[:, k, j * ER + h * P:j * ER + (h + 1) * P],
                                       x1T[:, k, c * CH:(c + 1) * CH], start=(k == 0), stop=(k == KD - 1))
                elif what == "mask":
                    pe.wait_ge(r1_own, NT * j + 4 * c + 4)
                    for i in range(4):
                        mm = pe.matmul(dst[:, i * P:(i + 1) * P], expert_of[j][:, 4 * c + i, h * P:(h + 1) * P], identb,
                                       start=True, stop=True)
                else:
                    pe.wait_ge(r1_share, 4 * (n - 16) + 4)
                    for i in range(4):
                        mm = pe.transpose(dst[:, i * P:(i + 1) * P], share_rep[:, i, :], ident)
                mm.then_inc(fill_mm, 1)

            def scores1(g, b, k, u):
                pe.wait_ge(bl_q, g + 1)
                at_least(pe, bl_min, 2 * g - 2)
                dst = bank[3 + u % 2]
                keys = qkT[:, 2 + k, bass.ds(b * S, S)]
                pe.matmul(dst[:, 0:P], q_head[k][:, u, 0:P], qkT[:, 2 + k, bass.ds(b * S, P)], start=True, stop=False,
                          skip_group_check=True)
                pe.matmul(dst[:, 0:P], identb, tableb("causal"), start=False, stop=True, skip_group_check=True)
                pe.matmul(dst[:, P:3 * P], q_head[k][:, u, P:S], keys, start=True, stop=False, skip_group_check=True)
                pe.matmul(dst[:, 2 * P:3 * P], identb, tableb("causal"), start=False, stop=True, skip_group_check=True)\
                    .then_inc(bl_s, 1)

            def probs1_turn(g, u):
                pe.wait_ge(bl_exp, 2 * g + 2)
                at_least(pe, bl_tout, g - 1)
                for j in range(3):
                    mm = pe.transpose(bank[5 + u % 2][:, j * P:(j + 1) * P], probs1[:, u % 4, j * P:(j + 1) * P], ident)
                mm.then_inc(bl_t, 1)

            def values1(g, b, k, u):
                pe.wait_ge(bl_tout, g + 1)
                at_least(pe, bl_o, g - 1)
                dst = bank[2 + 5 * (u % 2)]
                v = [v_tok[:, bass.ds(QT * b + j, 1), k * P:(k + 1) * P].rearrange("p o n -> p (o n)") for j in range(QT)]
                pe.matmul(dst[:, 0:P], probs1T[:, u % 2, 0:P], v[0], start=True, stop=True)
                pe.matmul(dst[:, P:2 * P], probs1T[:, u % 2, P:2 * P], v[0], start=True, stop=False)
                pe.matmul(dst[:, P:2 * P], probs1T[:, u % 2, 2 * P:3 * P], v[1], start=False, stop=True).then_inc(bl_v, 1)

            def group(G, b, k, before):
                for u in range(HG):
                    g = HG * G + u
                    scores1(g, b, k, u)
                    if u >= 2:
                        probs1_turn(g - 2, u - 2)
                    elif before is not None:
                        probs1_turn(g - 2, u + HG - 2)
                    if u >= 3:
                        values1(g - 3, b, k, u - 3)
                    elif before is not None:
                        values1(g - 3, before, 1 - k, u + HG - 3)

            pe.wait_ge(fill_out, len(fills()))
            group(0, 0, 0, None)
            with pe.Fori(0, GROUPS // 2 - 1) as i:
                group(2 * i + 1, i, 1, i)
                group(2 * i + 2, i + 1, 0, i)
            group(GROUPS - 1, B - 1, 1, B - 1)
            G = GROUPS * HG
            probs1_turn(G - 2, HG - 2)
            values1(G - 3, B - 1, 1, HG - 3)
            probs1_turn(G - 1, HG - 1)
            values1(G - 2, B - 1, 1, HG - 2)
            values1(G - 1, B - 1, 1, HG - 1)

            def hidden1(f, c, m):
                at_least(pe, f_h, m)
                for j in range(2):
                    dst, a = bank[2 * (f % 3) + j], j * F1 + f * P
                    for k in range(KD):
                        pe.matmul(dst[:, :], w13[:, k, a:a + P], x1T[:, k, c * CH:(c + 1) * CH], start=(k == 0), stop=False,
                                  skip_group_check=True)
                    for h in range(2):
                        mm = pe.matmul(dst[:, :], b13[:, h, a:a + P], am_first[j][:, h, c * CH:(c + 1) * CH],
                                       start=False, stop=(h == 1), skip_group_check=True)
                mm.then_inc(f_mm, 1)

            def hidden2(f, c, m):
                pe.wait_ge(f_h, m)
                for j in range(2):
                    dst, a = bank[2 * (f % 3) + j], j * F1 + f * P
                    for h in range(2):
                        mm = pe.matmul(dst[:, :], b13[:, h, a:a + P], am_step[j][:, h, c * CH:(c + 1) * CH],
                                       start=False, stop=(h == 1), skip_group_check=True)
                mm.then_inc(f_mm, 1)

            pe.wait_ge(low_rank, 4)
            pe.wait_ge(b13_in, 16)
            pe.wait_ge(bl_o, GROUPS * HG)
            m = 0
            for c in range(TOK // CH):
                if c:
                    pe.wait_ge(y_done, 4 * c)
                done = {}
                for n, (f, k) in enumerate(uses()):
                    if k == 0:
                        hidden1(f, c, done.get((f - 3, 1), m if f == 0 else 0))
                    else:
                        hidden2(f, c, done[f, 0])
                    m += 1
                    done[f, k] = m
                    if c == 0 and n == 4:
                        for g in range(12, 16):
                            turn1(g, o_tok, on_done, 2)
                pe.wait_ge(f_x2, NF1 * (c + 1) - 1)
                pe.wait_ge(w2_in, 48)
                at_least(pe, f_am2, 6 * c)
                for j, src in enumerate((h_first, h_both)):
                    for h in range(2):
                        for f in range(NF1):
                            if f == NF1 - 1:
                                pe.wait_ge(f_x2, NF1 * (c + 1))
                            mm = pe.matmul(bank[4 + 2 * j + h][:, :], a2[:, f, h * P:(h + 1) * P], src[:, f, :],
                                           start=(f == 0), stop=(f == NF1 - 1))
                mm.then_inc(f_a2, 1)
                pe.wait_ge(turned_out, 16)
                pe.wait_ge(f_h, m)
                for i in range(4):
                    terms = [(h_both[:, f, i * P:(i + 1) * P], w2[:, f, :]) for f in range(NF1)]
                    terms += [(oT[:, k, (4 * c + i) * P:(4 * c + i + 1) * P], w_o1[:, k, :]) for k in range(KD)]
                    terms += [(am2[:, h, i * P:(i + 1) * P], b2[:, h, :]) for h in range(2)]
                    for n, (lhs, rhs) in enumerate(terms):
                        if n == NF1 + KD:
                            pe.wait_ge(f_am2, 6 * c + 6)
                        mm = pe.matmul(bank[i][:, 0:D], lhs, rhs, start=(n == 0), stop=(n == len(terms) - 1))
                    mm.then_inc(f_down, 1)


def kernel(**inputs):
    import concourse.bacc as bacc
    from concourse.bass_utils import run_bass_kernel_spmd

    arrays = lay_out(inputs)
    nc = bacc.Bacc("TRN2", target_bir_lowering=False, num_devices=1)
    t = {name: nc.dram_tensor(f"in_{name}", a.shape, mybir.dt.from_np(a.dtype), kind="ExternalInput").ap()
         for name, a in arrays.items()}
    y = nc.dram_tensor("out", (TOK, D), F32, kind="ExternalOutput").ap()
    program(nc, t, y)
    r = run_bass_kernel_spmd(nc, [{f"in_{name}": a for name, a in arrays.items()}], core_ids=[0])
    return r.results[0]["out"].reshape(B, S, D)
```

```python
from contextlib import ExitStack

import numpy as np

import concourse.bass as bass
from concourse import mybir

F32 = mybir.dt.float32
BF16 = mybir.dt.bfloat16
U32 = mybir.dt.uint32
ALU = mybir.AluOpType
ACT = mybir.ActivationFunctionType
AX = mybir.AxisListType

P = 128
B, S, D = 4, 256, 256
TOK = B * S
NT = TOK // P
QT = S // P
KD = D // P
H0, QL, KVL, DN, DR, DV = 16, 192, 64, 128, 64, 128
PAIRS = H0 // 2
UNITS = 2 * B
LATW = QL + KVL + 2 * DR
E0, TOPK0, F0, FS, CAP = 32, 4, 176, 704, 128
FH = F0 // 2
NF = -(-FS // P)
SETS = 2
EPP = 5
LOOPED = PAIRS - 2
TURNS = {(0, 0): 0, (1, 2): 1, (3, 1): 2, (4, 2): 3, (6, 1): 4}
GATES = {(0, 2): 0, (2, 1): 1, (4, 0): 2, (5, 2): 3, (7, 1): 4}
HIDDEN = {(0, 2): 0, (2, 1): 1, (4, 1): 2, (5, 2): 3, (7, 1): 4}
FIRST_ROWS, FIRST_GATE, FIRST_HIDDEN = (6, 1), (7, 1), (7, 1)
assert EPP * LOOPED == E0 - 2
H1, CHUNK, TOPK1 = 16, 32, 4
D1 = D // H1
NB = S // CHUNK
GROUPS = 8
HG = H1 // 2
F1, E1, R1 = 896, 8, 32
ER = E1 * R1
NF1 = F1 // P
CH = 512
BIG = 1e30
HUGE = 3e38


def columns(spec):
    at, out = 0, {}
    for name, n in spec:
        out[name] = (at, n)
        at += n
    return out, at


CF, CF_N = columns([("ident", P), ("q_even", S), ("q_odd", S), ("q_sin", S), ("k_cos", QT * DR), ("k_sin", QT * DR),
                    ("iota", E0), ("cos1", QT * D1), ("sin1", QT * D1), ("keep", QT * H1 * NB),
                    ("force", QT * H1 * NB), ("future", QT * H1 * NB), ("later", NB), ("head_mean", HG),
                    ("head_scale", HG), ("slot_expert", ER), ("ones", P), ("eps_norm", 1)])
CB, CB_N = columns([("ident", P), ("before", P), ("ones", P), ("causal", P)])
BC, BC_N = columns([("lat_w", QL + KVL), ("lat_b", QL + KVL), ("w_norm", D), ("o_norm", D1)])

SMALL = 2304
REGIONS = (SMALL, 4 * NT * D, 17920, 8448, 9728)
SB_COLS = CF_N + BC_N + NT * D + sum(REGIONS)


def tables():
    cf = np.zeros((P, CF_N), np.float32)
    cb = np.zeros((P, CB_N), np.float32)

    def put(name, a):
        at, n = CF[name]
        cf[:, at:at + n] = np.asarray(a, np.float32).reshape(P, n)

    def putb(name, a):
        at, n = CB[name]
        cb[:, at:at + n] = a

    i = np.arange(P)
    put("ident", np.eye(P))
    inv = 1.0 / 10000.0 ** (np.arange(0, DR, 2, dtype=np.float32) / DR)
    fr = np.outer(np.arange(S, dtype=np.float32), inv)
    emb = np.concatenate([fr, fr], -1)
    cos, sin = np.cos(emb), np.sin(emb)
    signed = np.concatenate([-sin[:, :DR // 2], sin[:, DR // 2:]], -1)
    sc = np.float32(-1.0 / np.sqrt(DN + DR))
    one = np.full((DR, S), sc, np.float32)
    put("q_even", np.concatenate([one, sc * cos.T]))
    put("q_odd", np.concatenate([sc * cos.T, one]))
    put("q_sin", np.concatenate([sc * signed.T, sc * signed.T]))
    put("k_cos", cos.reshape(QT, P, DR).transpose(1, 0, 2))
    put("k_sin", signed.reshape(QT, P, DR).transpose(1, 0, 2))
    put("iota", np.tile(np.arange(E0), (P, 1)))
    inv1 = (1.0 / np.float32(10000.0) ** (np.arange(0, D1, 2).astype(np.float32) / np.float32(D1))).astype(np.float32)
    f1 = np.arange(S, dtype=np.float32)[:, None] * inv1
    c1, s1 = np.cos(f1), np.sin(f1)
    put("cos1", np.concatenate([c1, c1], -1).reshape(QT, P, D1).transpose(1, 0, 2))
    put("sin1", np.concatenate([-s1, s1], -1).reshape(QT, P, D1).transpose(1, 0, 2))
    own = np.arange(S)[:, None] // CHUNK
    n = np.arange(NB)[None, :]

    def rows(a):
        return np.repeat(a.reshape(QT, P, 1, NB), H1, 2).transpose(1, 0, 2, 3)

    put("keep", rows((n < own).astype(np.float32)))
    put("force", rows(np.where(n > own, -BIG, np.where(n == own, BIG, 0.0))))
    put("future", rows(np.where(n > own, BIG, 0.0)))
    put("later", np.tile(NB - 1 - np.arange(NB), (P, 1)))
    mine = (i[:, None] // D1 == np.arange(HG)[None, :]).astype(np.float32)
    put("head_mean", mine / CHUNK)
    put("head_scale", -mine * D1 ** -0.5)
    put("slot_expert", np.tile(np.arange(ER) // R1, (P, 1)))
    put("ones", np.ones((P, P)))
    put("eps_norm", np.full((P, 1), 1e-5))
    putb("ident", np.eye(P))
    putb("before", i[:, None] < i[None, :])
    putb("ones", 1.0)
    putb("causal", np.where(i[None, :] > i[:, None], BIG, 0.0))
    return cf, cb.astype(mybir.dt.np(BF16))


def lay_out(a):
    f = {k: np.asarray(v) for k, v in a.items()}

    def tiles(w):
        return w.reshape(-1, P, w.shape[1]).transpose(1, 0, 2)

    def rep(*v):
        return np.tile(np.concatenate(v)[None, :], (P, 1))

    def swap(w):
        return np.concatenate([w[..., DR // 2:, :], w[..., :DR // 2, :]], -2)

    out = {"x": f["L0_attn_hidden_states"].reshape(TOK, D)}
    out["consts"], out["consts_b"] = tables()
    out["rows"] = rep(f["L0_attn_q_a_ln_w"], f["L0_attn_kv_a_ln_w"], f["L0_attn_q_a_ln_b"], f["L0_attn_kv_a_ln_b"],
                      f["L0_ffn_w_norm"], f["L1_attn_o_norm_w"])
    kva = f["L0_attn_kv_a_w"]
    out["w_lat"] = tiles(np.concatenate([f["L0_attn_q_a_w"], kva[:KVL], kva[KVL:], swap(kva[KVL:])]).T)
    wq = f["L0_attn_q_b_w"].reshape(PAIRS, 2, DN, QL).transpose(0, 2, 1, 3)
    kvb = f["L0_attn_kv_b_w"].reshape(PAIRS, 2, 2, DN, KVL)
    vkv = np.concatenate([kvb[:, :, 1], kvb[:, :, 0], kvb[:, :, 1]], -1).transpose(0, 2, 1, 3)
    wo = f["L0_attn_o_w"].T.reshape(PAIRS, 2, DV, D).transpose(0, 2, 1, 3)
    out["w_pair"] = np.concatenate([w.reshape(PAIRS, P, -1) for w in (wq, vkv, wo)], -1)
    qr = f["L0_attn_q_rope_w"].reshape(PAIRS, 2, DR, QL)
    qs = swap(qr)
    out["w_rope"] = np.stack([np.concatenate([qr[:, 0], qr[:, 1]], 1), np.concatenate([qs[:, 1], qs[:, 0]], 1)],
                             1).transpose(0, 3, 1, 2)
    out["w_route"] = tiles(np.concatenate([f["L0_ffn_w_router"], f["L0_ffn_w_shared_gate"],
                                           np.zeros((D, P - E0 - 1), np.float32)], 1))
    pad = np.zeros((D, NF * P - FS), np.float32)
    out["sw_up"] = tiles(np.concatenate([f["L0_ffn_sw_gate"], pad, f["L0_ffn_sw_up"], pad], 1))
    out["sw_down"] = tiles(np.concatenate([f["L0_ffn_sw_down"], np.zeros((NF * P - FS, D), np.float32)]))
    gu = np.stack([f["L0_ffn_w_gate"], f["L0_ffn_w_up"]], 2)
    out["w_gate_up"] = gu.reshape(E0, KD, P, 2 * F0).transpose(0, 2, 1, 3)
    out["w_down"] = f["L0_ffn_w_down"].reshape(E0, 2, FH, D).transpose(0, 2, 1, 3)
    out["w_qkvg"] = tiles(np.concatenate([f["L1_attn_Wq"], f["L1_attn_Wk"], f["L1_attn_Wv"], f["L1_ffn_Wg"]]).T)
    out["w_o1"] = tiles(f["L1_attn_Wo"].T)
    out["w13"] = tiles(np.concatenate([f["L1_ffn_W1"], f["L1_ffn_W3"]]).T)
    out["a13"] = tiles(np.concatenate([f["L1_ffn_A1"].reshape(ER, D), f["L1_ffn_A3"].reshape(ER, D)]).T)
    out["b13"] = tiles(np.concatenate([f["L1_ffn_B1"].transpose(0, 2, 1).reshape(ER, F1),
                                       f["L1_ffn_B3"].transpose(0, 2, 1).reshape(ER, F1)], 1))
    out["w2"] = tiles(f["L1_ffn_W2"].T)
    out["a2"] = tiles(f["L1_ffn_A2"].reshape(ER, F1).T)
    out["b2"] = tiles(f["L1_ffn_B2"].transpose(0, 2, 1).reshape(ER, D))
    return {k: np.ascontiguousarray(v) for k, v in out.items()}


class Strip:

    def __init__(self, whole, at, n):
        self.whole, self.at, self.end = whole, at, at + n

    def take(self, *shape):
        n = int(np.prod(shape))
        assert self.at + n <= self.end, "the strip is full"
        ap = self.whole[:, self.at:self.at + n]
        self.at += n
        if len(shape) == 2:
            return ap.rearrange("p (a b) -> p a b", b=shape[1])
        if len(shape) == 3:
            return ap.rearrange("p (a b c) -> p a b c", b=shape[1], c=shape[2])
        return ap

    def take_b(self, *shape):
        n = int(np.prod(shape))
        ap = self.take(n // 2).bitcast(BF16)
        if len(shape) == 2:
            return ap.rearrange("p (a b) -> p a b", b=shape[1])
        if len(shape) == 3:
            return ap.rearrange("p (a b c) -> p a b c", b=shape[1], c=shape[2])
        return ap


def along(ap, *dims):
    for at, n in dims:
        ap = ap.unsqueeze(at)
        shape = list(ap.shape)
        shape[at] = n
        ap = ap.broadcast_to(shape)
    return ap


def at_least(eng, sem, n):
    if not isinstance(n, int) or n > 0:
        eng.wait_ge(sem, n)


def program(nc, t, y):
    ctx = ExitStack()
    with ctx:
        def sem(name):
            return ctx.enter_context(nc.semaphore(name))

        sb = ctx.enter_context(nc.sbuf_tensor("sb", [P, SB_COLS], F32))
        cb = ctx.enter_context(nc.sbuf_tensor("cb", [P, CB_N], BF16))
        bank = [ctx.enter_context(nc.psum_tensor(f"bank{i}", [P, 512], F32)) for i in range(8)]
        whole = Strip(sb, 0, SB_COLS)
        cf = whole.take(CF_N)
        rows = whole.take(BC_N)
        acc = whole.take(NT, D)
        small = whole.take(SMALL)
        region1 = whole.take(4 * NT * D)
        region2 = whole.take(17920)
        region3 = whole.take(8448)
        region4 = whole.take(9728)

        def strip(region):
            return Strip(region, 0, region.shape[1])

        def table(name, *shape):
            at, n = CF[name]
            ap = cf[:, at:at + n]
            if len(shape) == 2:
                return ap.rearrange("p (a b) -> p a b", b=shape[1])
            return ap

        def row(name):
            at, n = BC[name]
            return rows[:, at:at + n]

        def tableb(name):
            at, n = CB[name]
            return cb[:, at:at + n]

        ident, identb = table("ident"), tableb("ident")

        sm = Strip(small, 0, SMALL)
        stats = sm.take(NT, 6)
        mv = sm.take(NT, 2)
        var, sd, rstd = sm.take(NT), sm.take(NT), sm.take(NT)
        ms, sd2, rrms = sm.take(NT), sm.take(NT), sm.take(NT)
        lat_stats, lat_mv = sm.take(2 * NT, 6), sm.take(2 * NT, 2)
        lat_var, lat_sd, lat_rstd = sm.take(2 * NT), sm.take(2 * NT), sm.take(2 * NT)
        gate_z, gate_e, gate1, gate = sm.take(NT), sm.take(NT), sm.take(NT), sm.take(NT)
        weight4 = sm.take(NT * TOPK0)
        dest = sm.take(NT * TOPK0).bitcast(U32)
        source = sm.take(NT * TOPK0).bitcast(U32)
        row_min = sm.take(4, QT)
        row_sum = sm.take(4, QT)
        row_inv = sm.take(4, QT)

        r1 = strip(region1)
        xn, xnT = r1.take(NT, D), r1.take(KD, TOK)
        x2, x2T = r1.take(NT, D), r1.take(KD, TOK)
        picked = strip(region1).take(NT * TOPK0, D)

        r2 = strip(region2)
        lat = r2.take(NT, LATW)
        w_lat = r2.take(KD, LATW)
        w_route = r2.take(KD, P)
        sw_up = r2.take(KD, 2 * NF * P)
        sw_down = r2.take(NF, D)
        hT = r2.take(NF, TOK)
        sgate, sup = r2.take(2, CH), r2.take(2, CH)
        zeros = small[:, SMALL - D:SMALL]
        r2 = strip(region2)
        qb = [r2.take(2, TOK) for _ in range(2)]
        q_tmp = r2.take(CH)
        probs = r2.take(4, QT, S)
        probsT = r2.take(2, QT, S)
        ctxT = r2.take(PAIRS, TOK)
        w_vo = r2.take(PAIRS, D)

        r3 = strip(region3)
        xe = r3.take(SETS, D)
        w_gu = [r3.take(KD, 2 * F0) for _ in range(SETS)]
        w_dn = [r3.take(2, D) for _ in range(SETS)]
        xeT = [r3.take(KD, P) for _ in range(2)]
        e_act, e_gu, e_hid = r3.take(2, 2, P), r3.take(2, 2, P), r3.take(2, 2, P)
        ye = r3.take(SETS, D)

        r4 = strip(region4)
        w_pair = [r4.take(2 * QL + 2 * 3 * KVL + 2 * D) for _ in range(2)]
        w_q = [w[:, 0:2 * QL].rearrange("p (h n) -> p h n", h=2) for w in w_pair]
        w_vk = [w[:, 2 * QL:2 * QL + 6 * KVL].rearrange("p (h n) -> p h n", h=2) for w in w_pair]
        w_o = [w[:, 2 * QL + 6 * KVL:].rearrange("p (h n) -> p h n", h=2) for w in w_pair]
        w_eff = [r4.take(2, 6 * DR) for _ in range(2)]
        qk = r4.take(4, TOK)
        kv_tok = r4.take(NT, 3 * KVL)
        r4 = strip(region4)
        logit, expo, prob = r4.take(NT, E0), r4.take(NT, E0), r4.take(NT, E0)
        route_max, route_sum, route_inv = r4.take(NT), r4.take(NT), r4.take(NT)
        top, top_at = r4.take(NT, 8), r4.take(NT, 8).bitcast(U32)
        chosen = r4.take(NT, TOPK0)
        onehot = r4.take(NT, TOPK0, E0)
        mask = r4.take(NT, E0)
        maskb = r4.take_b(NT, E0)
        place4, over, clipped = r4.take(NT * TOPK0), r4.take(NT * TOPK0), r4.take(NT * TOPK0)
        dest_f, source_f = r4.take(NT * TOPK0), r4.take(NT * TOPK0)
        assert r4.at <= 2 * 1280 + 2 * 768

        logit1, expo1, prob1 = sm.take(NT, E1), sm.take(NT, E1), sm.take(NT, E1)
        max1, sum1, inv1 = sm.take(NT), sm.take(NT), sm.take(NT)
        top1, top1_at, chosen1 = sm.take(NT, 8), sm.take(NT, 8).bitcast(U32), sm.take(NT, 2)
        share = sm.take(NT, 2)
        bias_g = sm.take(2, QT, HG * NB)
        o_var, o_sd, o_inv = sm.take(NT, H1), sm.take(NT, H1), sm.take(NT, H1)
        assert sm.at <= SMALL - D
        r1 = strip(region1)
        x1T = r1.take(KD, TOK)
        qkT = r1.take(4, TOK)
        v_tok = r1.take(NT, D)
        r1 = Strip(region1, KD * TOK, 4 * TOK + NT * D)
        w2, a2, b2 = r1.take(NF1, D), r1.take(NF1, ER), r1.take(2, D)
        oT = r1.take(KD, TOK)
        xn1 = strip(region2).take(NT, D)
        r2 = strip(region2)
        am_first = [r2.take(2, TOK) for _ in range(2)]
        am_step = [r2.take(2, TOK) for _ in range(2)]
        phase = r2.at
        r2.take(NT * D)
        qk_tok = r2.take(NT, 2 * D)
        rope_tmp = r2.take(2, 2, 2 * D)
        kmean = r2.take(KD, B, H1 * NB)
        kblock = r2.take(KD, B * NB)
        r2 = Strip(region2, phase, NT * D)
        expert_of = [r2.take_b(NT, ER) for _ in range(2)]
        first_maskT = Strip(region2, phase + 7936, TOK).take_b(2, TOK)
        r2 = Strip(region2, phase, region2.shape[1] - phase)
        q_head = [r2.take(HG, S) for _ in range(2)]
        masked = r2.take(4, 3 * P)
        probs1 = r2.take(4, 3 * P)
        probs1T = r2.take(2, 3 * P)
        r2 = Strip(region2, phase, region2.shape[1] - phase)
        h_first = r2.take(NF1, CH)
        h_both = r2.take(NF1, CH)
        f_act, f_hid = r2.take(2, CH), r2.take(2, CH)
        squares = h_both.rearrange("p f n -> p (f n)")[:, 0:NT * D].rearrange("p (t h d) -> p (t h) d", h=H1, d=D1)
        r3 = strip(region3)
        w_qkvg = r3.take(KD, 3 * D + E1)
        w_o1, a13, w13 = r3.take(KD, D), r3.take(KD, 2 * ER), r3.take(KD, 2 * F1)
        rank = r3.take(NT, H1 * NB)
        share_rep = r3.take(4, P)
        r3 = strip(region3)
        am2, am2_tmp = r3.take(2, CH), r3.take(CH)
        r4 = strip(region4)
        b13 = r4.take(2, 2 * F1)
        second_maskT, step_maskT = r4.take_b(2, TOK), r4.take_b(2, TOK)
        shareT = r4.take(2, TOK)
        o_tok = r4.take(NT, D)
        r4 = strip(region4)
        score_blk = r4.take(NT * H1, NB)
        beats_first = [r4.take_b(QT * H1, NB - d) for d in range(1, NB)]
        beats_rest = [r4.take_b((NT - QT) * H1, NB - d) for d in range(1, NB)]
        assert r4.at <= 2 * 2 * F1

        buf = nc.dram_tensor("expert_in", [E0 * CAP, D], F32).ap()
        res = nc.dram_tensor("expert_out", [E0 * CAP, D], F32).ap()

        x_in = [sem(f"x_in{i}") for i in range(4)]
        cf_in, cb_in, rows_in, lat_in, route_in = (sem(n) for n in ("cf_in", "cb_in", "rows_in", "lat_in", "route_in"))
        up_in, down_in, zero_set, zero_in = (sem(n) for n in ("up_in", "down_in", "zero_set", "zero_in"))
        ln_stats, ln_mv, ln_var, ln_sd, ln_rstd = (sem(n) for n in ("ln_stats", "ln_mv", "ln_var", "ln_sd", "ln_rstd"))
        xn_done, ms_step, ms_var, ms_sd, ms_inv, x2_done = (
            sem(n) for n in ("xn_done", "ms_step", "ms_var", "ms_sd", "ms_inv", "x2_done"))
        acc_done = sem("acc_done")
        turned, turned_out = sem("turned"), sem("turned_out")
        lat_mm, lat_out, logit_mm = sem("lat_mm"), sem("lat_out"), sem("logit_mm")
        lat_st, lat_ag, lat_vr, lat_sdev, lat_rs, lat_norm, lat_scaled, lat_rope, lat_done = (
            sem(n) for n in ("lat_st", "lat_ag", "lat_vr", "lat_sdev", "lat_rs", "lat_norm", "lat_scaled", "lat_rope",
                             "lat_done"))
        pad_set, latT_mm, latT_out = sem("pad_set"), sem("latT_mm"), sem("latT_out")
        rt_max, rt_sub, rt_exp, rt_step, rt_mask, rt_pos, rt_dest = (
            sem(n) for n in ("rt_max", "rt_sub", "rt_exp", "rt_step", "rt_mask", "rt_pos", "rt_dest"))
        sh_mm, sh_act, sh_h, sh_down, sh_add = (sem(n) for n in ("sh_mm", "sh_act", "sh_h", "sh_down", "sh_add"))
        eff_pad = sem("eff_pad")
        scattered, combined = sem("scattered"), sem("combined")
        gathered = [sem(f"gathered{i}") for i in range(NT)]
        ew_in = [sem(f"ew_in{s}") for s in range(SETS)]
        ed_in = [sem(f"ed_in{s}") for s in range(SETS)]
        ye_free = sem("ye_free")
        eb_in = [sem(f"eb_in{s}") for s in range(SETS)]
        y_stored = [sem(f"y_stored{s}") for s in range(SETS)]
        ex_t, ex_tout, ex_g, ex_act, ex_gu, ex_h, ex_done, ex_y = (
            sem(n) for n in ("ex_t", "ex_tout", "ex_g", "ex_act", "ex_gu", "ex_h", "ex_done", "ex_y"))
        pair_in = [sem(f"pair_in{i}") for i in range(2)]
        at_m, at_eff, at_q, at_qrope, at_qe = (sem(n) for n in ("at_m", "at_eff", "at_q", "at_qrope", "at_qe"))
        at_s, at_min, at_exp, at_inv, at_norm, at_t, at_tout, at_pv, at_ctx = (
            sem(n) for n in ("at_s", "at_min", "at_exp", "at_inv", "at_norm", "at_t", "at_tout", "at_pv", "at_ctx"))
        op_mm, op_add = sem("op_mm"), sem("op_add")
        l1_sd = sem("l1_sd")
        w3_in, b13_in, w2_in = sem("w3_in"), sem("b13_in"), sem("w2_in")
        qkv_mm, rope_mul, rope_add, v_out, qkT_mm, qkT_out = (
            sem(n) for n in ("qkv_mm", "rope_mul", "rope_add", "v_out", "qkT_mm", "qkT_out"))
        kmean_set, kmean_done, blk_mm, blk_step = (sem(n) for n in ("kmean_set", "kmean_done", "blk_mm", "blk_step"))
        blk_beats, blk_count, rest_beats, rest_count = (
            sem(n) for n in ("blk_beats", "blk_count", "rest_beats", "rest_count"))
        r1_step, r1_sub, r1_exp, r1_own, r1_share = (sem(n) for n in ("r1_step", "r1_sub", "r1_exp", "r1_own", "r1_share"))
        fill_mm, fill_out, step_mask, low_rank = (sem(n) for n in ("fill_mm", "fill_out", "step_mask", "low_rank"))
        bl_q, bl_bias, bl_s, bl_min, bl_exp, bl_inv, bl_t, bl_tout, bl_v, bl_o = (
            sem(n) for n in ("bl_q", "bl_bias", "bl_s", "bl_min", "bl_exp", "bl_inv", "bl_t", "bl_tout", "bl_v", "bl_o"))
        on_sq, on_step, on_sd, on_done = (sem(n) for n in ("on_sq", "on_step", "on_sd", "on_done"))
        f_mm, f_silu, f_h, f_x, f_x2, f_a2, f_am2, f_down = (
            sem(n) for n in ("f_mm", "f_silu", "f_h", "f_x", "f_x2", "f_a2", "f_am2", "f_down"))
        y_done, stored = sem("y_done"), sem("stored")

        def fills():
            out = [("low", j, h, c) for j in range(2) for h in range(2) for c in range(TOK // CH)]
            out += [("mask", k, h, c) for k in range(2) for h in range(2) for c in range(TOK // CH)]
            return out + [("share", k, 0, c) for k in range(2) for c in range(TOK // CH)]

        def turn_bank(g):
            return g % 4 if g < 8 else (2 if g < 12 else 6) + g % 2

        def uses():
            out = [(0, 0)]
            for f in range(1, NF1):
                out += [(f, 0), (f - 1, 1)]
            return out + [(NF1 - 1, 1)]

        first_heads, rest_heads = slice(0, QT * H1), slice(QT * H1, NT * H1)

        def compare(eng, heads, beats, step):
            for d in range(1, NB):
                eng.tensor_tensor(beats[d - 1], score_blk[:, heads, 0:NB - d], score_blk[:, heads, d:NB], ALU.is_ge)\
                    .then_inc(step, 1)

        def count(eng, heads, beats, step, n):
            ranks = rank.rearrange("p t (h n) -> p (t h) n", n=NB)[:, heads, :]
            for d in range(1, NB):
                eng.tensor_tensor(ranks[:, :, d:NB], ranks[:, :, d:NB], beats[d - 1], ALU.add).then_inc(step, 1)
                eng.wait_ge(step, n + 2 * d - 1)
                eng.tensor_tensor(ranks[:, :, 0:NB - d], ranks[:, :, 0:NB - d], beats[d - 1], ALU.subtract)\
                    .then_inc(step, 1)
                eng.wait_ge(step, n + 2 * d)

        block = ctx.enter_context(nc.Block())

        @block.sync
        def _(sp):
            x_t = t["x"].rearrange("(t p) d -> p t d", p=P)
            for i in range(4):
                sp.dma_start(acc[:, 2 * i:2 * i + 2, :], x_t[:, 2 * i:2 * i + 2, :]).then_inc(x_in[i], 16)
            sp.dma_start(cf, t["consts"]).then_inc(cf_in, 16)
            sp.dma_start(rows, t["rows"]).then_inc(rows_in, 16)
            sp.dma_start(w_lat, t["w_lat"]).then_inc(lat_in, 16)
            sp.dma_start(w_route, t["w_route"]).then_inc(route_in, 16)
            sp.dma_start(cb[:, :], t["consts_b"]).then_inc(cb_in, 16)
            sp.dma_start(sw_up, t["sw_up"]).then_inc(up_in, 16)
            sp.dma_start(sw_down, t["sw_down"]).then_inc(down_in, 16)

            def expert_gate_up(e, s):
                sp.dma_start(w_gu[s], t["w_gate_up"][bass.ds(e, 1)].rearrange("o p k n -> p (o k) n"))\
                    .then_inc(ew_in[s], 16)

            def expert_down(e, s):
                sp.dma_start(w_dn[s][0:FH], t["w_down"][bass.ds(e, 1)].rearrange("o p k n -> p (o k) n"))\
                    .then_inc(ed_in[s], 16)

            def expert_rows(e, s):
                sp.dma_start(xe[:, s, :], buf[bass.ds(e * CAP, CAP), :]).then_inc(eb_in[s], 16)

            for s in range(SETS):
                expert_gate_up(s, s)
                expert_down(s, s)
            sp.wait_ge(zero_set, 1)
            sp.dma_start(buf.rearrange("(r p) d -> p r d", p=P), along(zeros, (1, E0))).then_inc(zero_in, 16)

            def pair_weights(p, i):
                half = [w_eff[i][:, k, :].rearrange("p (g c) -> p g c", g=2)[:, :, DR:3 * DR] for k in range(2)]
                rope = t["w_rope"][bass.ds(p, 1)].rearrange("o l g c -> l (o g) c")
                sp.dma_start(w_pair[i], t["w_pair"][bass.ds(p, 1)].rearrange("o p n -> p (o n)")).then_inc(pair_in[i], 16)
                sp.dma_start(half[0], rope[0:P]).then_inc(pair_in[i], 16)
                sp.dma_start(half[1][0:QL - P], rope[P:QL]).then_inc(pair_in[i], 16)

            sp.wait_ge(rt_dest, 2)
            sp.wait_ge(eff_pad, 2)
            for i in range(2):
                pair_weights(i, i)
            sp.wait_ge(scattered, 16 * NT * TOPK0)
            for s in range(SETS):
                expert_rows(s, s)

            def next_experts(base, odd):
                for j in range(EPP):
                    e, s = base + j, (odd + j) % SETS
                    sp.wait_ge(ex_g, e + 1)
                    expert_rows(e + SETS, s)
                    expert_gate_up(e + SETS, s)
                    sp.wait_ge(ex_done, e + 1)
                    expert_down(e + SETS, s)

            for p in range(2, 4):
                sp.wait_ge(at_q, 6 * (p - 2) + 6)
                pair_weights(p, p % 2)
            next_experts(0, 0)
            with sp.Fori(0, LOOPED // 2 - 1) as i:
                for k in range(2):
                    sp.wait_ge(at_q, 12 * i + 6 * k + 18)
                    pair_weights(2 * i + k + 4, k)
                    next_experts(2 * EPP * i + EPP * (k + 1), (k + 1) % 2)
            next_experts(EPP * (LOOPED - 1), 1)
            sp.wait_ge(ex_y, E0)
            for s in range(SETS):
                sp.wait_ge(y_stored[s], 16 * E0 // SETS)
            for dst, name in ((w_qkvg, "w_qkvg"), (w_o1, "w_o1"), (a13, "a13"), (w13, "w13")):
                sp.dma_start(dst, t[name]).then_inc(w3_in, 16)
            sp.wait_ge(blk_count, 2 * (NB - 1))
            sp.wait_ge(rest_count, 2 * (NB - 1))
            sp.dma_start(b13, t["b13"]).then_inc(b13_in, 16)
            sp.wait_ge(bl_q, GROUPS * HG)
            sp.wait_ge(bl_s, GROUPS * HG)
            for dst, name in ((w2, "w2"), (a2, "a2"), (b2, "b2")):
                sp.dma_start(dst, t[name]).then_inc(w2_in, 16)
            for i in range(NT):
                sp.wait_ge(y_done, i + 1)
                sp.dma_start(y[i * P:(i + 1) * P, :], acc[:, i, :]).then_inc(stored, 16)
            sp.wait_ge(stored, 16 * NT)

        @block.gpsimd
        def _(pool):
            pool.memset(zeros, 0.0).then_inc(zero_set, 1)
            for i in range(NT):
                pool.wait_ge(xn_done, i + 1)
                pool.tensor_tensor(acc[:, i, :], acc[:, i, :], xn[:, i, :], ALU.add).then_inc(acc_done, 1)
            for u in range(2 * NF):
                pool.wait_ge(sh_act, 2 * u + 2)
                pool.tensor_tensor(hT[:, u // 2, (u % 2) * CH:(u % 2 + 1) * CH], sgate[:, u % 2, :], sup[:, u % 2, :],
                                   ALU.mult).then_inc(sh_h, 1)
            pool.wait_ge(rt_dest, 2)
            pool.wait_ge(zero_in, 16)
            for j in range(NT * TOPK0):
                pool.indirect_dma_start(buf[:, :], bass.IndirectOffsetOnAxis(ap=dest[:, j:j + 1], axis=0),
                                        x2[:, j // TOPK0, :], None, bounds_check=E0 * CAP - 1, oob_is_err=False)\
                    .then_inc(scattered, 16)
            pool.sem_inc(ye_free, SETS)
            with pool.Fori(0, E0 // SETS) as i:
                for s in range(SETS):
                    pool.wait_ge(ex_y, SETS * i + s + 1)
                    pool.dma_start(res[bass.ds((SETS * i + s) * CAP, CAP), :], ye[:, s, :]).then_inc(y_stored[s], 16)
                    pool.wait_ge(y_stored[s], 16 * i + 16)
                    pool.sem_inc(ye_free, 1)
            for s in range(SETS):
                pool.wait_ge(y_stored[s], 16 * E0 // SETS)
            for i in range(NT):
                for k in range(TOPK0):
                    j = i * TOPK0 + k
                    pool.indirect_dma_start(picked[:, j, :], None, res[:, :],
                                            bass.IndirectOffsetOnAxis(ap=source[:, j:j + 1], axis=0),
                                            bounds_check=E0 * CAP - 1, oob_is_err=False).then_inc(gathered[i], 16)

            pool.wait_ge(op_mm, NT)
            pool.memset(kmean, 0.0).then_inc(kmean_set, 1)
            for i in range(NT):
                pool.wait_ge(rope_mul, 3 * i + 3)
                pool.tensor_tensor(qk_tok[:, i, :], rope_tmp[:, i % 2, 0, :], rope_tmp[:, i % 2, 1, :], ALU.add)\
                    .then_inc(rope_add, 1)
            pool.wait_ge(rest_beats, NB - 1)
            count(pool, rest_heads, beats_rest, rest_count, 0)
            pool.wait_ge(fill_out, 16)
            pool.tensor_tensor(step_maskT, second_maskT, first_maskT, ALU.subtract).then_inc(step_mask, 1)
            for j in range(2):
                pool.tensor_tensor(am_first[j], am_step[j], first_maskT, ALU.mult).then_inc(low_rank, 1)
            pool.wait_ge(step_mask, 1)
            for j in range(2):
                pool.wait_ge(low_rank, j + 1)
                pool.tensor_tensor(am_step[j], am_step[j], step_maskT, ALU.mult).then_inc(low_rank, 1)

        @block.scalar
        def _(act):
            act.wait_ge(ln_var, 1)
            act.activation(sd, var, ACT.Sqrt).then_inc(ln_sd, 1)
            act.wait_ge(ms_var, 1)
            act.activation(sd2, ms, ACT.Sqrt).then_inc(ms_sd, 1)

            def turned_copy(g, dst):
                act.wait_ge(turned, g + 1)
                act.activation(dst[:, :, (g % 4) * 2 * P:(g % 4 + 1) * 2 * P],
                               bank[turn_bank(g)][:, :].rearrange("p (k n) -> p k n", k=KD), ACT.Copy)\
                    .then_inc(turned_out, 1)

            for g in range(4):
                turned_copy(g, xnT)
            for i in range(NT):
                act.wait_ge(lat_mm, i + 1)
                act.activation(lat[:, i, :], bank[4 + i % 2][:, 0:LATW], ACT.Copy).then_inc(lat_out, 1)
            for g in range(4, 8):
                turned_copy(g, x2T)
            act.wait_ge(lat_vr, 1)
            act.activation(lat_sd, lat_var, ACT.Sqrt).then_inc(lat_sdev, 1)
            act.wait_ge(rt_sub, 4)
            act.activation(expo, logit, ACT.Exp).then_inc(rt_exp, 1)
            act.activation(gate_e, gate_z, ACT.Exp, scale=-1.0).then_inc(rt_exp, 1)
            for u in range(2 * NF):
                act.wait_ge(sh_mm, u + 1)
                if u >= 2:
                    act.wait_ge(sh_h, u - 1)
                act.activation(sgate[:, u % 2, :], bank[2 * (u % 2)][:, :], ACT.Silu).then_inc(sh_act, 1)
                act.activation(sup[:, u % 2, :], bank[2 * (u % 2) + 1][:, :], ACT.Copy).then_inc(sh_act, 1)
            def expert_tanh(e, s):
                act.wait_ge(ex_g, e + 1)
                act.activation(e_act[0:FH, s], bank[1][0:FH, 0:2 * P].rearrange("p (f n) -> p f n", f=2), ACT.Tanh,
                               scale=0.5).then_inc(ex_act, 1)

            def experts_in(u, base, odd, count=EPP):
                for place in range(3):
                    j = GATES.get((u, place), count)
                    if j < count:
                        expert_tanh(base + j + 1, (odd + j + 1) % 2)

            def unit(p, u):
                g = UNITS * p + u
                copy_probsT(act, g - 3, (u - 3) % 4)
                act.wait_ge(at_min, g + 1)
                at_least(act, at_t, g - 3)
                for q in range(QT):
                    act.activation(probs[:, u % 4, q, :], bank[3 + u % 2][:, q * S:(q + 1) * S], ACT.Exp, scale=-1.0,
                                   bias=row_min[:, u % 4, q:q + 1], accum_out=row_sum[:, u % 4, q:q + 1])\
                        .then_inc(at_exp, 1)

            def copy_probsT(act, g, slot):
                if isinstance(g, int) and g < 0:
                    return
                act.wait_ge(at_t, g + 1)
                at_least(act, at_pv, g - 1)
                act.activation(probsT[:, slot % 2], bank[5 + slot % 2][:, :].rearrange("p (a b) -> p a b", a=QT), ACT.Copy)\
                    .then_inc(at_tout, 1)

            for u in range(UNITS):
                unit(0, u)
            expert_tanh(0, 0)
            with act.Fori(0, LOOPED // 2) as i:
                for k in range(2):
                    for u in range(UNITS):
                        unit(2 * i + 1 + k, u)
                        experts_in(u, 2 * EPP * i + EPP * k, k)
            for u in range(UNITS):
                unit(PAIRS - 1, u)
                experts_in(u, E0 - 2, 0, 1)
            for g in range(PAIRS * UNITS - 3, PAIRS * UNITS):
                copy_probsT(act, g, g % 4)

            act.wait_ge(cf_in, 16)
            for i in range(NT):
                act.wait_ge(ln_mv, NT + i + 1)
                act.activation(sd[:, i:i + 1], mv[:, i, 1:2], ACT.Sqrt, bias=table("eps_norm")).then_inc(l1_sd, 1)
                if i in (3, 5, 7):
                    turned_copy(8 + (i - 3) // 2, x1T)
            for i in range(NT):
                if i == 4:
                    turned_copy(11, x1T)
                act.wait_ge(qkv_mm, i + 1)
                src = bank[5 + 2 * (i % 2)]
                act.activation(v_tok[:, i, :], src[:, 0:D], ACT.Copy)
                act.activation(logit1[:, i, :], src[:, D:D + E1], ACT.Copy).then_inc(v_out, 1)
            for i in range(NT):
                act.wait_ge(qkT_mm, i + 1)
                act.activation(qkT[:, :, i * P:(i + 1) * P], bank[i % 4][:, :].rearrange("p (a n) -> p a n", a=4), ACT.Copy)\
                    .then_inc(qkT_out, 1)
            act.wait_ge(r1_sub, 1)
            act.activation(expo1, logit1, ACT.Exp).then_inc(r1_exp, 1)
            for n, (what, j, h, c) in enumerate(fills()):
                act.wait_ge(fill_mm, n + 1)
                cols = slice(c * CH, (c + 1) * CH)
                dst = {"low": am_step[j][:, h, cols], "mask": (first_maskT, second_maskT)[j][:, h, cols],
                       "share": shareT[:, j, cols]}[what]
                act.activation(dst, bank[4 + n % 4][:, :], ACT.Copy).then_inc(fill_out, 1)

            def unit1(g, u):
                copy_probs1T(g - 2, (u - 2) % HG)
                act.wait_ge(bl_min, 2 * g + 2)
                at_least(act, bl_t, g - 3)
                at_least(act, bl_inv, g - 3)
                for q, (a, b) in enumerate(((0, P), (P, 3 * P))):
                    act.activation(probs1[:, u % 4, a:b], masked[:, u % 4, a:b], ACT.Exp, scale=-1.0,
                                   bias=row_min[:, u % 4, q:q + 1], accum_out=row_sum[:, u % 4, q:q + 1])\
                        .then_inc(bl_exp, 1)

            def copy_probs1T(g, u):
                if isinstance(g, int) and g < 0:
                    return
                act.wait_ge(bl_t, g + 1)
                at_least(act, bl_v, g - 1)
                act.activation(probs1T[:, u % 2, :], bank[5 + u % 2][:, 0:3 * P], ACT.Copy).then_inc(bl_tout, 1)

            for u in range(HG):
                unit1(u, u)
            with act.Fori(0, GROUPS // 2 - 1) as i:
                for k in range(2):
                    for u in range(HG):
                        unit1(HG * (2 * i + 1 + k) + u, u)
            for u in range(HG):
                unit1(HG * (GROUPS - 1) + u, u)
            for g in range(GROUPS * HG - 2, GROUPS * HG):
                copy_probs1T(g, g % HG)
            act.wait_ge(bl_o, GROUPS * HG)
            act.activation(squares, o_tok.rearrange("p t (h d) -> p (t h) d", d=D1), ACT.Square).then_inc(on_sq, 1)
            act.wait_ge(on_step, 2)
            act.activation(o_sd, o_var, ACT.Sqrt).then_inc(on_sd, 1)
            m = 0
            for c in range(TOK // CH):
                for n, (f, k) in enumerate(uses()):
                    act.wait_ge(f_mm, m + 1)
                    at_least(act, f_h, m - 1)
                    act.activation(f_act[:, m % 2, :], bank[2 * (f % 3)][:, :], ACT.Silu).then_inc(f_silu, 1)
                    m += 1
                    if c == 0 and n == 4:
                        for g in range(12, 16):
                            turned_copy(g, oT)

        @block.vector
        def _(dve):
            for i in range(NT):
                dve.wait_ge(x_in[i // 2], 16)
                dve.bn_stats(stats[:, i, :], acc[:, i, :]).then_inc(ln_stats, 1)
            for i in range(NT):
                dve.wait_ge(ln_stats, i + 1)
                dve.bn_aggr(mv[:, i, :], stats[:, i, :]).then_inc(ln_mv, 1)
            dve.wait_ge(ln_mv, NT)
            dve.tensor_scalar(var, mv[:, :, 1], 1e-5, None, ALU.add).then_inc(ln_var, 1)
            dve.wait_ge(ln_sd, 1)
            dve.reciprocal(rstd, sd).then_inc(ln_rstd, 1)
            dve.wait_ge(ln_rstd, 1)
            dve.tensor_tensor(ms, mv[:, :, 1], rstd, ALU.mult).then_inc(ms_step, 1)
            for i in range(NT):
                dve.tensor_scalar(xn[:, i, :], acc[:, i, :], mv[:, i, 0:1], rstd[:, i:i + 1], ALU.subtract, ALU.mult)\
                    .then_inc(xn_done, 1)
                if i == 0:
                    dve.wait_ge(ms_step, 1)
                    dve.tensor_tensor(ms, ms, rstd, ALU.mult).then_inc(ms_step, 1)
                if i == 1:
                    dve.wait_ge(ms_step, 2)
                    dve.tensor_scalar(ms, ms, 1e-6, None, ALU.add).then_inc(ms_var, 1)
            dve.wait_ge(ms_sd, 1)
            dve.reciprocal(rrms, sd2).then_inc(ms_inv, 1)
            dve.wait_ge(ms_inv, 1)
            dve.wait_ge(rows_in, 16)
            for i in range(NT):
                dve.wait_ge(xn_done, i + 1)
                dve.scalar_tensor_tensor(x2[:, i, :], xn[:, i, :], rrms[:, i:i + 1], row("w_norm"), ALU.mult, ALU.mult)\
                    .then_inc(x2_done, 1)

            for i in range(NT):
                dve.wait_ge(lat_out, i + 1)
                dve.bn_stats(lat_stats[:, 2 * i, :], lat[:, i, 0:QL]).then_inc(lat_st, 1)
                dve.bn_stats(lat_stats[:, 2 * i + 1, :], lat[:, i, QL:QL + KVL]).then_inc(lat_st, 1)
            for i in range(2 * NT):
                dve.wait_ge(lat_st, i + 1)
                dve.bn_aggr(lat_mv[:, i, :], lat_stats[:, i, :]).then_inc(lat_ag, 1)
            dve.wait_ge(lat_ag, 2 * NT)
            dve.tensor_scalar(lat_var, lat_mv[:, :, 1], 1e-5, None, ALU.add).then_inc(lat_vr, 1)

            scores = [bank[6 + i][:, :].rearrange("p (t n) -> p t n", t=4) for i in range(2)]
            for i in range(2):
                dve.wait_ge(logit_mm, 4 * i + 4)
                dve.tensor_reduce(route_max[:, 4 * i:4 * i + 4], scores[i][:, :, 0:E0], AX.X, ALU.max).then_inc(rt_max, 1)
            for i in range(2):
                dve.wait_ge(rt_max, i + 1)
                dve.tensor_tensor(logit[:, 4 * i:4 * i + 4, :], scores[i][:, :, 0:E0],
                                  along(route_max[:, 4 * i:4 * i + 4], (2, E0)), ALU.subtract).then_inc(rt_sub, 1)
                dve.tensor_copy(gate_z[:, 4 * i:4 * i + 4], scores[i][:, :, E0]).then_inc(rt_sub, 1)

            dve.wait_ge(lat_sdev, 1)
            dve.reciprocal(lat_rstd, lat_sd).then_inc(lat_rs, 1)
            dve.wait_ge(lat_rs, 1)
            for i in range(NT):
                for j, a, b in ((2 * i, 0, QL), (2 * i + 1, QL, QL + KVL)):
                    dve.tensor_scalar(lat[:, i, a:b], lat[:, i, a:b], lat_mv[:, j, 0:1], lat_rstd[:, j:j + 1],
                                      ALU.subtract, ALU.mult).then_inc(lat_norm, 1)
            for q in range(QT):
                for name, a in (("k_cos", QL + KVL), ("k_sin", QL + KVL + DR)):
                    part = lat[:, q::QT, a:a + DR]
                    dve.tensor_tensor(part, part, along(table(name, QT, DR)[:, q, :], (1, B)), ALU.mult)\
                        .then_inc(lat_rope, 1)
            dve.wait_ge(lat_norm, 2 * NT)
            dve.tensor_tensor(lat[:, :, 0:QL + KVL], lat[:, :, 0:QL + KVL], along(row("lat_w"), (1, NT)), ALU.mult)\
                .then_inc(lat_scaled, 1)
            dve.wait_ge(lat_rope, 4)
            dve.tensor_tensor(kv_tok[:, :, KVL:2 * KVL], lat[:, :, QL + KVL:QL + KVL + DR], lat[:, :, QL + KVL + DR:LATW],
                              ALU.add).then_inc(lat_done, 1)
            dve.wait_ge(lat_scaled, 1)
            kv_b = along(row("lat_b")[:, QL:QL + KVL], (1, NT))
            for a in (0, 2 * KVL):
                dve.tensor_tensor(kv_tok[:, :, a:a + KVL], lat[:, :, QL:QL + KVL], kv_b, ALU.add).then_inc(lat_done, 1)
            dve.tensor_tensor(lat[:, :, 0:QL], lat[:, :, 0:QL], along(row("lat_b")[:, 0:QL], (1, NT)), ALU.add)\
                .then_inc(lat_done, 1)

            dve.wait_ge(rt_exp, 2)
            dve.tensor_reduce(route_sum, expo, AX.X, ALU.add).then_inc(rt_step, 1)
            dve.tensor_scalar(gate1, gate_e, 1.0, None, ALU.add).then_inc(rt_step, 1)
            dve.wait_ge(rt_step, 2)
            dve.reciprocal(route_inv, route_sum).then_inc(rt_step, 1)
            dve.reciprocal(gate, gate1).then_inc(rt_step, 1)
            dve.wait_ge(rt_step, 4)
            dve.tensor_tensor(prob, expo, along(route_inv, (2, E0)), ALU.mult).then_inc(rt_step, 1)
            dve.wait_ge(rt_step, 5)
            for i in range(NT):
                dve.max(top[:, i, :], prob[:, i, :]).then_inc(rt_step, 1)
            for i in range(NT):
                dve.wait_ge(rt_step, 6 + i)
                dve.max_index(top_at[:, i, :], top[:, i, :], prob[:, i, :]).then_inc(rt_step, 1)
            dve.wait_ge(rt_step, 5 + 2 * NT)
            dve.tensor_copy(chosen, top_at[:, :, 0:TOPK0]).then_inc(rt_step, 1)
            dve.wait_ge(rt_step, 6 + 2 * NT)
            flat = onehot.rearrange("p t k e -> p (t k) e")
            chosen_flat = chosen.rearrange("p t k -> p (t k)")
            dve.tensor_tensor(flat, along(table("iota"), (1, NT * TOPK0)), along(chosen_flat, (2, E0)), ALU.is_equal)\
                .then_inc(rt_step, 1)
            dve.wait_ge(rt_step, 7 + 2 * NT)
            dve.tensor_reduce(mask, onehot.rearrange("p t k e -> p t e k"), AX.X, ALU.add).then_inc(rt_step, 1)
            dve.wait_ge(rt_step, 8 + 2 * NT)
            dve.tensor_copy(maskb, mask).then_inc(rt_mask, 1)

            dve.memset(qk[QL - P:P, 3, :], 0.0).then_inc(pad_set, 1)
            for i in range(NT):
                dve.wait_ge(latT_mm, i + 1)
                src = bank[4 + i % 2][:, :].rearrange("p (a n) -> p a n", a=4)
                dve.tensor_copy(qk[:, 0:3, i * P:(i + 1) * P], src[:, 0:3, :]).then_inc(latT_out, 1)
                dve.tensor_copy(qk[0:QL - P, 3, i * P:(i + 1) * P], src[0:QL - P, 3, :]).then_inc(latT_out, 1)

            dve.wait_ge(rt_pos, 1)
            pos = bank[6][:, 0:NT * E0].rearrange("p (t e) -> p t e", e=E0)
            dve.tensor_tensor(onehot, onehot, along(pos, (2, TOPK0)), ALU.mult).then_inc(rt_step, 1)
            n = 9 + 2 * NT
            dve.wait_ge(rt_step, n)
            dve.tensor_reduce(place4, flat, AX.X, ALU.add).then_inc(rt_step, 1)
            dve.wait_ge(rt_step, n + 1)
            dve.tensor_scalar(over, place4, CAP - 0.5, None, ALU.is_gt).then_inc(rt_step, 1)
            dve.tensor_scalar(clipped, place4, CAP - 1.0, None, ALU.min).then_inc(rt_step, 1)
            dve.wait_ge(rt_step, n + 3)
            dve.scalar_tensor_tensor(source_f, chosen_flat, float(CAP), clipped, ALU.mult, ALU.add).then_inc(rt_step, 1)
            dve.scalar_tensor_tensor(weight4.rearrange("p (t k) -> p t k", k=TOPK0),
                                     over.rearrange("p (t k) -> p t k", k=TOPK0), 0.5, top[:, :, 0:TOPK0],
                                     ALU.is_lt, ALU.mult).then_inc(rt_step, 1)
            dve.wait_ge(rt_step, n + 5)
            dve.scalar_tensor_tensor(dest_f, over, 65536.0, source_f, ALU.mult, ALU.add).then_inc(rt_step, 1)
            dve.wait_ge(rt_step, n + 6)
            dve.tensor_copy(dest, dest_f).then_inc(rt_dest, 1)
            dve.tensor_copy(source, source_f).then_inc(rt_dest, 1)
            dve.wait_ge(rt_dest, 2)
            for i in range(2):
                dve.memset(w_eff[i][QL - P:P, 1, :], 0.0).then_inc(eff_pad, 1)

            for i in range(NT):
                dve.wait_ge(sh_down, i + 1)
                dve.wait_ge(acc_done, i + 1)
                dve.scalar_tensor_tensor(acc[:, i, :], bank[i % 4][:, 0:D], gate[:, i:i + 1], acc[:, i, :],
                                         ALU.mult, ALU.add).then_inc(sh_add, 1)

            def rows_out(s):
                dve.tensor_copy(xeT[s], bank[1][:, 0:KD * P].rearrange("p (k n) -> p k n", k=KD)).then_inc(ex_tout, 1)

            def results_out(e, s, rows):
                dve.wait_ge(ex_done, e + 1)
                dve.wait_ge(ye_free, e + 1)
                dve.tensor_copy(ye[:, s, :], bank[1][:, KD * P:KD * P + D]).then_inc(ex_y, 1)
                if rows:
                    rows_out(1 - s)

            def hidden(e, s):
                dve.wait_ge(ex_act, e + 1)
                gate_up = bank[1][0:FH, :].rearrange("p (j f n) -> p j f n", j=2, f=2)
                dve.scalar_tensor_tensor(e_gu[0:FH, s], e_act[0:FH, s], 1.0, gate_up[:, 0], ALU.add, ALU.mult)\
                    .then_inc(ex_gu, 1)
                dve.wait_ge(ex_gu, e + 1)
                dve.scalar_tensor_tensor(e_hid[0:FH, s], e_gu[0:FH, s], 0.5, gate_up[:, 1], ALU.mult, ALU.mult)\
                    .then_inc(ex_h, 1)

            def experts_in(u, place, base, odd, count=EPP):
                j = TURNS.get((u, place), EPP)
                if j <= count and j < EPP:
                    results_out(base + j, (odd + j) % 2, j < count)
                j = HIDDEN.get((u, place), count)
                if j < count:
                    hidden(base + j + 1, (odd + j + 1) % 2)

            def effective_qk(p, i):
                dve.wait_ge(at_m, 2 * p + 1)
                at_least(dve, at_q, 6 * (p - 1))
                m = bank[0][:, :].rearrange("p (h k n) -> p h k n", h=2, k=2)
                for h, a in ((0, 0), (1, 3 * DR)):
                    dve.tensor_copy(w_eff[i][:, 0, a:a + DR], m[:, h, 0, 0:KVL])
                    ins = dve.tensor_copy(w_eff[i][0:QL - P, 1, a:a + DR], m[0:QL - P, h, 1, 0:KVL])
                ins.then_inc(at_eff, 1)

            def effective_vo(p, where):
                dve.wait_ge(at_m, 2 * p + 2)
                for h in range(2):
                    rows_h = slice(h * KVL, (h + 1) * KVL)
                    ins = dve.tensor_copy(w_vo[rows_h, bass.ds(p, 1), :], where[rows_h, h * D:(h + 1) * D].unsqueeze(1))
                ins.then_inc(at_eff, 1)

            def queries(p, m, i, where):
                c, j = m // 3, m % 3
                half = slice(c * CH, (c + 1) * CH)
                dve.wait_ge(at_q, 6 * p + m + 1)
                at_least(dve, at_s, UNITS * (p - 1))
                at_least(dve, at_qe, 4 * p + 2 * c)
                name, dst = (("q_sin", q_tmp), ("q_even", qb[i][:, 0, half]), ("q_odd", qb[i][:, 1, half]))[j]
                dve.tensor_tensor(dst.rearrange("p (b s) -> p b s", s=S),
                                  where[:, :].rearrange("p (b s) -> p b s", s=S),
                                  along(table(name), (1, CH // S)), ALU.mult).then_inc(at_qrope, 1)
                if j == 2:
                    dve.wait_ge(at_qrope, 6 * p + m + 1)
                    dve.tensor_tensor(qb[i][DR:P, 0, half], qb[i][DR:P, 0, half], q_tmp[DR:P], ALU.add)\
                        .then_inc(at_qe, 1)
                    dve.tensor_tensor(qb[i][0:DR, 1, half], qb[i][0:DR, 1, half], q_tmp[0:DR], ALU.add)\
                        .then_inc(at_qe, 1)

            def minimum(g, u):
                dve.wait_ge(at_s, g + 1)
                at_least(dve, at_exp, 2 * g - 6)
                dve.tensor_reduce(row_min[:, u % 4, :], bank[3 + u % 2][:, :].rearrange("p (q n) -> p q n", q=QT),
                                  AX.X, ALU.min).then_inc(at_min, 1)

            def normalise(g, u):
                dve.wait_ge(at_exp, 2 * g + 2)
                dve.reciprocal(row_inv[:, u % 4, :], row_sum[:, u % 4, :]).then_inc(at_inv, 1)
                dve.wait_ge(at_inv, g + 1)
                for q in range(QT):
                    ins = dve.tensor_scalar(probs[:, u % 4, q, :], probs[:, u % 4, q, :], row_inv[:, u % 4, q:q + 1], None,
                                            ALU.mult)
                ins.then_inc(at_norm, 1)

            def context(g, p, u):
                dve.wait_ge(at_pv, g + 1)
                b, h = u // 2, u % 2
                dve.tensor_copy(ctxT[h * KVL:(h + 1) * KVL, bass.ds(p, 1), b * S:(b + 1) * S],
                                bank[2 + 5 * h][0:KVL, 0:S].unsqueeze(1)).then_inc(at_ctx, 1)

            def pair(p, i, first, last, experts):
                for u in range(UNITS):
                    g = UNITS * p + u
                    minimum(g, u)
                    experts(u, 0)
                    if not (first and u < 4):
                        context(g - 4, p - 1 if u < 4 else p, (u - 4) % UNITS)
                    if not (first and u < 1):
                        normalise(g - 1, u - 1)
                    experts(u, 1)
                    if not last:
                        if u == 0:
                            effective_qk(p + 1, 1 - i)
                        elif u == 1:
                            effective_vo(p + 1, bank[0])
                        else:
                            queries(p + 1, u - 2, 1 - i, bank[0])
                    experts(u, 2)

            def first_expert(u, place):
                if (u, place) == FIRST_ROWS:
                    dve.wait_ge(ex_t, 1)
                    rows_out(0)
                if (u, place) == FIRST_HIDDEN:
                    hidden(0, 0)

            effective_qk(0, 0)
            effective_vo(0, bank[1])
            for m in range(6):
                queries(0, m, 0, bank[m % 2])
            pair(0, 0, True, False, first_expert)
            with dve.Fori(0, LOOPED // 2) as i:
                for k in range(2):
                    pair(2 * i + 1 + k, 1 - k, False, False,
                         lambda u, place: experts_in(u, place, 2 * EPP * i + EPP * k, k))
            pair(PAIRS - 1, 1, False, True, lambda u, place: experts_in(u, place, E0 - 2, 0, 1))
            G = PAIRS * UNITS
            normalise(G - 1, UNITS - 1)
            for g in range(G - 4, G):
                context(g, PAIRS - 1, g % UNITS)

            dve.wait_ge(sh_add, NT)

            def normal1(i):
                dve.wait_ge(l1_sd, i + 1)
                dve.reciprocal(rstd[:, i:i + 1], sd[:, i:i + 1]).then_inc(ln_rstd, 1)
                dve.wait_ge(ln_rstd, i + 2)
                dve.tensor_scalar(xn1[:, i, :], acc[:, i, :], mv[:, i, 0:1], rstd[:, i:i + 1], ALU.subtract, ALU.mult)\
                    .then_inc(xn_done, 1)

            for i in range(NT):
                dve.wait_ge(gathered[i], 16 * TOPK0)
                for k in range(TOPK0):
                    j = i * TOPK0 + k
                    if k:
                        dve.wait_ge(combined, j)
                    dve.scalar_tensor_tensor(acc[:, i, :], picked[:, j, :], weight4[:, j:j + 1], acc[:, i, :],
                                             ALU.mult, ALU.add).then_inc(combined, 1)
                dve.wait_ge(op_mm, i + 1)
                dve.wait_ge(combined, TOPK0 * (i + 1))
                dve.tensor_tensor(acc[:, i, :], bank[i % 2][:, 0:D], acc[:, i, :], ALU.add).then_inc(op_add, 1)
                dve.wait_ge(op_add, i + 1)
                dve.bn_stats(stats[:, i, :], acc[:, i, :]).then_inc(ln_stats, 1)
                dve.wait_ge(ln_stats, NT + i + 1)
                dve.bn_aggr(mv[:, i, :], stats[:, i, :]).then_inc(ln_mv, 1)
                if i:
                    normal1(i - 1)
            normal1(NT - 1)

            for i in range(NT):
                dve.wait_ge(qkv_mm, i + 1)
                at_least(dve, rope_add, i - 1)
                src = bank[4 + 2 * (i % 2)][:, :].rearrange("p (h d) -> p h d", d=D1)
                cos_t = table("cos1", QT, D1)[:, i % QT, :]
                sin_t = table("sin1", QT, D1)[:, i % QT, :]
                by_cos = rope_tmp[:, i % 2, 0, :].rearrange("p (h d) -> p h d", d=D1)
                by_sin = rope_tmp[:, i % 2, 1, :].rearrange("p (h d) -> p h d", d=D1)
                half = D1 // 2
                dve.tensor_tensor(by_cos, src, along(cos_t, (1, 2 * H1)), ALU.mult).then_inc(rope_mul, 1)
                dve.tensor_tensor(by_sin[:, :, 0:half], src[:, :, half:D1], along(sin_t[:, 0:half], (1, 2 * H1)), ALU.mult)\
                    .then_inc(rope_mul, 1)
                dve.tensor_tensor(by_sin[:, :, half:D1], src[:, :, 0:half], along(sin_t[:, half:D1], (1, 2 * H1)), ALU.mult)\
                    .then_inc(rope_mul, 1)

            dve.wait_ge(v_out, NT)
            dve.tensor_reduce(max1, logit1, AX.X, ALU.max).then_inc(r1_step, 1)
            dve.wait_ge(r1_step, 1)
            dve.tensor_tensor(logit1, logit1, along(max1, (2, E1)), ALU.subtract).then_inc(r1_sub, 1)

            dve.wait_ge(qkT_out, NT)
            dve.tensor_reduce(kblock, qkT[:, 2:4, :].rearrange("p k (n c) -> p k n c", c=CHUNK), AX.X, ALU.add)\
                .then_inc(kmean_done, 1)
            dve.wait_ge(kmean_done, 1)
            dve.wait_ge(kmean_set, 1)
            for k in range(KD):
                for h in range(HG):
                    at = (k * HG + h) * NB
                    dve.tensor_scalar(kmean[:, k, :, at:at + NB], kblock[:, k, :].rearrange("p (b n) -> p b n", n=NB),
                                      table("head_mean")[:, h:h + 1], None, ALU.mult).then_inc(kmean_done, 1)

            dve.wait_ge(r1_exp, 1)
            dve.tensor_reduce(sum1, expo1, AX.X, ALU.add).then_inc(r1_step, 1)
            dve.wait_ge(r1_step, 2)
            dve.reciprocal(inv1, sum1).then_inc(r1_step, 1)
            dve.wait_ge(r1_step, 3)
            dve.tensor_tensor(prob1, expo1, along(inv1, (2, E1)), ALU.mult).then_inc(r1_step, 1)
            dve.wait_ge(r1_step, 4)
            for i in range(NT):
                dve.max(top1[:, i, :], prob1[:, i, :]).then_inc(r1_step, 1)
            for i in range(NT):
                dve.wait_ge(r1_step, 5 + i)
                dve.max_index(top1_at[:, i, :], top1[:, i, :], prob1[:, i, :]).then_inc(r1_step, 1)
            dve.wait_ge(r1_step, 4 + 2 * NT)
            dve.tensor_copy(chosen1, top1_at[:, :, 0:2]).then_inc(r1_step, 1)
            dve.tensor_tensor(sum1, top1[:, :, 0], top1[:, :, 1], ALU.add).then_inc(r1_step, 1)
            dve.wait_ge(r1_step, 6 + 2 * NT)
            dve.reciprocal(inv1, sum1).then_inc(r1_step, 1)

            g_b = score_blk.rearrange("p (b n) m -> p b (n m)", b=B)
            for i in range(2):
                dve.wait_ge(blk_mm, 4 * i + 4)
                dve.tensor_tensor(g_b[:, 2 * i:2 * i + 2, :], bank[i][:, :].rearrange("p (b n) -> p b n", b=2),
                                  along(table("keep"), (1, 2)), ALU.mult).then_inc(blk_step, 1)
            dve.tensor_copy(rank.rearrange("p t (h n) -> p (t h) n", n=NB), along(table("later"), (1, NT * H1))).then_inc(blk_step, 1)
            dve.wait_ge(blk_step, 2)
            dve.tensor_tensor(g_b, g_b, along(table("force"), (1, B)), ALU.add).then_inc(blk_step, 1)
            dve.wait_ge(blk_step, 4)
            compare(dve, rest_heads, beats_rest, rest_beats)
            compare(dve, first_heads, beats_first, blk_beats)

            for k in range(2):
                for i in range(NT):
                    dve.tensor_scalar(expert_of[k][:, i, :], table("slot_expert"), chosen1[:, i, k:k + 1], None,
                                      ALU.is_equal).then_inc(r1_own, 1)
            dve.wait_ge(r1_step, 7 + 2 * NT)
            dve.tensor_tensor(share, top1[:, :, 0:2], along(inv1, (2, 2)), ALU.mult).then_inc(r1_step, 1)
            dve.wait_ge(r1_step, 8 + 2 * NT)
            for n in range(2 * NT):
                k, i = n // NT, n % NT
                if n >= 4:
                    dve.wait_ge(fill_mm, 16 + n // 4)
                dve.tensor_scalar(share_rep[:, n % 4, :], table("ones"), share[:, i, k:k + 1], None, ALU.mult)\
                    .then_inc(r1_share, 1)

            dve.wait_ge(blk_beats, NB - 1)
            count(dve, first_heads, beats_first, blk_count, 0)

            def own_queries(G, b, k, u):
                at_least(dve, bl_s, HG * (G - 1))
                dve.tensor_scalar(q_head[k][:, u, :], qkT[:, k, bass.ds(b * S, S)], table("head_scale")[:, u:u + 1], None,
                                  ALU.mult).then_inc(bl_q, 1)

            def own_bias(G, b, k):
                at_least(dve, bl_min, 2 * HG * (G - 1))
                if not (isinstance(b, int) and b == 0):
                    dve.wait_ge(rest_count, 2 * (NB - 1))
                half = slice(k * HG * NB, (k + 1) * HG * NB)
                dve.tensor_scalar(bias_g[:, k], rank[:, bass.ds(QT * b, QT), half], TOPK1 - 0.5, BIG, ALU.is_gt, ALU.mult)\
                    .then_inc(bl_bias, 1)
                dve.wait_ge(bl_bias, 2 * G + 1)
                dve.tensor_tensor(bias_g[:, k], bias_g[:, k],
                                  table("future").rearrange("p (q n) -> p q n", q=QT)[:, :, half], ALU.max)\
                    .then_inc(bl_bias, 1)

            def masked_minimum(g, G, k, u, meanwhile):
                dve.wait_ge(bl_s, g + 1)
                dve.wait_ge(bl_bias, 2 * G + 2)
                at_least(dve, bl_exp, 2 * g - 6)
                meanwhile()
                for q, (a, b) in enumerate(((0, P), (P, 3 * P))):
                    n = (b - a) // CHUNK
                    dve.tensor_tensor_reduce(
                        masked[:, u % 4, a:b].rearrange("p (n c) -> p n c", c=CHUNK),
                        bank[3 + u % 2][:, a:b].rearrange("p (n c) -> p n c", c=CHUNK),
                        along(bias_g[:, k, q, u * NB:u * NB + n], (2, CHUNK)), 1.0, HUGE, ALU.add, ALU.min,
                        row_min[:, u % 4, q:q + 1]).then_inc(bl_min, 1)

            def inverse(g, u):
                dve.wait_ge(bl_exp, 2 * g + 2)
                at_least(dve, bl_o, g - 3)
                dve.reciprocal(row_inv[:, u % 4, :], row_sum[:, u % 4, :]).then_inc(bl_inv, 1)

            def head_out(g, b, k, u):
                dve.wait_ge(bl_v, g + 1)
                dve.wait_ge(bl_inv, g + 1)
                h = (k * HG + u) * D1
                dve.tensor_tensor(o_tok[:, bass.ds(QT * b, QT), h:h + D1],
                                  bank[2 + 5 * (u % 2)][:, 0:2 * P].rearrange("p (q n) -> p q n", q=QT)[:, :, u * D1:(u + 1) * D1],
                                  along(row_inv[:, u % 4, :], (2, D1)), ALU.mult).then_inc(bl_o, 1)

            def group(G, b, k, before, after):
                if after is not None:
                    own_bias(G + 1, after, 1 - k)
                for u in range(HG):
                    g = HG * G + u
                    masked_minimum(g, G, k, u, lambda: own_queries(G + 1, after, 1 - k, u) if after is not None else None)
                    if u >= 4:
                        head_out(g - 4, b, k, u - 4)
                    elif before is not None:
                        head_out(g - 4, before, 1 - k, u + 4)
                    if u >= 2 or before is not None:
                        inverse(g - 2, (u - 2) % HG)

            own_bias(0, 0, 0)
            for u in range(HG):
                own_queries(0, 0, 0, u)
            group(0, 0, 0, None, 0)
            with dve.Fori(0, GROUPS // 2 - 1) as i:
                group(2 * i + 1, i, 1, i, i + 1)
                group(2 * i + 2, i + 1, 0, i, i + 1)
            group(GROUPS - 1, B - 1, 1, B - 1, None)
            G = GROUPS * HG
            inverse(G - 2, HG - 2)
            inverse(G - 1, HG - 1)
            for g in range(G - 4, G):
                head_out(g, B - 1, 1, g % HG)

            o_heads = o_tok.rearrange("p t (h d) -> p (t h) d", d=D1)
            o_var_f, o_inv_f = o_var.rearrange("p t h -> p (t h)"), o_inv.rearrange("p t h -> p (t h)")
            dve.wait_ge(on_sq, 1)
            dve.tensor_reduce(o_var_f, squares, AX.X, ALU.add).then_inc(on_step, 1)
            dve.wait_ge(on_step, 1)
            dve.tensor_scalar(o_var, o_var, 1.0 / D1, 1e-6, ALU.mult, ALU.add).then_inc(on_step, 1)
            dve.wait_ge(on_sd, 1)
            dve.reciprocal(o_inv, o_sd).then_inc(on_step, 1)
            dve.wait_ge(on_step, 3)
            dve.tensor_tensor(o_heads, o_heads, along(o_inv_f, (2, D1)), ALU.mult).then_inc(on_step, 1)
            dve.wait_ge(on_step, 4)
            dve.tensor_tensor(o_heads, o_heads, along(row("o_norm"), (1, NT * H1)), ALU.mult).then_inc(on_done, 2)

            m = 0
            for c in range(TOK // CH):
                cols = slice(c * CH, (c + 1) * CH)
                for f, k in uses():
                    dve.wait_ge(f_silu, m + 1)
                    at_least(dve, f_x, m - 1)
                    dve.tensor_tensor(f_hid[:, m % 2, :], f_act[:, m % 2, :], bank[2 * (f % 3) + 1][:, :], ALU.mult)\
                        .then_inc(f_h, 1)
                    dve.wait_ge(f_h, m + 1)
                    if k == 0:
                        at_least(dve, f_a2, c)
                        dve.tensor_tensor(h_first[:, f, :], f_hid[:, m % 2, :], shareT[:, 0, cols], ALU.mult)\
                            .then_inc(f_x, 1)
                    else:
                        at_least(dve, f_down, 4 * c)
                        dve.tensor_tensor(h_both[:, f, :], f_hid[:, m % 2, :], shareT[:, 1, cols], ALU.mult)\
                            .then_inc(f_x, 1)
                        dve.wait_ge(f_x, m + 1)
                        dve.tensor_tensor(h_both[:, f, :], h_both[:, f, :], h_first[:, f, :], ALU.add).then_inc(f_x2, 1)
                    m += 1
                dve.wait_ge(f_a2, c + 1)
                at_least(dve, f_down, 4 * c)
                for h in range(2):
                    at_least(dve, f_am2, 3 * (2 * c + h))
                    dve.tensor_tensor(am2_tmp, bank[4 + h][:, :], step_maskT[:, h, cols], ALU.mult).then_inc(f_am2, 1)
                    dve.tensor_tensor(am2[:, h, :], bank[6 + h][:, :], second_maskT[:, h, cols], ALU.mult).then_inc(f_am2, 1)
                    dve.wait_ge(f_am2, 3 * (2 * c + h) + 2)
                    dve.tensor_tensor(am2[:, h, :], am2[:, h, :], am2_tmp, ALU.subtract).then_inc(f_am2, 1)
                for i in range(4):
                    dve.wait_ge(f_down, 4 * c + i + 1)
                    dve.tensor_tensor(acc[:, 4 * c + i, :], bank[i][:, 0:D], acc[:, 4 * c + i, :], ALU.add)\
                        .then_inc(y_done, 1)

        @block.tensor
        def _(pe):
            def turn(g, src, ready):
                pe.wait_ge(ready, 2 * (g % 4) + 2)
                at_least(pe, turned_out, g - 3)
                for k in range(KD):
                    for i in range(2):
                        mm = pe.transpose(bank[g % 4][:, (2 * k + i) * P:(2 * k + i + 1) * P],
                                          src[:, 2 * (g % 4) + i, k * P:(k + 1) * P], ident)
                mm.then_inc(turned, 1)

            pe.wait_ge(cf_in, 16)
            for g in range(4):
                turn(g, xn, xn_done)
            pe.wait_ge(lat_in, 16)
            for i in range(NT):
                pe.wait_ge(turned_out, i // 2 + 1)
                at_least(pe, lat_out, i - 1)
                for k in range(KD):
                    mm = pe.matmul(bank[4 + i % 2][:, 0:LATW], xnT[:, k, i * P:(i + 1) * P], w_lat[:, k, :],
                                   start=(k == 0), stop=(k == KD - 1))
                mm.then_inc(lat_mm, 1)
            for g in range(4, 8):
                turn(g, x2, x2_done)
            pe.wait_ge(route_in, 16)
            for i in range(NT):
                pe.wait_ge(turned_out, 5 + i // 2)
                for k in range(KD):
                    mm = pe.matmul(bank[6 + i // 4][:, (i % 4) * P:(i % 4 + 1) * P], x2T[:, k, i * P:(i + 1) * P],
                                   w_route[:, k, :], start=(k == 0), stop=(k == KD - 1))
                mm.then_inc(logit_mm, 1)

            def shared_up(u):
                f, c = u // 2, u % 2
                at_least(pe, sh_act, 2 * u - 2)
                for j in range(2):
                    for k in range(KD):
                        mm = pe.matmul(bank[2 * (u % 2) + j][:, :],
                                       sw_up[:, k, (j * NF + f) * P:(j * NF + f + 1) * P],
                                       x2T[:, k, c * CH:(c + 1) * CH], start=(k == 0), stop=(k == KD - 1))
                mm.then_inc(sh_mm, 1)

            def latents_turn(i):
                at_least(pe, latT_out, 2 * i - 2)
                dst = bank[4 + i % 2][:, :].rearrange("p (a n) -> p a n", a=4)
                pe.transpose(dst[:, 0, :], lat[:, i, 0:P], ident)
                pe.transpose(dst[:, 1, :], kv_tok[:, i, 0:2 * KVL], ident)
                pe.transpose(dst[:, 2, :], kv_tok[:, i, KVL:3 * KVL], ident)
                pe.transpose(dst[0:QL - P, 3, :], lat[:, i, P:QL], ident).then_inc(latT_mm, 1)

            pe.wait_ge(up_in, 16)
            for u in range(2 * NF):
                shared_up(u)
                if u == 6:
                    pe.wait_ge(lat_done, 4)
                    for i in range(NT):
                        latents_turn(i)
                if u == 7:
                    pe.wait_ge(rt_mask, 1)
                    pe.wait_ge(cb_in, 16)
                    pe.matmul(bank[6][:, 0:NT * E0], tableb("before"), maskb.rearrange("p t e -> p (t e)"),
                              start=True, stop=False, skip_group_check=True)
                    for i in range(NT - 1):
                        mm = pe.matmul(bank[6][:, (i + 1) * E0:NT * E0].rearrange("p (t e) -> p t e", e=E0),
                                       tableb("ones"), along(maskb[:, i, :], (1, NT - 1 - i)),
                                       start=False, stop=(i == NT - 2), skip_group_check=True)
                    mm.then_inc(rt_pos, 1)
            pe.wait_ge(down_in, 16)
            pe.wait_ge(sh_act, 4 * NF)
            pe.wait_ge(sh_h, 2 * NF)
            for i in range(NT):
                at_least(pe, sh_add, i - 3)
                for f in range(NF):
                    mm = pe.matmul(bank[i % 4][:, 0:D], hT[:, f, i * P:(i + 1) * P], sw_down[:, f, :],
                                   start=(f == 0), stop=(f == NF - 1))
                mm.then_inc(sh_down, 1)

            def rows_turn(s, before):
                pe.wait_ge(eb_in[s], 16 * before + 16)
                for k in range(KD):
                    mm = pe.transpose(bank[1][:, k * P:(k + 1) * P], xe[:, s, k * P:(k + 1) * P], ident)
                return mm

            def gate_up(e, s, before):
                pe.wait_ge(ex_tout, e + 1)
                pe.wait_ge(ew_in[s], 16 * before + 16)
                for j in range(4):
                    for k in range(KD):
                        mm = pe.matmul(bank[1][0:FH, j * P:(j + 1) * P], w_gu[s][:, k, j * FH:(j + 1) * FH],
                                       xeT[s][:, k, :], start=(k == 0), stop=(k == KD - 1))
                mm.then_inc(ex_g, 1)

            def down(e, s, before):
                pe.wait_ge(ed_in[s], 16 * before + 16)
                for f in range(2):
                    mm = pe.matmul(bank[1][:, KD * P:KD * P + D], e_hid[0:FH, s, f, :], w_dn[s][0:FH, f, :],
                                   start=(f == 0), stop=(f == 1))
                mm.then_inc(ex_done, 1)

            def experts_in(u, place, base, before, odd, count=EPP):
                j = TURNS.get((u, place), EPP)
                if j <= count and j < EPP:
                    pe.wait_ge(ex_h, base + j + 1)
                    if j < count:
                        rows_turn((odd + j + 1) % 2, before + (odd + j + 1) // 2)
                    down(base + j, (odd + j) % 2, before + (odd + j) // 2)
                j = GATES.get((u, place), count)
                if j < count:
                    gate_up(base + j + 1, (odd + j + 1) % 2, before + (odd + j + 1) // 2)

            def first_expert(u, place):
                if (u, place) == FIRST_ROWS:
                    rows_turn(0, 0).then_inc(ex_t, 1)
                if (u, place) == FIRST_GATE:
                    gate_up(0, 0, 0)

            def merge_qk(p, i, turn_):
                pe.wait_ge(pair_in[i], 48 * turn_ + 48)
                at_least(pe, at_qrope, 6 * p)
                for h in range(2):
                    for k, n in ((0, P), (1, QL - P)):
                        mm = pe.matmul(bank[0][0:n, (2 * h + k) * P:(2 * h + k + 1) * P], w_q[i][:, h, k * P:k * P + n],
                                       w_vk[i][:, h, KVL:3 * KVL], start=True, stop=True)
                mm.then_inc(at_m, 1)

            def merge_vo(p, i, where):
                for h in range(2):
                    mm = pe.matmul(where[:, h * D:(h + 1) * D], w_vk[i][:, h, h * KVL:h * KVL + 2 * KVL], w_o[i][:, h, :],
                                   start=True, stop=True)
                mm.then_inc(at_m, 1)

            def project(p, m, i, where):
                c, part = m // 3, (2, 0, 1)[m % 3]
                for k in range(2):
                    mm = pe.matmul(where[:, :], w_eff[i][:, k, part * P:(part + 1) * P],
                                   qk[:, 3 * k, c * CH:(c + 1) * CH], start=(k == 0), stop=(k == 1))
                mm.then_inc(at_q, 1)

            def scores(g, p, u, i):
                b, h = u // 2, u % 2
                pe.wait_ge(at_qe, 4 * p + 2 * (b // 2) + 2)
                at_least(pe, at_exp, 2 * g - 2)
                for q in range(QT):
                    mm = pe.matmul(bank[3 + u % 2][:, q * S:(q + 1) * S],
                                   qb[i][:, h, b * S + q * P:b * S + (q + 1) * P], qk[:, 1 + h, b * S:(b + 1) * S],
                                   start=True, stop=True)
                mm.then_inc(at_s, 1)

            def probs_turn(g, u):
                pe.wait_ge(at_norm, g + 1)
                at_least(pe, at_tout, g - 1)
                dst = bank[5 + u % 2][:, :].rearrange("p (k n) -> p k n", k=QT)
                for k in range(QT):
                    for q in range(QT):
                        mm = pe.transpose(dst[:, k, q * P:(q + 1) * P], probs[:, u % 4, q, k * P:(k + 1) * P], ident)
                mm.then_inc(at_t, 1)

            def values(g, u):
                b, h = u // 2, u % 2
                pe.wait_ge(at_tout, g + 1)
                at_least(pe, at_ctx, g - 1)
                for k in range(QT):
                    mm = pe.matmul(bank[2 + 5 * h][0:KVL, 0:S], kv_tok[:, QT * b + k, 0:KVL],
                                   probsT[:, u % 2, k, :], start=(k == 0), stop=(k == QT - 1))
                mm.then_inc(at_pv, 1)

            def pair(p, i, turn_, first, last, experts):
                for u in range(UNITS):
                    g = UNITS * p + u
                    scores(g, p, u, i)
                    experts(u, 0)
                    if not (first and u < 2):
                        probs_turn(g - 2, (u - 2) % UNITS)
                    if not (first and u < 3):
                        values(g - 3, (u - 3) % UNITS)
                    experts(u, 1)
                    if not last:
                        if u == 0:
                            merge_qk(p + 1, 1 - i, turn_)
                        elif u == 1:
                            pe.wait_ge(at_eff, 2 * p + 3)
                            merge_vo(p + 1, 1 - i, bank[0])
                        else:
                            if u == 2:
                                pe.wait_ge(at_eff, 2 * p + 4)
                            else:
                                pe.wait_ge(at_qrope, 6 * p + 6 + u - 2)
                            project(p + 1, u - 2, 1 - i, bank[0])
                    experts(u, 2)

            pe.wait_ge(sh_add, NT)
            pe.wait_ge(latT_out, 2 * NT)
            merge_qk(0, 0, 0)
            merge_vo(0, 0, bank[1])
            for m in range(6):
                pe.wait_ge(at_eff, min(m + 1, 2))
                at_least(pe, at_qrope, m - 1)
                project(0, m, 0, bank[m % 2])
            pair(0, 0, 0, True, False, first_expert)
            with pe.Fori(0, LOOPED // 2) as i:
                for k in range(2):
                    pair(2 * i + 1 + k, 1 - k, i + 1, False, False,
                         lambda u, place: experts_in(u, place, 2 * EPP * i + EPP * k, EPP * i + EPP // 2 * k, k))
            pair(PAIRS - 1, 1, 0, False, True, lambda u, place: experts_in(u, place, E0 - 2, E0 // 2 - 1, 0, 1))
            G = PAIRS * UNITS
            probs_turn(G - 2, UNITS - 2)
            values(G - 3, UNITS - 3)
            probs_turn(G - 1, UNITS - 1)
            values(G - 2, UNITS - 2)
            values(G - 1, UNITS - 1)

            def turn1(g, src, ready, n):
                pe.wait_ge(ready, n)
                at_least(pe, turned_out, g - 1)
                for k in range(KD):
                    for i in range(2):
                        mm = pe.transpose(bank[turn_bank(g)][:, (2 * k + i) * P:(2 * k + i + 1) * P],
                                          src[:, 2 * (g % 4) + i, k * P:(k + 1) * P], ident)
                mm.then_inc(turned, 1)

            for i in range(NT):
                pe.wait_ge(at_ctx, G - UNITS + 2 * (i // QT) + 2)
                at_least(pe, op_add, i - 1)
                for p in range(PAIRS):
                    mm = pe.matmul(bank[i % 2][:, 0:D], ctxT[:, p, i * P:(i + 1) * P], w_vo[:, p, :],
                                   start=(p == 0), stop=(p == PAIRS - 1))
                mm.then_inc(op_mm, 1)
                if i in (3, 5, 7):
                    g = 8 + (i - 3) // 2
                    turn1(g, xn1, xn_done, NT + 2 * (g % 4) + 2)

            pe.wait_ge(op_add, NT)
            pe.wait_ge(w3_in, 64)
            for i in range(NT):
                if i == 4:
                    turn1(11, xn1, xn_done, 2 * NT)
                pe.wait_ge(turned_out, 9 + i // 2)
                at_least(pe, rope_mul, 3 * (i - 1))
                at_least(pe, v_out, i - 1)
                for part, (a, b) in enumerate(((0, 2 * D), (2 * D, 3 * D + E1))):
                    for k in range(KD):
                        mm = pe.matmul(bank[4 + 2 * (i % 2) + part][:, 0:b - a], x1T[:, k, i * P:(i + 1) * P],
                                       w_qkvg[:, k, a:b], start=(k == 0), stop=(k == KD - 1))
                mm.then_inc(qkv_mm, 1)
            for i in range(NT):
                pe.wait_ge(rope_add, i + 1)
                at_least(pe, qkT_out, i - 3)
                for j in range(4):
                    mm = pe.transpose(bank[i % 4][:, j * P:(j + 1) * P], qk_tok[:, i, j * P:(j + 1) * P], ident)
                mm.then_inc(qkT_mm, 1)
            pe.wait_ge(rope_mul, 3 * NT)
            pe.wait_ge(v_out, NT)
            pe.wait_ge(kmean_done, 1 + KD * HG)
            for i in range(NT):
                for k in range(KD):
                    mm = pe.matmul(bank[i // 4][:, (i % 4) * P:(i % 4 + 1) * P], qkT[:, k, i * P:(i + 1) * P],
                                   kmean[:, k, i // QT, :], start=(k == 0), stop=(k == KD - 1))
                mm.then_inc(blk_mm, 1)
            for n, (what, j, h, c) in enumerate(fills()):
                at_least(pe, fill_out, n - 3)
                dst = bank[4 + n % 4]
                if what == "low":
                    for k in range(KD):
                        mm = pe.matmul(dst[:, :], a13[:, k, j * ER + h * P:j * ER + (h + 1) * P],
                                       x1T[:, k, c * CH:(c + 1) * CH], start=(k == 0), stop=(k == KD - 1))
                elif what == "mask":
                    pe.wait_ge(r1_own, NT * j + 4 * c + 4)
                    for i in range(4):
                        mm = pe.matmul(dst[:, i * P:(i + 1) * P], expert_of[j][:, 4 * c + i, h * P:(h + 1) * P], identb,
                                       start=True, stop=True)
                else:
                    pe.wait_ge(r1_share, 4 * (n - 16) + 4)
                    for i in range(4):
                        mm = pe.transpose(dst[:, i * P:(i + 1) * P], share_rep[:, i, :], ident)
                mm.then_inc(fill_mm, 1)

            def scores1(g, b, k, u):
                pe.wait_ge(bl_q, g + 1)
                at_least(pe, bl_min, 2 * g - 2)
                dst = bank[3 + u % 2]
                keys = qkT[:, 2 + k, bass.ds(b * S, S)]
                pe.matmul(dst[:, 0:P], q_head[k][:, u, 0:P], qkT[:, 2 + k, bass.ds(b * S, P)], start=True, stop=False,
                          skip_group_check=True)
                pe.matmul(dst[:, 0:P], identb, tableb("causal"), start=False, stop=True, skip_group_check=True)
                pe.matmul(dst[:, P:3 * P], q_head[k][:, u, P:S], keys, start=True, stop=False, skip_group_check=True)
                pe.matmul(dst[:, 2 * P:3 * P], identb, tableb("causal"), start=False, stop=True, skip_group_check=True)\
                    .then_inc(bl_s, 1)

            def probs1_turn(g, u):
                pe.wait_ge(bl_exp, 2 * g + 2)
                at_least(pe, bl_tout, g - 1)
                for j in range(3):
                    mm = pe.transpose(bank[5 + u % 2][:, j * P:(j + 1) * P], probs1[:, u % 4, j * P:(j + 1) * P], ident)
                mm.then_inc(bl_t, 1)

            def values1(g, b, k, u):
                pe.wait_ge(bl_tout, g + 1)
                at_least(pe, bl_o, g - 1)
                dst = bank[2 + 5 * (u % 2)]
                v = [v_tok[:, bass.ds(QT * b + j, 1), k * P:(k + 1) * P].rearrange("p o n -> p (o n)") for j in range(QT)]
                pe.matmul(dst[:, 0:P], probs1T[:, u % 2, 0:P], v[0], start=True, stop=True)
                pe.matmul(dst[:, P:2 * P], probs1T[:, u % 2, P:2 * P], v[0], start=True, stop=False)
                pe.matmul(dst[:, P:2 * P], probs1T[:, u % 2, 2 * P:3 * P], v[1], start=False, stop=True).then_inc(bl_v, 1)

            def group(G, b, k, before):
                for u in range(HG):
                    g = HG * G + u
                    scores1(g, b, k, u)
                    if u >= 2:
                        probs1_turn(g - 2, u - 2)
                    elif before is not None:
                        probs1_turn(g - 2, u + HG - 2)
                    if u >= 3:
                        values1(g - 3, b, k, u - 3)
                    elif before is not None:
                        values1(g - 3, before, 1 - k, u + HG - 3)

            pe.wait_ge(fill_out, len(fills()))
            group(0, 0, 0, None)
            with pe.Fori(0, GROUPS // 2 - 1) as i:
                group(2 * i + 1, i, 1, i)
                group(2 * i + 2, i + 1, 0, i)
            group(GROUPS - 1, B - 1, 1, B - 1)
            G = GROUPS * HG
            probs1_turn(G - 2, HG - 2)
            values1(G - 3, B - 1, 1, HG - 3)
            probs1_turn(G - 1, HG - 1)
            values1(G - 2, B - 1, 1, HG - 2)
            values1(G - 1, B - 1, 1, HG - 1)

            def hidden1(f, c, m):
                at_least(pe, f_h, m)
                for j in range(2):
                    dst, a = bank[2 * (f % 3) + j], j * F1 + f * P
                    for k in range(KD):
                        pe.matmul(dst[:, :], w13[:, k, a:a + P], x1T[:, k, c * CH:(c + 1) * CH], start=(k == 0), stop=False,
                                  skip_group_check=True)
                    for h in range(2):
                        mm = pe.matmul(dst[:, :], b13[:, h, a:a + P], am_first[j][:, h, c * CH:(c + 1) * CH],
                                       start=False, stop=(h == 1), skip_group_check=True)
                mm.then_inc(f_mm, 1)

            def hidden2(f, c, m):
                pe.wait_ge(f_h, m)
                for j in range(2):
                    dst, a = bank[2 * (f % 3) + j], j * F1 + f * P
                    for h in range(2):
                        mm = pe.matmul(dst[:, :], b13[:, h, a:a + P], am_step[j][:, h, c * CH:(c + 1) * CH],
                                       start=False, stop=(h == 1), skip_group_check=True)
                mm.then_inc(f_mm, 1)

            pe.wait_ge(low_rank, 4)
            pe.wait_ge(b13_in, 16)
            pe.wait_ge(bl_o, GROUPS * HG)
            m = 0
            for c in range(TOK // CH):
                if c:
                    pe.wait_ge(y_done, 4 * c)
                done = {}
                for n, (f, k) in enumerate(uses()):
                    if k == 0:
                        hidden1(f, c, done.get((f - 3, 1), m if f == 0 else 0))
                    else:
                        hidden2(f, c, done[f, 0])
                    m += 1
                    done[f, k] = m
                    if c == 0 and n == 4:
                        for g in range(12, 16):
                            turn1(g, o_tok, on_done, 2)
                pe.wait_ge(f_x2, NF1 * (c + 1) - 1)
                pe.wait_ge(w2_in, 48)
                at_least(pe, f_am2, 6 * c)
                for j, src in enumerate((h_first, h_both)):
                    for h in range(2):
                        for f in range(NF1):
                            if f == NF1 - 1:
                                pe.wait_ge(f_x2, NF1 * (c + 1))
                            mm = pe.matmul(bank[4 + 2 * j + h][:, :], a2[:, f, h * P:(h + 1) * P], src[:, f, :],
                                           start=(f == 0), stop=(f == NF1 - 1))
                mm.then_inc(f_a2, 1)
                pe.wait_ge(turned_out, 16)
                pe.wait_ge(f_h, m)
                for i in range(4):
                    terms = [(h_both[:, f, i * P:(i + 1) * P], w2[:, f, :]) for f in range(NF1)]
                    terms += [(oT[:, k, (4 * c + i) * P:(4 * c + i + 1) * P], w_o1[:, k, :]) for k in range(KD)]
                    terms += [(am2[:, h, i * P:(i + 1) * P], b2[:, h, :]) for h in range(2)]
                    for n, (lhs, rhs) in enumerate(terms):
                        if n == NF1 + KD:
                            pe.wait_ge(f_am2, 6 * c + 6)
                        mm = pe.matmul(bank[i][:, 0:D], lhs, rhs, start=(n == 0), stop=(n == len(terms) - 1))
                    mm.then_inc(f_down, 1)


def kernel(**inputs):
    import concourse.bacc as bacc
    from concourse.bass_utils import run_bass_kernel_spmd

    arrays = lay_out(inputs)
    nc = bacc.Bacc("TRN2", target_bir_lowering=False, num_devices=1)
    t = {name: nc.dram_tensor(f"in_{name}", a.shape, mybir.dt.from_np(a.dtype), kind="ExternalInput").ap()
         for name, a in arrays.items()}
    y = nc.dram_tensor("out", (TOK, D), F32, kind="ExternalOutput").ap()
    program(nc, t, y)
    r = run_bass_kernel_spmd(nc, [{f"in_{name}": a for name, a in arrays.items()}], core_ids=[0])
    return r.results[0]["out"].reshape(B, S, D)
```

```python
from contextlib import ExitStack

import numpy as np

import concourse.bass as bass
from concourse import mybir

F32 = mybir.dt.float32
F32R = mybir.dt.float32r
BF16 = mybir.dt.bfloat16
U32 = mybir.dt.uint32
ALU = mybir.AluOpType
ACT = mybir.ActivationFunctionType
AX = mybir.AxisListType

P = 128
B, S, D = 4, 256, 256
TOK = B * S
NT = TOK // P
QT = S // P
KD = D // P
H0, QL, KVL, DN, DR, DV = 16, 192, 64, 128, 64, 128
PAIRS = H0 // 2
UNITS = 2 * B
LATW = QL + KVL + 2 * DR
E0, TOPK0, F0, FS, CAP = 32, 4, 176, 704, 128
FH = F0 // 2
NF = -(-FS // P)
SETS = 2
EPP = 5
LOOPED = PAIRS - 2
TURNS = {(0, 0): 0, (1, 2): 1, (3, 1): 2, (4, 2): 3, (6, 1): 4}
GATES = {(0, 2): 0, (2, 1): 1, (4, 0): 2, (5, 2): 3, (7, 1): 4}
HIDDEN = {(0, 2): 0, (2, 1): 1, (4, 1): 2, (5, 2): 3, (7, 1): 4}
FIRST_ROWS, FIRST_GATE, FIRST_HIDDEN = (6, 1), (7, 1), (7, 1)
assert EPP * LOOPED == E0 - 2
TURN_LAG, COPY_LAG, VALUE_LAG, CONTEXT_LAG = 3, 4, 5, 6
H1, CHUNK, TOPK1 = 16, 32, 4
D1 = D // H1
NB = S // CHUNK
GROUPS = 8
HG = H1 // 2
F1, E1, R1 = 896, 8, 32
ER = E1 * R1
NF1 = F1 // P
CH = 512
BIG = 1e30
HUGE = 3e38


def columns(spec):
    at, out = 0, {}
    for name, n in spec:
        out[name] = (at, n)
        at += n
    return out, at


CF, CF_N = columns([("ident", P), ("q_even", S), ("q_odd", S), ("q_sin", S), ("k_cos", QT * DR), ("k_sin", QT * DR),
                    ("iota", E0), ("cos1", QT * D1), ("sin1", QT * D1), ("keep", QT * H1 * NB),
                    ("force", QT * H1 * NB), ("future", QT * NB), ("later", NB), ("head_mean", HG),
                    ("head_scale", HG), ("eps_norm", 1)])
CB, CB_N = columns([("ident", P), ("before", P), ("ones", P), ("causal", P)])
BC, BC_N = columns([("lat_w", QL + KVL), ("lat_b", QL + KVL), ("w_norm", D), ("o_norm", D1)])

SMALL = 2304
REGIONS = (SMALL, 4 * NT * D, 18432, 6672, 6528)
ROUNDED = 3 * 2 * TOK
ALIGN = 8
LEAD = -(-(CF_N + BC_N + NT * D + SMALL) // ALIGN) * ALIGN
SB_COLS = LEAD + sum(REGIONS[1:])
V_AT, PT_AT = 3 * NT * D // 2, 3 * NT * D
TILE_AT = (0, 1, 2, 4, 5, 3, 6, 7)
LATE = 5
A13_AT = KD * (3 * D + E1) + KD * D
B13_END = 2 * 2 * F1 + 2 * TOK


def tables():
    cf = np.zeros((P, CF_N), np.float32)
    cb = np.zeros((P, CB_N), np.float32)

    def put(name, a):
        at, n = CF[name]
        cf[:, at:at + n] = np.asarray(a, np.float32).reshape(P, n)

    def putb(name, a):
        at, n = CB[name]
        cb[:, at:at + n] = a

    i = np.arange(P)
    put("ident", np.eye(P))
    inv = 1.0 / 10000.0 ** (np.arange(0, DR, 2, dtype=np.float32) / DR)
    fr = np.outer(np.arange(S, dtype=np.float32), inv)
    emb = np.concatenate([fr, fr], -1)
    cos, sin = np.cos(emb), np.sin(emb)
    signed = np.concatenate([-sin[:, :DR // 2], sin[:, DR // 2:]], -1)
    sc = np.float32(-1.0 / np.sqrt(DN + DR))
    one = np.full((DR, S), sc, np.float32)
    put("q_even", np.concatenate([one, sc * cos.T]))
    put("q_odd", np.concatenate([sc * cos.T, one]))
    put("q_sin", np.concatenate([sc * signed.T, sc * signed.T]))
    put("k_cos", cos.reshape(QT, P, DR).transpose(1, 0, 2))
    put("k_sin", signed.reshape(QT, P, DR).transpose(1, 0, 2))
    put("iota", np.tile(np.arange(E0), (P, 1)))
    inv1 = (1.0 / np.float32(10000.0) ** (np.arange(0, D1, 2).astype(np.float32) / np.float32(D1))).astype(np.float32)
    f1 = np.arange(S, dtype=np.float32)[:, None] * inv1
    c1, s1 = np.cos(f1), np.sin(f1)
    put("cos1", np.concatenate([c1, c1], -1).reshape(QT, P, D1).transpose(1, 0, 2))
    put("sin1", np.concatenate([-s1, s1], -1).reshape(QT, P, D1).transpose(1, 0, 2))
    own = np.arange(S)[:, None] // CHUNK
    n = np.arange(NB)[None, :]

    def rows(a):
        return np.repeat(a.reshape(QT, P, 1, NB), H1, 2).transpose(1, 0, 2, 3)

    put("keep", rows((n < own).astype(np.float32)))
    put("force", rows(np.where(n > own, -BIG, np.where(n == own, BIG, 0.0))))
    put("future", np.where(n > own, BIG, 0.0).reshape(QT, P, NB).transpose(1, 0, 2))
    put("later", np.tile(NB - 1 - np.arange(NB), (P, 1)))
    mine = (i[:, None] // D1 == np.arange(HG)[None, :]).astype(np.float32)
    put("head_mean", mine / CHUNK)
    put("head_scale", -mine * D1 ** -0.5)
    put("eps_norm", np.full((P, 1), 1e-5))
    putb("ident", np.eye(P))
    putb("before", i[:, None] < i[None, :])
    putb("ones", 1.0)
    putb("causal", np.where(i[None, :] > i[:, None], BIG, 0.0))
    return cf, cb.astype(mybir.dt.np(BF16))


def lay_out(a):
    f = {k: np.asarray(v) for k, v in a.items()}

    def tiles(w):
        return w.reshape(-1, P, w.shape[1]).transpose(1, 0, 2)

    def rep(*v):
        return np.tile(np.concatenate(v)[None, :], (P, 1))

    def swap(w):
        return np.concatenate([w[..., DR // 2:, :], w[..., :DR // 2, :]], -2)

    out = {"x": f["L0_attn_hidden_states"].reshape(TOK, D)}
    out["consts"], out["consts_b"] = tables()
    out["rows"] = rep(f["L0_attn_q_a_ln_w"], f["L0_attn_kv_a_ln_w"], f["L0_attn_q_a_ln_b"], f["L0_attn_kv_a_ln_b"],
                      f["L0_ffn_w_norm"], f["L1_attn_o_norm_w"])
    kva = f["L0_attn_kv_a_w"]
    out["w_lat"] = tiles(np.concatenate([f["L0_attn_q_a_w"], kva[:KVL], kva[KVL:], swap(kva[KVL:])]).T)
    wq = f["L0_attn_q_b_w"].reshape(PAIRS, 2, DN, QL).transpose(0, 2, 1, 3)
    kvb = f["L0_attn_kv_b_w"].reshape(PAIRS, 2, 2, DN, KVL)
    vkv = np.concatenate([kvb[:, :, 1], kvb[:, :, 0], kvb[:, :, 1]], -1).transpose(0, 2, 1, 3)
    wo = f["L0_attn_o_w"].T.reshape(PAIRS, 2, DV, D).transpose(0, 2, 1, 3)
    wq = np.concatenate([wq, wq[..., P:]], -1)
    out["w_pair"] = np.concatenate([w.reshape(PAIRS, P, -1) for w in (wq, vkv, wo)], -1)
    qr = f["L0_attn_q_rope_w"].reshape(PAIRS, 2, DR, QL)
    qs = swap(qr)
    out["w_rope"] = np.stack([np.concatenate([qr[:, 0], qr[:, 1]], 1), np.concatenate([qs[:, 1], qs[:, 0]], 1)],
                             1).transpose(0, 3, 1, 2)
    out["w_route"] = tiles(np.concatenate([f["L0_ffn_w_router"], f["L0_ffn_w_shared_gate"],
                                           np.zeros((D, P - E0 - 1), np.float32)], 1))
    pad = np.zeros((D, NF * P - FS), np.float32)
    out["sw_up"] = tiles(np.concatenate([f["L0_ffn_sw_gate"], pad, f["L0_ffn_sw_up"], pad], 1))
    out["sw_down"] = tiles(np.concatenate([f["L0_ffn_sw_down"], np.zeros((NF * P - FS, D), np.float32)]))
    gu = np.stack([f["L0_ffn_w_gate"], f["L0_ffn_w_up"]], 2)
    out["w_gate_up"] = gu.reshape(E0, KD, P, 2 * F0).transpose(0, 2, 1, 3)
    out["w_down"] = f["L0_ffn_w_down"].reshape(E0, 2, FH, D).transpose(0, 2, 1, 3)
    out["w_qkvg"] = tiles(np.concatenate([f["L1_attn_Wq"], f["L1_attn_Wk"], f["L1_attn_Wv"], f["L1_ffn_Wg"]]).T)
    out["w_o1"] = tiles(f["L1_attn_Wo"].T)
    out["w13"] = tiles(np.concatenate([f["L1_ffn_W1"], f["L1_ffn_W3"]]).T)
    out["a13"] = tiles(np.concatenate([f["L1_ffn_A1"].reshape(ER, D), f["L1_ffn_A3"].reshape(ER, D)]).T)
    out["b13"] = tiles(np.concatenate([f["L1_ffn_B1"].transpose(0, 2, 1).reshape(ER, F1),
                                       f["L1_ffn_B3"].transpose(0, 2, 1).reshape(ER, F1)], 1))
    out["w2"] = tiles(f["L1_ffn_W2"].T)
    out["a2"] = tiles(f["L1_ffn_A2"].reshape(ER, F1).T)
    out["b2"] = tiles(f["L1_ffn_B2"].transpose(0, 2, 1).reshape(ER, D))
    return {k: np.ascontiguousarray(v) for k, v in out.items()}


class Strip:

    def __init__(self, whole, at, n):
        self.whole, self.at, self.end = whole, at, at + n

    def take(self, *shape):
        n = int(np.prod(shape))
        assert self.at + n <= self.end, "the strip is full"
        ap = self.whole[:, self.at:self.at + n]
        self.at += n
        if len(shape) == 2:
            return ap.rearrange("p (a b) -> p a b", b=shape[1])
        if len(shape) == 3:
            return ap.rearrange("p (a b c) -> p a b c", b=shape[1], c=shape[2])
        return ap

    def take_b(self, *shape):
        n = int(np.prod(shape))
        ap = self.take(n // 2).bitcast(BF16)
        if len(shape) == 2:
            return ap.rearrange("p (a b) -> p a b", b=shape[1])
        if len(shape) == 3:
            return ap.rearrange("p (a b c) -> p a b c", b=shape[1], c=shape[2])
        return ap


def along(ap, *dims):
    for at, n in dims:
        ap = ap.unsqueeze(at)
        shape = list(ap.shape)
        shape[at] = n
        ap = ap.broadcast_to(shape)
    return ap


def at_least(eng, sem, n):
    if not isinstance(n, int) or n > 0:
        eng.wait_ge(sem, n)


def program(nc, t, y):
    ctx = ExitStack()
    with ctx:
        def sem(name):
            return ctx.enter_context(nc.semaphore(name))

        with ExitStack() as overlay:
            end = 0

            def over(name, at, n):
                nonlocal end
                if at > end:
                    overlay.enter_context(nc.sbuf_tensor(f"before_{name}", [P, at - end], F32))
                end = at + n
                return overlay.enter_context(nc.sbuf_tensor(name, [P, n], F32))

            start = [LEAD + sum(REGIONS[1:i]) for i in range(1, 5)]
            v_parts = over("v_parts", start[0] + V_AT, NT * P)
            pt_parts = over("pt_parts", start[0] + PT_AT, 2 * 2 * S * QT)
            am_first_lo = over("am_first_lo", start[1], 2 * TOK)
            am_step_lo = over("am_step_lo", start[1] + 2 * 2 * TOK, 2 * TOK)
            b1_hi0 = over("b1_hi0", start[2] + A13_AT, F1)
            b1_lo = over("b1_lo", start[3], 2 * 2 * F1)
            b1_hi1 = over("b1_hi1", start[3] + B13_END, F1)
        sb = ctx.enter_context(nc.sbuf_tensor("sb", [P, SB_COLS], F32))
        rd = ctx.enter_context(nc.sbuf_tensor("rounded", [P, ROUNDED], F32))
        cb = ctx.enter_context(nc.sbuf_tensor("cb", [P, CB_N], BF16))
        bank = [ctx.enter_context(nc.psum_tensor(f"bank{i}", [P, 512], F32)) for i in range(8)]
        whole = Strip(sb, 0, SB_COLS)
        cf = whole.take(CF_N)
        rows = whole.take(BC_N)
        acc = whole.take(NT, D)
        small = whole.take(REGIONS[0])
        whole.at = LEAD
        region1 = whole.take(REGIONS[1])
        region2 = whole.take(REGIONS[2])
        region3 = whole.take(REGIONS[3])
        region4 = whole.take(REGIONS[4])

        def strip(region):
            return Strip(region, 0, region.shape[1])

        def table(name, *shape):
            at, n = CF[name]
            ap = cf[:, at:at + n]
            if len(shape) == 2:
                return ap.rearrange("p (a b) -> p a b", b=shape[1])
            return ap

        def row(name):
            at, n = BC[name]
            return rows[:, at:at + n]

        def tableb(name):
            at, n = CB[name]
            return cb[:, at:at + n]

        ident, identb = table("ident"), tableb("ident")

        sm = Strip(small, 0, SMALL)
        stats = sm.take(NT, 6)
        mv = sm.take(NT, 2)
        var, sd, rstd = sm.take(NT), sm.take(NT), sm.take(NT)
        ms, sd2, rrms = sm.take(NT), sm.take(NT), sm.take(NT)
        lat_stats, lat_mv = sm.take(2 * NT, 6), sm.take(2 * NT, 2)
        lat_var, lat_sd, lat_rstd = sm.take(2 * NT), sm.take(2 * NT), sm.take(2 * NT)
        gate_z, gate_e, gate1, gate = sm.take(NT), sm.take(NT), sm.take(NT), sm.take(NT)
        weight4 = sm.take(NT * TOPK0)
        dest = sm.take(NT * TOPK0).bitcast(U32)
        source = sm.take(NT * TOPK0).bitcast(U32)
        row_min = sm.take(4, QT)
        row_sum = sm.take(4, QT)
        row_inv = sm.take(4, QT)

        r1 = strip(region1)
        xn, xnT = r1.take(NT, D), r1.take(KD, TOK)
        x2, x2T = r1.take(NT, D), r1.take(KD, TOK)
        picked = strip(region1).take(NT * TOPK0, D)
        v_parts = v_parts[:, :].rearrange("p (t c) -> p t c", t=NT)
        pt_parts = pt_parts[:, :].rearrange("p (h s k n) -> p h s k n", h=2, s=2, k=QT)
        probs_hi, probs_lo = pt_parts[:, 0], pt_parts[:, 1]

        r2 = strip(region2)
        lat = r2.take(NT, LATW)
        w_lat = r2.take(KD, LATW)
        w_route = r2.take(KD, P)
        sw_up = r2.take(KD, 2 * NF * P)
        sw_down = r2.take(NF, D)
        hT = r2.take(NF, TOK)
        sgate, sup = r2.take(2, CH), r2.take(2, CH)
        zeros = small[:, SMALL - D:SMALL]
        r2 = strip(region2)
        qb = [r2.take(2, TOK) for _ in range(2)]
        q_tmp = r2.take(CH)
        probs = r2.take(4, QT, S)
        ctx_low = r2.take(2, S)
        ctxT = r2.take(PAIRS, TOK)
        w_vo = r2.take(PAIRS, D)

        r3 = strip(region3)
        xe = r3.take(SETS, D)
        w_gu = [r3.take(KD, 2 * F0) for _ in range(SETS)]
        w_dn = [r3.take(2, D) for _ in range(SETS)]
        xeT = [r3.take(KD, P) for _ in range(2)]
        e_act, e_gu, e_hid = r3.take(2, 2, P), r3.take(2, 2, P), r3.take(2, 2, P)
        ye = r3.take(SETS, D)
        rope_raw = [r3.take(2, 4 * DR) for _ in range(2)]

        r4 = strip(region4)
        wq_n, wvk_n = 2 * 2 * P, 2 * 3 * KVL
        w_pair = [r4.take(wq_n + wvk_n + 2 * D) for _ in range(2)]
        w_q = [w[:, 0:wq_n].rearrange("p (h n) -> p h n", h=2) for w in w_pair]
        w_vk = [w[:, wq_n:wq_n + wvk_n].rearrange("p (h n) -> p h n", h=2) for w in w_pair]
        w_o = [w[:, wq_n + wvk_n:].rearrange("p (h n) -> p h n", h=2) for w in w_pair]
        rounded = Strip(rd, 0, ROUNDED)
        q_hi, q_lo, q_rest = (rounded.take(TOK) for _ in range(3))
        w_hi, w_lo, w_rhi, w_rlo = ([rounded.take(6 * DR) for _ in range(2)] for _ in range(4))
        keys = r4.take(2, TOK)
        kv_tok = r4.take(NT, 3 * KVL)
        r4 = strip(region4)
        logit, expo, prob = r4.take(NT, E0), r4.take(NT, E0), r4.take(NT, E0)
        route_max, route_sum, route_inv = r4.take(NT), r4.take(NT), r4.take(NT)
        top, top_at = r4.take(NT, 8), r4.take(NT, 8).bitcast(U32)
        chosen = r4.take(NT, TOPK0)
        onehot = r4.take(NT, TOPK0, E0)
        mask = r4.take(NT, E0)
        maskb = r4.take_b(NT, E0)
        place4, over, clipped = r4.take(NT * TOPK0), r4.take(NT * TOPK0), r4.take(NT * TOPK0)
        dest_f, source_f = r4.take(NT * TOPK0), r4.take(NT * TOPK0)
        assert r4.at <= 2 * (wq_n + wvk_n + 2 * D)

        logit1, expo1, prob1 = sm.take(NT, E1), sm.take(NT, E1), sm.take(NT, E1)
        max1, sum1, inv1 = sm.take(NT), sm.take(NT), sm.take(NT)
        top1, top1_at, chosen1 = sm.take(NT, 8), sm.take(NT, 8).bitcast(U32), sm.take(NT, 2)
        share = sm.take(NT, 2)
        bias_g = sm.take(2, QT, HG * NB)
        o_var, o_sd, o_inv = sm.take(NT, H1), sm.take(NT, H1), sm.take(NT, H1)
        assert sm.at <= SMALL - D
        r1 = strip(region1)
        x1T = r1.take(KD, TOK)
        qkT = r1.take(4, TOK)
        v_tok = r1.take(NT, D)
        r1 = Strip(region1, KD * TOK, 4 * TOK + NT * D)
        w2, a2, b2 = r1.take(NF1, D), r1.take(NF1, ER), r1.take(2, D)
        oT = r1.take(KD, TOK)
        xn1 = strip(region2).take(NT, D)
        r2 = strip(region2)
        am_first = [r2.take(2, TOK) for _ in range(2)]
        am_step = [r2.take(2, TOK) for _ in range(2)]
        phase = r2.at
        r2.take(NT * D)
        qk_tok = r2.take(NT, 2 * D)
        rope_tmp = r2.take(2, 2, 2 * D)
        kmean = r2.take(KD, B, H1 * NB)
        kblock = r2.take(KD, B * NB)
        r2 = Strip(region2, phase + 2 * NT * D, NT * D)
        expert_of = [r2.take_b(NT, ER) for _ in range(2)]
        share_rep = Strip(region2, phase + NT * D, 2 * NT * P).take(2 * NT, P)
        r2 = Strip(region2, phase, region2.shape[1] - phase)
        q_head = [r2.take(HG, S) for _ in range(2)]
        masked = r2.take(4, 3 * P)
        probs1 = r2.take(4, 3 * P)
        probs1T = r2.take(2, 3 * P)
        probs1_end = r2.at
        r2 = Strip(region2, phase, region2.shape[1] - phase)
        h_first = r2.take(NF1, CH)
        h_both = r2.take(NF1, CH)
        f_act = r2.take(2, CH)
        o_tok = r2.take(NT, D)
        assert probs1_end <= phase + 2 * NF1 * CH + 2 * CH
        squares = h_both.rearrange("p f n -> p (f n)")[:, 0:NT * D].rearrange("p (t h d) -> p (t h) d", h=H1, d=D1)
        r3 = strip(region3)
        w_qkvg = r3.take(KD, 3 * D + E1)
        w_o1, a13, w13 = r3.take(KD, D), r3.take(KD, 2 * ER), r3.take(KD, 2 * F1)
        rank = strip(region3).take(NT, H1 * NB)
        r3 = strip(region3)
        am2, am2_tmp = r3.take(2, CH), r3.take(CH)
        r4 = strip(region4)
        b13 = r4.take(2, 2 * F1)
        shareT = r4.take(2, TOK)
        rounded = Strip(rd, 0, ROUNDED)
        first_maskT, second_maskT, step_maskT = (rounded.take(2, TOK) for _ in range(3))
        b1_hi = [b1_hi0[:, :], b1_hi1[:, :]]
        b1_lo = [b1_lo[:, h * 2 * F1:h * 2 * F1 + F1] for h in range(2)]
        rounded = Strip(rd, 0, 2 * TOK)
        am_first_hi, am_step_hi = rounded.take(2, CH), rounded.take(2, CH)
        am_first_lo, am_step_lo = (a[:, :].rearrange("p (h n) -> p h n", h=2) for a in (am_first_lo, am_step_lo))
        r4 = strip(region4)
        score_blk = r4.take(NT * H1, NB)
        beats_first = [r4.take_b(QT * H1, NB - d) for d in range(1, NB)]
        beats_rest = [r4.take_b((NT - QT) * H1, NB - d) for d in range(1, NB)]
        assert r4.at <= 2 * 2 * F1

        buf = nc.dram_tensor("expert_in", [E0 * CAP, D], F32).ap()
        res = nc.dram_tensor("expert_out", [E0 * CAP, D], F32).ap()

        x_in = [sem(f"x_in{i}") for i in range(4)]
        cf_in, cb_in, rows_in, lat_in, route_in = (sem(n) for n in ("cf_in", "cb_in", "rows_in", "lat_in", "route_in"))
        up_in, down_in, zero_set, zero_in = (sem(n) for n in ("up_in", "down_in", "zero_set", "zero_in"))
        ln_stats, ln_mv, ln_var, ln_sd, ln_rstd = (sem(n) for n in ("ln_stats", "ln_mv", "ln_var", "ln_sd", "ln_rstd"))
        xn_done, ms_step, ms_var, ms_sd, ms_inv, x2_done = (
            sem(n) for n in ("xn_done", "ms_step", "ms_var", "ms_sd", "ms_inv", "x2_done"))
        acc_done = sem("acc_done")
        turned, turned_out = sem("turned"), sem("turned_out")
        lat_mm, lat_out, logit_mm = sem("lat_mm"), sem("lat_out"), sem("logit_mm")
        lat_st, lat_ag, lat_vr, lat_sdev, lat_rs, lat_norm, lat_scaled, lat_rope, lat_done = (
            sem(n) for n in ("lat_st", "lat_ag", "lat_vr", "lat_sdev", "lat_rs", "lat_norm", "lat_scaled", "lat_rope",
                             "lat_done"))
        latT_mm, latT_out = sem("latT_mm"), sem("latT_out")
        rt_max, rt_sub, rt_exp, rt_step, rt_mask, rt_pos, rt_dest = (
            sem(n) for n in ("rt_max", "rt_sub", "rt_exp", "rt_step", "rt_mask", "rt_pos", "rt_dest"))
        sh_mm, sh_act, sh_h, sh_down, sh_add = (sem(n) for n in ("sh_mm", "sh_act", "sh_h", "sh_down", "sh_add"))
        at_split, rope_split = sem("at_split"), sem("rope_split")
        scattered, combined = sem("scattered"), sem("combined")
        gathered = [sem(f"gathered{i}") for i in range(NT)]
        ew_in = [sem(f"ew_in{s}") for s in range(SETS)]
        ed_in = [sem(f"ed_in{s}") for s in range(SETS)]
        ye_free = sem("ye_free")
        eb_in = [sem(f"eb_in{s}") for s in range(SETS)]
        y_stored = [sem(f"y_stored{s}") for s in range(SETS)]
        ex_t, ex_tout, ex_g, ex_act, ex_gu, ex_h, ex_done, ex_y = (
            sem(n) for n in ("ex_t", "ex_tout", "ex_g", "ex_act", "ex_gu", "ex_h", "ex_done", "ex_y"))
        pair_in = [sem(f"pair_in{i}") for i in range(2)]
        at_m, at_eff, at_q, at_qrope, at_qe = (sem(n) for n in ("at_m", "at_eff", "at_q", "at_qrope", "at_qe"))
        at_s, at_min, at_exp, at_inv, at_norm, at_t, at_tout, at_pv, at_ctx = (
            sem(n) for n in ("at_s", "at_min", "at_exp", "at_inv", "at_norm", "at_t", "at_tout", "at_pv", "at_ctx"))
        at_v, at_lo, at_cl = sem("at_v"), sem("at_lo"), sem("at_cl")
        op_mm, op_add = sem("op_mm"), sem("op_add")
        l1_sd = sem("l1_sd")
        w3_in, b13_in, w2_in = sem("w3_in"), sem("b13_in"), sem("w2_in")
        qkv_mm, rope_mul, rope_add, v_out, qkT_mm, qkT_out = (
            sem(n) for n in ("qkv_mm", "rope_mul", "rope_add", "v_out", "qkT_mm", "qkT_out"))
        kmean_set, kmean_done, blk_mm, blk_step = (sem(n) for n in ("kmean_set", "kmean_done", "blk_mm", "blk_step"))
        blk_beats, blk_count, rest_beats, rest_count = (
            sem(n) for n in ("blk_beats", "blk_count", "rest_beats", "rest_count"))
        r1_step, r1_sub, r1_exp, r1_own, r1_share = (sem(n) for n in ("r1_step", "r1_sub", "r1_exp", "r1_own", "r1_share"))
        b1_split, am_split = sem("b1_split"), sem("am_split")
        fill_mm, fill_out, step_mask, low_rank = (sem(n) for n in ("fill_mm", "fill_out", "step_mask", "low_rank"))
        bl_q, bl_bias, bl_s, bl_min, bl_exp, bl_inv, bl_t, bl_tout, bl_v, bl_o = (
            sem(n) for n in ("bl_q", "bl_bias", "bl_s", "bl_min", "bl_exp", "bl_inv", "bl_t", "bl_tout", "bl_v", "bl_o"))
        on_sq, on_step, on_sd, on_done = (sem(n) for n in ("on_sq", "on_step", "on_sd", "on_done"))
        f_mm, f_silu, f_h, f_x, f_x2, f_a2, f_am2, f_down = (
            sem(n) for n in ("f_mm", "f_silu", "f_h", "f_x", "f_x2", "f_a2", "f_am2", "f_down"))
        y_done, stored = sem("y_done"), sem("stored")

        def r(ap):
            return ap.bitcast(F32R)

        def merged(w):
            return w.rearrange("p (h c) -> p h c", h=2)[:, :, 0:DR]

        def rope(w):
            return w.rearrange("p (h c) -> p h c", h=2)[:, :, DR:3 * DR]

        def fills():
            out = [("low", j, h, c) for j in range(2) for h in range(2) for c in range(TOK // CH)]
            out += [("mask", k, h, c) for k in range(2) for h in range(2) for c in range(TOK // CH)]
            return out + [("share", k, 0, c) for k in range(2) for c in range(TOK // CH)]

        def turn_bank(g):
            return g % 4 if g < 8 else (2 if g < 12 else 6) + g % 2

        def uses():
            out = [(0, 0)]
            for f in range(1, NF1):
                out += [(f, 0), (f - 1, 1)]
            return out + [(NF1 - 1, 1)]

        first_heads, rest_heads = slice(0, QT * H1), slice(QT * H1, NT * H1)

        def compare(eng, heads, beats, step, d):
            eng.tensor_tensor(beats[d - 1], score_blk[:, heads, 0:NB - d], score_blk[:, heads, d:NB], ALU.is_ge)\
                .then_inc(step, 1)

        def count(eng, heads, beats, compared, step):
            ranks = rank.rearrange("p t (h n) -> p (t h) n", n=NB)[:, heads, :]
            for d in range(1, NB):
                eng.wait_ge(compared, d)
                eng.tensor_tensor(ranks[:, :, d:NB], ranks[:, :, d:NB], beats[d - 1], ALU.add).then_inc(step, 1)
                eng.wait_ge(step, 2 * d - 1)
                eng.tensor_tensor(ranks[:, :, 0:NB - d], ranks[:, :, 0:NB - d], beats[d - 1], ALU.subtract)\
                    .then_inc(step, 1)
                eng.wait_ge(step, 2 * d)

        block = ctx.enter_context(nc.Block())

        @block.sync
        def _(sp):
            x_t = t["x"].rearrange("(t p) d -> p t d", p=P)
            for i in range(4):
                sp.dma_start(acc[:, 2 * i:2 * i + 2, :], x_t[:, 2 * i:2 * i + 2, :]).then_inc(x_in[i], 16)
            sp.dma_start(cf, t["consts"]).then_inc(cf_in, 16)
            sp.dma_start(rows, t["rows"]).then_inc(rows_in, 16)
            sp.dma_start(w_lat, t["w_lat"]).then_inc(lat_in, 16)
            sp.dma_start(w_route, t["w_route"]).then_inc(route_in, 16)
            sp.dma_start(cb[:, :], t["consts_b"]).then_inc(cb_in, 16)
            sp.dma_start(sw_up, t["sw_up"]).then_inc(up_in, 16)
            sp.dma_start(sw_down, t["sw_down"]).then_inc(down_in, 16)

            def expert_gate_up(e, s):
                sp.dma_start(w_gu[s], t["w_gate_up"][bass.ds(e, 1)].rearrange("o p k n -> p (o k) n"))\
                    .then_inc(ew_in[s], 16)

            def expert_down(e, s):
                sp.dma_start(w_dn[s][0:FH], t["w_down"][bass.ds(e, 1)].rearrange("o p k n -> p (o k) n"))\
                    .then_inc(ed_in[s], 16)

            def expert_rows(e, s):
                sp.dma_start(xe[:, s, :], buf[bass.ds(e * CAP, CAP), :]).then_inc(eb_in[s], 16)

            for s in range(SETS):
                expert_gate_up(s, s)
                expert_down(s, s)
            sp.wait_ge(zero_set, 1)
            sp.dma_start(buf.rearrange("(r p) d -> p r d", p=P), along(zeros, (1, E0))).then_inc(zero_in, 16)

            def pair_weights(p, i):
                rows_r = t["w_rope"][bass.ds(p, 1)].rearrange("o l g c -> l (o g c)")
                sp.dma_start(w_pair[i], t["w_pair"][bass.ds(p, 1)].rearrange("o p n -> p (o n)")).then_inc(pair_in[i], 16)
                sp.dma_start(rope_raw[i][:, 0, :], rows_r[0:P]).then_inc(pair_in[i], 16)
                for a in (0, QL - P):
                    sp.dma_start(rope_raw[i][a:a + QL - P, 1, :], rows_r[P:QL]).then_inc(pair_in[i], 16)

            sp.wait_ge(rt_dest, 2)
            for i in range(2):
                pair_weights(i, i)
            sp.wait_ge(scattered, 16 * NT * TOPK0)
            for s in range(SETS):
                expert_rows(s, s)

            def next_experts(base, odd):
                for j in range(EPP):
                    e, s = base + j, (odd + j) % SETS
                    sp.wait_ge(ex_g, e + 1)
                    expert_rows(e + SETS, s)
                    expert_gate_up(e + SETS, s)
                    sp.wait_ge(ex_done, e + 1)
                    expert_down(e + SETS, s)

            for p in range(2, 4):
                sp.wait_ge(at_q, 6 * (p - 2) + 6)
                pair_weights(p, p % 2)
            next_experts(0, 0)
            with sp.Fori(0, LOOPED // 2 - 1) as i:
                for k in range(2):
                    sp.wait_ge(at_q, 12 * i + 6 * k + 18)
                    pair_weights(2 * i + k + 4, k)
                    next_experts(2 * EPP * i + EPP * (k + 1), (k + 1) % 2)
            next_experts(EPP * (LOOPED - 1), 1)
            sp.wait_ge(ex_y, E0)
            for s in range(SETS):
                sp.wait_ge(y_stored[s], 16 * E0 // SETS)
            for dst, name in ((w_qkvg, "w_qkvg"), (w_o1, "w_o1"), (a13, "a13"), (w13, "w13")):
                sp.dma_start(dst, t[name]).then_inc(w3_in, 16)
            sp.wait_ge(blk_count, 2 * (NB - 1))
            sp.wait_ge(rest_count, 2 * (NB - 1))
            sp.dma_start(b13, t["b13"]).then_inc(b13_in, 16)
            sp.wait_ge(bl_q, GROUPS * HG)
            sp.wait_ge(bl_s, GROUPS * HG)
            for dst, name in ((w2, "w2"), (a2, "a2"), (b2, "b2")):
                sp.dma_start(dst, t[name]).then_inc(w2_in, 16)
            for i in range(NT):
                sp.wait_ge(y_done, i + 1)
                sp.dma_start(y[i * P:(i + 1) * P, :], acc[:, i, :]).then_inc(stored, 16)
            sp.wait_ge(stored, 16 * NT)

        @block.gpsimd
        def _(pool):
            pool.memset(zeros, 0.0).then_inc(zero_set, 1)
            for i in range(NT):
                pool.wait_ge(xn_done, i + 1)
                pool.tensor_tensor(acc[:, i, :], acc[:, i, :], xn[:, i, :], ALU.add).then_inc(acc_done, 1)
            for u in range(2 * NF):
                pool.wait_ge(sh_act, 2 * u + 2)
                pool.tensor_tensor(hT[:, u // 2, (u % 2) * CH:(u % 2 + 1) * CH], sgate[:, u % 2, :], sup[:, u % 2, :],
                                   ALU.mult).then_inc(sh_h, 1)

            def split_rope(i, before):
                pool.wait_ge(pair_in[i], 64 * before + 64)
                nothing = zeros.rearrange("p (g c) -> p g c", g=2)
                for k, hi, lo in ((0, w_hi[i], w_lo[i]), (1, w_rhi[i], w_rlo[i])):
                    raw = rope_raw[i][:, k, :].rearrange("p (g c) -> p g c", g=2)
                    pool.tensor_tensor(r(rope(hi)), raw, nothing, ALU.add).then_inc(rope_split, 1)
                for n, (k, hi, lo) in enumerate(((0, w_hi[i], w_lo[i]), (1, w_rhi[i], w_rlo[i]))):
                    raw = rope_raw[i][:, k, :].rearrange("p (g c) -> p g c", g=2)
                    pool.wait_ge(rope_split, 4 * (2 * before + i) + 1 + n)
                    pool.tensor_tensor(r(rope(lo)), raw, rope(hi), ALU.subtract).then_inc(rope_split, 1)

            for p in range(2):
                split_rope(p, 0)
            pool.wait_ge(rt_dest, 2)
            pool.wait_ge(zero_in, 16)
            for j in range(NT * TOPK0):
                pool.indirect_dma_start(buf[:, :], bass.IndirectOffsetOnAxis(ap=dest[:, j:j + 1], axis=0),
                                        x2[:, j // TOPK0, :], None, bounds_check=E0 * CAP - 1, oob_is_err=False)\
                    .then_inc(scattered, 16)
            pool.sem_inc(ye_free, SETS)

            def store(e, s, before):
                pool.wait_ge(ex_y, e + 1)
                pool.dma_start(res[bass.ds(e * CAP, CAP), :], ye[:, s, :]).then_inc(y_stored[s], 16)
                pool.wait_ge(y_stored[s], 16 * before + 16)
                pool.sem_inc(ye_free, 1)

            with pool.Fori(0, LOOPED // 2) as i:
                for k in range(2):
                    split_rope(k, i + 1)
                    for j in range(EPP):
                        store(2 * EPP * i + EPP * k + j, (k + j) % 2, EPP * i + EPP // 2 * k + (k + j) // 2)
            for e in range(EPP * LOOPED, E0):
                store(e, e % 2, e // 2)
            for s in range(SETS):
                pool.wait_ge(y_stored[s], 16 * E0 // SETS)
            for i in range(NT):
                if i == LATE:
                    pool.wait_ge(at_pv, PAIRS * UNITS)
                for k in range(TOPK0):
                    j = i * TOPK0 + k
                    pool.indirect_dma_start(picked[:, TILE_AT[i] * TOPK0 + k, :], None, res[:, :],
                                            bass.IndirectOffsetOnAxis(ap=source[:, j:j + 1], axis=0),
                                            bounds_check=E0 * CAP - 1, oob_is_err=False).then_inc(gathered[i], 16)

            pool.wait_ge(op_mm, NT)
            pool.memset(kmean, 0.0).then_inc(kmean_set, 1)
            for i in range(NT):
                pool.wait_ge(rope_mul, 3 * i + 3)
                pool.tensor_tensor(qk_tok[:, i, :], rope_tmp[:, i % 2, 0, :], rope_tmp[:, i % 2, 1, :], ALU.add)\
                    .then_inc(rope_add, 1)
            count(pool, rest_heads, beats_rest, rest_beats, rest_count)
            pool.wait_ge(fill_out, 16)
            pool.tensor_tensor(r(step_maskT), second_maskT, first_maskT, ALU.subtract).then_inc(step_mask, 1)
            for j in range(2):
                pool.tensor_tensor(am_first[j], am_step[j], first_maskT, ALU.mult).then_inc(low_rank, 1)
            pool.wait_ge(step_mask, 1)
            for j in range(2):
                pool.wait_ge(low_rank, j + 1)
                pool.tensor_tensor(am_step[j], am_step[j], step_maskT, ALU.mult).then_inc(low_rank, 1)
            pool.wait_ge(b13_in, 16)
            for h in range(2):
                pool.tensor_copy(r(b1_hi[h]), b13[:, h, 0:F1]).then_inc(b1_split, 1)
            for h in range(2):
                pool.wait_ge(b1_split, h + 1)
                pool.tensor_tensor(r(b1_lo[h]), b13[:, h, 0:F1], b1_hi[h], ALU.subtract).then_inc(b1_split, 1)
            pool.wait_ge(low_rank, 4)
            for c in range(TOK // CH):
                cols = slice(c * CH, (c + 1) * CH)
                at_least(pool, f_mm, 2 * NF1 * c)
                parts = ((am_first[0], am_first_hi, am_first_lo), (am_step[0], am_step_hi, am_step_lo))
                for whole_, hi, lo in parts:
                    pool.tensor_copy(r(hi), whole_[:, :, cols]).then_inc(am_split, 1)
                for n, (whole_, hi, lo) in enumerate(parts):
                    pool.wait_ge(am_split, 4 * c + n + 1)
                    pool.tensor_tensor(r(lo[:, :, cols]), whole_[:, :, cols], hi, ALU.subtract).then_inc(am_split, 1)

        @block.scalar
        def _(act):
            act.wait_ge(ln_var, 1)
            act.activation(sd, var, ACT.Sqrt).then_inc(ln_sd, 1)
            act.wait_ge(ms_var, 1)
            act.activation(sd2, ms, ACT.Sqrt).then_inc(ms_sd, 1)

            def turned_copy(g, dst):
                act.wait_ge(turned, g + 1)
                act.activation(dst[:, :, (g % 4) * 2 * P:(g % 4 + 1) * 2 * P],
                               bank[turn_bank(g)][:, :].rearrange("p (k n) -> p k n", k=KD), ACT.Copy)\
                    .then_inc(turned_out, 1)

            for g in range(4):
                turned_copy(g, xnT)
            for i in range(NT):
                act.wait_ge(lat_mm, i + 1)
                act.activation(lat[:, i, :], bank[4 + i % 2][:, 0:LATW], ACT.Copy).then_inc(lat_out, 1)
            for g in range(4, 8):
                turned_copy(g, x2T)
            act.wait_ge(lat_vr, 1)
            act.activation(lat_sd, lat_var, ACT.Sqrt).then_inc(lat_sdev, 1)
            act.wait_ge(rt_sub, 4)
            act.activation(expo, logit, ACT.Exp).then_inc(rt_exp, 1)
            act.activation(gate_e, gate_z, ACT.Exp, scale=-1.0).then_inc(rt_exp, 1)
            for u in range(2 * NF):
                act.wait_ge(sh_mm, u + 1)
                if u >= 2:
                    act.wait_ge(sh_h, u - 1)
                act.activation(sgate[:, u % 2, :], bank[2 * (u % 2)][:, :], ACT.Silu).then_inc(sh_act, 1)
                act.activation(sup[:, u % 2, :], bank[2 * (u % 2) + 1][:, :], ACT.Copy).then_inc(sh_act, 1)
            def expert_tanh(e, s):
                act.wait_ge(ex_g, e + 1)
                act.activation(e_act[0:FH, s], bank[1][0:FH, 0:2 * P].rearrange("p (f n) -> p f n", f=2), ACT.Tanh,
                               scale=0.5).then_inc(ex_act, 1)

            def experts_in(u, base, odd, count=EPP):
                for place in range(3):
                    j = GATES.get((u, place), count)
                    if j < count:
                        expert_tanh(base + j + 1, (odd + j + 1) % 2)

            def unit(p, u):
                g = UNITS * p + u
                if not (isinstance(g, int) and g < CONTEXT_LAG):
                    low_context(g - CONTEXT_LAG, (u - CONTEXT_LAG) % UNITS)
                if not (isinstance(g, int) and g < COPY_LAG):
                    copy_probsT(g - COPY_LAG, (u - COPY_LAG) % UNITS)
                act.wait_ge(at_min, g + 1)
                at_least(act, at_t, g - 3)
                for q in range(QT):
                    act.activation(probs[:, u % 4, q, :], bank[3 + u % 2][:, q * S:(q + 1) * S], ACT.Exp, scale=-1.0,
                                   bias=row_min[:, u % 4, q:q + 1], accum_out=row_sum[:, u % 4, q:q + 1])\
                        .then_inc(at_exp, 1)

            def normalise(g, slot):
                act.wait_ge(at_inv, g + 1)
                for q in range(QT):
                    ins = act.activation(probs[:, slot, q, :], probs[:, slot, q, :], ACT.Copy, scale=row_inv[:, slot, q:q + 1])
                ins.then_inc(at_norm, 1)

            def low_context(g, u):
                act.wait_ge(at_pv, g + 1)
                at_least(act, at_ctx, g - 1)
                act.activation(ctx_low[0:KVL, u % 2, :], bank[2 + 5 * (u % 2)][KVL:2 * KVL, 0:S], ACT.Copy).then_inc(at_cl, 1)

            def copy_probsT(g, slot):
                act.wait_ge(at_t, g + 1)
                at_least(act, at_pv, g - 1)
                act.activation(r(probs_hi[:, slot % 2]), bank[5 + slot % 2][:, :].rearrange("p (a b) -> p a b", a=QT),
                               ACT.Copy).then_inc(at_tout, 1)

            for u in range(UNITS):
                unit(0, u)
                if u == UNITS - 1:
                    expert_tanh(0, 0)
                if u:
                    normalise(u - 1, (u - 1) % 4)
            with act.Fori(0, LOOPED // 2) as i:
                for k in range(2):
                    for u in range(UNITS):
                        unit(2 * i + 1 + k, u)
                        experts_in(u, 2 * EPP * i + EPP * k, k)
                        normalise(UNITS * (2 * i + 1 + k) + u - 1, (u - 1) % 4)
            for u in range(UNITS):
                unit(PAIRS - 1, u)
                experts_in(u, E0 - 2, 0, 1)
                normalise(UNITS * (PAIRS - 1) + u - 1, (u - 1) % 4)
            G = PAIRS * UNITS
            normalise(G - 1, (G - 1) % 4)
            for g in range(G, G + CONTEXT_LAG):
                low_context(g - CONTEXT_LAG, (g - CONTEXT_LAG) % UNITS)
                if g - COPY_LAG < G:
                    copy_probsT(g - COPY_LAG, (g - COPY_LAG) % UNITS)

            act.wait_ge(cf_in, 16)
            for i in range(NT):
                act.wait_ge(ln_mv, NT + i + 1)
                act.activation(sd[:, i:i + 1], mv[:, i, 1:2], ACT.Sqrt, bias=table("eps_norm")).then_inc(l1_sd, 1)
                if i in (3, 5, 7):
                    turned_copy(8 + (i - 3) // 2, x1T)
            for i in range(NT):
                if i == 4:
                    turned_copy(11, x1T)
                act.wait_ge(qkv_mm, i + 1)
                src = bank[5 + 2 * (i % 2)]
                act.activation(v_tok[:, i, :], src[:, 0:D], ACT.Copy)
                act.activation(logit1[:, i, :], src[:, D:D + E1], ACT.Copy).then_inc(v_out, 1)
            for i in range(NT):
                act.wait_ge(qkT_mm, i + 1)
                act.activation(qkT[:, :, i * P:(i + 1) * P], bank[i % 4][:, :].rearrange("p (a n) -> p a n", a=4), ACT.Copy)\
                    .then_inc(qkT_out, 1)
            act.wait_ge(r1_sub, 1)
            act.activation(expo1, logit1, ACT.Exp).then_inc(r1_exp, 1)
            for n, (what, j, h, c) in enumerate(fills()):
                act.wait_ge(fill_mm, n + 1)
                cols = slice(c * CH, (c + 1) * CH)
                dst = {"low": am_step[j][:, h, cols], "mask": r((first_maskT, second_maskT)[j][:, h, cols]),
                       "share": shareT[:, j, cols]}[what]
                act.activation(dst, bank[4 + n % 4][:, :], ACT.Copy).then_inc(fill_out, 1)

            def unit1(g, u):
                copy_probs1T(g - 2, (u - 2) % HG)
                act.wait_ge(bl_min, 2 * g + 2)
                at_least(act, bl_t, g - 3)
                at_least(act, bl_inv, g - 3)
                for q, (a, b) in enumerate(((0, P), (P, 3 * P))):
                    act.activation(probs1[:, u % 4, a:b], masked[:, u % 4, a:b], ACT.Exp, scale=-1.0,
                                   bias=row_min[:, u % 4, q:q + 1], accum_out=row_sum[:, u % 4, q:q + 1])\
                        .then_inc(bl_exp, 1)

            def copy_probs1T(g, u):
                if isinstance(g, int) and g < 0:
                    return
                act.wait_ge(bl_t, g + 1)
                at_least(act, bl_v, g - 1)
                act.activation(probs1T[:, u % 2, :], bank[5 + u % 2][:, 0:3 * P], ACT.Copy).then_inc(bl_tout, 1)

            for u in range(HG):
                unit1(u, u)
            with act.Fori(0, GROUPS // 2 - 1) as i:
                for k in range(2):
                    for u in range(HG):
                        unit1(HG * (2 * i + 1 + k) + u, u)
            for u in range(HG):
                unit1(HG * (GROUPS - 1) + u, u)
            for g in range(GROUPS * HG - 2, GROUPS * HG):
                copy_probs1T(g, g % HG)
            act.wait_ge(bl_o, GROUPS * HG)
            act.activation(squares, o_tok.rearrange("p t (h d) -> p (t h) d", d=D1), ACT.Square).then_inc(on_sq, 1)
            act.wait_ge(on_step, 2)
            act.activation(o_sd, o_var, ACT.Sqrt).then_inc(on_sd, 1)
            m = 0
            for c in range(TOK // CH):
                for n, (f, k) in enumerate(uses()):
                    act.wait_ge(f_mm, m + 1)
                    at_least(act, f_x, m - 1)
                    act.activation(f_act[:, m % 2, :], bank[2 * (f % 3)][:, :], ACT.Silu).then_inc(f_silu, 1)
                    m += 1
                    if c == 0 and n == 4:
                        for g in range(12, 16):
                            turned_copy(g, oT)

        @block.vector
        def _(dve):
            for i in range(NT):
                dve.wait_ge(x_in[i // 2], 16)
                dve.bn_stats(stats[:, i, :], acc[:, i, :]).then_inc(ln_stats, 1)
            for i in range(NT):
                dve.wait_ge(ln_stats, i + 1)
                dve.bn_aggr(mv[:, i, :], stats[:, i, :]).then_inc(ln_mv, 1)
            dve.wait_ge(ln_mv, NT)
            dve.tensor_scalar(var, mv[:, :, 1], 1e-5, None, ALU.add).then_inc(ln_var, 1)
            dve.wait_ge(ln_sd, 1)
            dve.reciprocal(rstd, sd).then_inc(ln_rstd, 1)
            dve.wait_ge(ln_rstd, 1)
            dve.tensor_tensor(ms, mv[:, :, 1], rstd, ALU.mult).then_inc(ms_step, 1)
            for i in range(NT):
                dve.tensor_scalar(xn[:, i, :], acc[:, i, :], mv[:, i, 0:1], rstd[:, i:i + 1], ALU.subtract, ALU.mult)\
                    .then_inc(xn_done, 1)
                if i == 0:
                    dve.wait_ge(ms_step, 1)
                    dve.tensor_tensor(ms, ms, rstd, ALU.mult).then_inc(ms_step, 1)
                if i == 1:
                    dve.wait_ge(ms_step, 2)
                    dve.tensor_scalar(ms, ms, 1e-6, None, ALU.add).then_inc(ms_var, 1)
            dve.wait_ge(ms_sd, 1)
            dve.reciprocal(rrms, sd2).then_inc(ms_inv, 1)
            dve.wait_ge(ms_inv, 1)
            dve.wait_ge(rows_in, 16)
            for i in range(NT):
                dve.wait_ge(xn_done, i + 1)
                dve.scalar_tensor_tensor(x2[:, i, :], xn[:, i, :], rrms[:, i:i + 1], row("w_norm"), ALU.mult, ALU.mult)\
                    .then_inc(x2_done, 1)

            for i in range(NT):
                dve.wait_ge(lat_out, i + 1)
                dve.bn_stats(lat_stats[:, 2 * i, :], lat[:, i, 0:QL]).then_inc(lat_st, 1)
                dve.bn_stats(lat_stats[:, 2 * i + 1, :], lat[:, i, QL:QL + KVL]).then_inc(lat_st, 1)
            for i in range(2 * NT):
                dve.wait_ge(lat_st, i + 1)
                dve.bn_aggr(lat_mv[:, i, :], lat_stats[:, i, :]).then_inc(lat_ag, 1)
            dve.wait_ge(lat_ag, 2 * NT)
            dve.tensor_scalar(lat_var, lat_mv[:, :, 1], 1e-5, None, ALU.add).then_inc(lat_vr, 1)

            scores = [bank[6 + i][:, :].rearrange("p (t n) -> p t n", t=4) for i in range(2)]
            for i in range(2):
                dve.wait_ge(logit_mm, 4 * i + 4)
                dve.tensor_reduce(route_max[:, 4 * i:4 * i + 4], scores[i][:, :, 0:E0], AX.X, ALU.max).then_inc(rt_max, 1)
            for i in range(2):
                dve.wait_ge(rt_max, i + 1)
                dve.tensor_tensor(logit[:, 4 * i:4 * i + 4, :], scores[i][:, :, 0:E0],
                                  along(route_max[:, 4 * i:4 * i + 4], (2, E0)), ALU.subtract).then_inc(rt_sub, 1)
                dve.tensor_copy(gate_z[:, 4 * i:4 * i + 4], scores[i][:, :, E0]).then_inc(rt_sub, 1)

            dve.wait_ge(lat_sdev, 1)
            dve.reciprocal(lat_rstd, lat_sd).then_inc(lat_rs, 1)
            dve.wait_ge(lat_rs, 1)
            for i in range(NT):
                for j, a, b in ((2 * i, 0, QL), (2 * i + 1, QL, QL + KVL)):
                    dve.tensor_scalar(lat[:, i, a:b], lat[:, i, a:b], lat_mv[:, j, 0:1], lat_rstd[:, j:j + 1],
                                      ALU.subtract, ALU.mult).then_inc(lat_norm, 1)
            for q in range(QT):
                for name, a in (("k_cos", QL + KVL), ("k_sin", QL + KVL + DR)):
                    part = lat[:, q::QT, a:a + DR]
                    dve.tensor_tensor(part, part, along(table(name, QT, DR)[:, q, :], (1, B)), ALU.mult)\
                        .then_inc(lat_rope, 1)
            dve.wait_ge(lat_norm, 2 * NT)
            dve.tensor_tensor(lat[:, :, 0:QL + KVL], lat[:, :, 0:QL + KVL], along(row("lat_w"), (1, NT)), ALU.mult)\
                .then_inc(lat_scaled, 1)
            dve.wait_ge(lat_rope, 4)
            dve.tensor_tensor(kv_tok[:, :, KVL:2 * KVL], lat[:, :, QL + KVL:QL + KVL + DR], lat[:, :, QL + KVL + DR:LATW],
                              ALU.add).then_inc(lat_done, 1)
            dve.wait_ge(lat_scaled, 1)
            kv_b = along(row("lat_b")[:, QL:QL + KVL], (1, NT))
            for a in (0, 2 * KVL):
                dve.tensor_tensor(kv_tok[:, :, a:a + KVL], lat[:, :, QL:QL + KVL], kv_b, ALU.add).then_inc(lat_done, 1)
            dve.wait_ge(lat_done, 3)
            dve.tensor_tensor(lat[:, :, QL:QL + QL - P], lat[:, :, P:QL], along(row("lat_b")[:, P:QL], (1, NT)), ALU.add)\
                .then_inc(lat_done, 1)
            dve.wait_ge(lat_done, 4)
            dve.tensor_tensor(lat[:, :, 0:QL], lat[:, :, 0:QL], along(row("lat_b")[:, 0:QL], (1, NT)), ALU.add)\
                .then_inc(lat_done, 1)

            dve.wait_ge(rt_exp, 2)
            dve.tensor_reduce(route_sum, expo, AX.X, ALU.add).then_inc(rt_step, 1)
            dve.tensor_scalar(gate1, gate_e, 1.0, None, ALU.add).then_inc(rt_step, 1)
            dve.wait_ge(rt_step, 2)
            dve.reciprocal(route_inv, route_sum).then_inc(rt_step, 1)
            dve.reciprocal(gate, gate1).then_inc(rt_step, 1)
            dve.wait_ge(rt_step, 4)
            dve.tensor_tensor(prob, expo, along(route_inv, (2, E0)), ALU.mult).then_inc(rt_step, 1)
            dve.wait_ge(rt_step, 5)
            for i in range(NT):
                dve.max(top[:, i, :], prob[:, i, :]).then_inc(rt_step, 1)
            for i in range(NT):
                dve.wait_ge(rt_step, 6 + i)
                dve.max_index(top_at[:, i, :], top[:, i, :], prob[:, i, :]).then_inc(rt_step, 1)
            dve.wait_ge(rt_step, 5 + 2 * NT)
            dve.tensor_copy(chosen, top_at[:, :, 0:TOPK0]).then_inc(rt_step, 1)
            dve.wait_ge(rt_step, 6 + 2 * NT)
            flat = onehot.rearrange("p t k e -> p (t k) e")
            chosen_flat = chosen.rearrange("p t k -> p (t k)")
            dve.tensor_tensor(flat, along(table("iota"), (1, NT * TOPK0)), along(chosen_flat, (2, E0)), ALU.is_equal)\
                .then_inc(rt_step, 1)
            dve.wait_ge(rt_step, 7 + 2 * NT)
            dve.tensor_reduce(mask, onehot.rearrange("p t k e -> p t e k"), AX.X, ALU.add).then_inc(rt_step, 1)
            dve.wait_ge(rt_step, 8 + 2 * NT)
            dve.tensor_copy(maskb, mask).then_inc(rt_mask, 1)

            for i in range(NT):
                dve.wait_ge(latT_mm, i + 1)
                src = bank[4 + i % 2][:, :].rearrange("p (a n) -> p a n", a=4)
                cols, low = slice(i * P, (i + 1) * P), slice(QL - P, P)
                dve.tensor_copy(r(q_hi[:, cols]), src[:, 0, :]).then_inc(latT_out, 1)
                dve.tensor_copy(r(q_rest[:, cols]), src[:, 3, :]).then_inc(latT_out, 1)
                dve.tensor_copy(keys[:, :, cols], src[:, 1:3, :]).then_inc(latT_out, 1)
                dve.wait_ge(latT_out, 5 * i + 2)
                dve.tensor_tensor(r(q_lo[:, cols]), src[:, 0, :], q_hi[:, cols], ALU.subtract).then_inc(latT_out, 1)
                dve.tensor_tensor(r(q_rest[low, cols]), src[low, 3, :], q_rest[low, cols], ALU.subtract).then_inc(latT_out, 1)

            dve.wait_ge(rt_pos, 1)
            pos = bank[6][:, 0:NT * E0].rearrange("p (t e) -> p t e", e=E0)
            dve.tensor_tensor(onehot, onehot, along(pos, (2, TOPK0)), ALU.mult).then_inc(rt_step, 1)
            n = 9 + 2 * NT
            dve.wait_ge(rt_step, n)
            dve.tensor_reduce(place4, flat, AX.X, ALU.add).then_inc(rt_step, 1)
            dve.wait_ge(rt_step, n + 1)
            dve.tensor_scalar(over, place4, CAP - 0.5, None, ALU.is_gt).then_inc(rt_step, 1)
            dve.tensor_scalar(clipped, place4, CAP - 1.0, None, ALU.min).then_inc(rt_step, 1)
            dve.wait_ge(rt_step, n + 3)
            dve.scalar_tensor_tensor(source_f, chosen_flat, float(CAP), clipped, ALU.mult, ALU.add).then_inc(rt_step, 1)
            dve.scalar_tensor_tensor(weight4.rearrange("p (t k) -> p t k", k=TOPK0),
                                     over.rearrange("p (t k) -> p t k", k=TOPK0), 0.5, top[:, :, 0:TOPK0],
                                     ALU.is_lt, ALU.mult).then_inc(rt_step, 1)
            dve.wait_ge(rt_step, n + 5)
            dve.scalar_tensor_tensor(dest_f, over, 65536.0, source_f, ALU.mult, ALU.add).then_inc(rt_step, 1)
            dve.wait_ge(rt_step, n + 6)
            dve.tensor_copy(dest, dest_f).then_inc(rt_dest, 1)
            dve.tensor_copy(source, source_f).then_inc(rt_dest, 1)
            dve.wait_ge(rt_dest, 2)

            for i in range(NT):
                dve.wait_ge(sh_down, i + 1)
                dve.wait_ge(acc_done, i + 1)
                dve.scalar_tensor_tensor(acc[:, i, :], bank[i % 4][:, 0:D], gate[:, i:i + 1], acc[:, i, :],
                                         ALU.mult, ALU.add).then_inc(sh_add, 1)

            def rows_out(s):
                dve.tensor_copy(xeT[s], bank[1][:, 0:KD * P].rearrange("p (k n) -> p k n", k=KD)).then_inc(ex_tout, 1)

            def results_out(e, s, rows):
                dve.wait_ge(ex_done, e + 1)
                dve.wait_ge(ye_free, e + 1)
                dve.tensor_copy(ye[:, s, :], bank[1][:, KD * P:KD * P + D]).then_inc(ex_y, 1)
                if rows:
                    rows_out(1 - s)

            def hidden(e, s):
                dve.wait_ge(ex_act, e + 1)
                gate_up = bank[1][0:FH, :].rearrange("p (j f n) -> p j f n", j=2, f=2)
                dve.scalar_tensor_tensor(e_gu[0:FH, s], e_act[0:FH, s], 1.0, gate_up[:, 0], ALU.add, ALU.mult)\
                    .then_inc(ex_gu, 1)
                dve.wait_ge(ex_gu, e + 1)
                dve.scalar_tensor_tensor(e_hid[0:FH, s], e_gu[0:FH, s], 0.5, gate_up[:, 1], ALU.mult, ALU.mult)\
                    .then_inc(ex_h, 1)

            def experts_in(u, place, base, odd, count=EPP):
                j = TURNS.get((u, place), EPP)
                if j <= count and j < EPP:
                    results_out(base + j, (odd + j) % 2, j < count)
                j = HIDDEN.get((u, place), count)
                if j < count:
                    hidden(base + j + 1, (odd + j + 1) % 2)

            def effective_qk(p, i):
                dve.wait_ge(at_m, 2 * p + 1)
                at_least(dve, at_q, 6 * (p - 1))
                m = bank[0][:, :].rearrange("p (h k n) -> p h k n", h=2, k=2)[:, :, :, 0:KVL]
                for k, hi in ((0, w_hi[i]), (1, w_rhi[i])):
                    dve.tensor_copy(r(merged(hi)), m[:, :, k]).then_inc(at_split, 1)
                for k, hi, lo in ((0, w_hi[i], w_lo[i]), (1, w_rhi[i], w_rlo[i])):
                    dve.wait_ge(at_split, 2 * p + 1 + k)
                    ins = dve.tensor_tensor(r(merged(lo)), m[:, :, k], merged(hi), ALU.subtract)
                ins.then_inc(at_eff, 1)

            def effective_vo(p, where):
                dve.wait_ge(at_m, 2 * p + 2)
                for h in range(2):
                    rows_h = slice(h * KVL, (h + 1) * KVL)
                    ins = dve.tensor_copy(w_vo[rows_h, bass.ds(p, 1), :], where[rows_h, h * D:(h + 1) * D].unsqueeze(1))
                ins.then_inc(at_eff, 1)

            def queries(p, m, i, where):
                c, j = m // 3, m % 3
                half = slice(c * CH, (c + 1) * CH)
                dve.wait_ge(at_q, 6 * p + m + 1)
                at_least(dve, at_s, UNITS * (p - 1))
                at_least(dve, at_qe, 4 * p + 2 * c)
                name, dst = (("q_sin", q_tmp), ("q_even", qb[i][:, 0, half]), ("q_odd", qb[i][:, 1, half]))[j]
                dve.tensor_tensor(dst.rearrange("p (b s) -> p b s", s=S),
                                  where[:, :].rearrange("p (b s) -> p b s", s=S),
                                  along(table(name), (1, CH // S)), ALU.mult).then_inc(at_qrope, 1)
                if j == 2:
                    dve.wait_ge(at_qrope, 6 * p + m + 1)
                    dve.tensor_tensor(qb[i][DR:P, 0, half], qb[i][DR:P, 0, half], q_tmp[DR:P], ALU.add)\
                        .then_inc(at_qe, 1)
                    dve.tensor_tensor(qb[i][0:DR, 1, half], qb[i][0:DR, 1, half], q_tmp[0:DR], ALU.add)\
                        .then_inc(at_qe, 1)

            def minimum(g, u):
                dve.wait_ge(at_s, g + 1)
                at_least(dve, at_exp, 2 * g - 6)
                dve.tensor_reduce(row_min[:, u % 4, :], bank[3 + u % 2][:, :].rearrange("p (q n) -> p q n", q=QT),
                                  AX.X, ALU.min).then_inc(at_min, 1)

            def inverse_sum(g, u):
                dve.wait_ge(at_exp, 2 * g + 2)
                at_least(dve, at_norm, g - 3)
                dve.reciprocal(row_inv[:, u % 4, :], row_sum[:, u % 4, :]).then_inc(at_inv, 1)

            def low_probsT(g, u):
                dve.wait_ge(at_tout, g + 1)
                dve.tensor_tensor(r(probs_lo[:, u % 2]), bank[5 + u % 2][:, :].rearrange("p (a b) -> p a b", a=QT),
                                  probs_hi[:, u % 2], ALU.subtract).then_inc(at_lo, 1)

            def context(g, p, u):
                dve.wait_ge(at_cl, g + 1)
                b, h = u // 2, u % 2
                dve.tensor_tensor(ctxT[h * KVL:(h + 1) * KVL, bass.ds(p, 1), b * S:(b + 1) * S],
                                  bank[2 + 5 * h][0:KVL, 0:S].unsqueeze(1), ctx_low[0:KVL, h, :].unsqueeze(1), ALU.add)\
                    .then_inc(at_ctx, 1)

            def pair(p, i, first, last, experts):
                for u in range(UNITS):
                    g = UNITS * p + u
                    minimum(g, u)
                    if not (first and u < 1):
                        inverse_sum(g - 1, (u - 1) % UNITS)
                    experts(u, 0)
                    if not (first and u < COPY_LAG):
                        low_probsT(g - COPY_LAG, (u - COPY_LAG) % UNITS)
                    if not (first and u < CONTEXT_LAG):
                        context(g - CONTEXT_LAG, p - 1 if u < CONTEXT_LAG else p, (u - CONTEXT_LAG) % UNITS)
                    experts(u, 1)
                    if not last:
                        if u == 0:
                            effective_qk(p + 1, 1 - i)
                        elif u == 1:
                            effective_vo(p + 1, bank[0])
                        else:
                            queries(p + 1, u - 2, 1 - i, bank[0])
                    experts(u, 2)

            def first_expert(u, place):
                if (u, place) == FIRST_ROWS:
                    dve.wait_ge(ex_t, 1)
                    rows_out(0)
                if (u, place) == FIRST_HIDDEN:
                    hidden(0, 0)

            dve.tensor_copy(r(v_parts[:, :, 0:KVL]), kv_tok[:, :, 0:KVL]).then_inc(at_v, 1)
            dve.wait_ge(at_v, 1)
            dve.tensor_tensor(r(v_parts[:, :, KVL:2 * KVL]), kv_tok[:, :, 0:KVL], v_parts[:, :, 0:KVL], ALU.subtract)\
                .then_inc(at_v, 1)
            effective_qk(0, 0)
            effective_vo(0, bank[1])
            for m in range(6):
                queries(0, m, 0, bank[m % 2])
            pair(0, 0, True, False, first_expert)
            with dve.Fori(0, LOOPED // 2) as i:
                for k in range(2):
                    pair(2 * i + 1 + k, 1 - k, False, False,
                         lambda u, place: experts_in(u, place, 2 * EPP * i + EPP * k, k))
            pair(PAIRS - 1, 1, False, True, lambda u, place: experts_in(u, place, E0 - 2, 0, 1))
            G = PAIRS * UNITS
            inverse_sum(G - 1, UNITS - 1)
            for g in range(G, G + CONTEXT_LAG):
                if g - COPY_LAG < G:
                    low_probsT(g - COPY_LAG, (g - COPY_LAG) % UNITS)
                context(g - CONTEXT_LAG, PAIRS - 1, (g - CONTEXT_LAG) % UNITS)

            dve.wait_ge(sh_add, NT)

            def normal1(i):
                dve.wait_ge(l1_sd, i + 1)
                dve.reciprocal(rstd[:, i:i + 1], sd[:, i:i + 1]).then_inc(ln_rstd, 1)
                dve.wait_ge(ln_rstd, i + 2)
                dve.tensor_scalar(xn1[:, i, :], acc[:, i, :], mv[:, i, 0:1], rstd[:, i:i + 1], ALU.subtract, ALU.mult)\
                    .then_inc(xn_done, 1)

            for i in range(NT):
                dve.wait_ge(gathered[i], 16 * TOPK0)
                for k in range(TOPK0):
                    j = i * TOPK0 + k
                    if k:
                        dve.wait_ge(combined, j)
                    dve.scalar_tensor_tensor(acc[:, i, :], picked[:, TILE_AT[i] * TOPK0 + k, :], weight4[:, j:j + 1], acc[:, i, :],
                                             ALU.mult, ALU.add).then_inc(combined, 1)
                dve.wait_ge(op_mm, i + 1)
                dve.wait_ge(combined, TOPK0 * (i + 1))
                dve.tensor_tensor(acc[:, i, :], bank[i % 2][:, 0:D], acc[:, i, :], ALU.add).then_inc(op_add, 1)
                dve.wait_ge(op_add, i + 1)
                dve.bn_stats(stats[:, i, :], acc[:, i, :]).then_inc(ln_stats, 1)
                dve.wait_ge(ln_stats, NT + i + 1)
                dve.bn_aggr(mv[:, i, :], stats[:, i, :]).then_inc(ln_mv, 1)
                if i:
                    normal1(i - 1)
            normal1(NT - 1)

            for i in range(NT):
                dve.wait_ge(qkv_mm, i + 1)
                at_least(dve, rope_add, i - 1)
                src = bank[4 + 2 * (i % 2)][:, :].rearrange("p (h d) -> p h d", d=D1)
                cos_t = table("cos1", QT, D1)[:, i % QT, :]
                sin_t = table("sin1", QT, D1)[:, i % QT, :]
                by_cos = rope_tmp[:, i % 2, 0, :].rearrange("p (h d) -> p h d", d=D1)
                by_sin = rope_tmp[:, i % 2, 1, :].rearrange("p (h d) -> p h d", d=D1)
                half = D1 // 2
                dve.tensor_tensor(by_cos, src, along(cos_t, (1, 2 * H1)), ALU.mult).then_inc(rope_mul, 1)
                dve.tensor_tensor(by_sin[:, :, 0:half], src[:, :, half:D1], along(sin_t[:, 0:half], (1, 2 * H1)), ALU.mult)\
                    .then_inc(rope_mul, 1)
                dve.tensor_tensor(by_sin[:, :, half:D1], src[:, :, 0:half], along(sin_t[:, half:D1], (1, 2 * H1)), ALU.mult)\
                    .then_inc(rope_mul, 1)

            dve.wait_ge(v_out, NT)
            dve.tensor_reduce(max1, logit1, AX.X, ALU.max).then_inc(r1_step, 1)
            dve.wait_ge(r1_step, 1)
            dve.tensor_tensor(logit1, logit1, along(max1, (2, E1)), ALU.subtract).then_inc(r1_sub, 1)

            dve.wait_ge(qkT_out, NT)
            dve.tensor_reduce(kblock, qkT[:, 2:4, :].rearrange("p k (n c) -> p k n c", c=CHUNK), AX.X, ALU.add)\
                .then_inc(kmean_done, 1)
            dve.wait_ge(kmean_done, 1)
            dve.wait_ge(kmean_set, 1)
            for k in range(KD):
                for h in range(HG):
                    at = (k * HG + h) * NB
                    dve.tensor_scalar(kmean[:, k, :, at:at + NB], kblock[:, k, :].rearrange("p (b n) -> p b n", n=NB),
                                      table("head_mean")[:, h:h + 1], None, ALU.mult).then_inc(kmean_done, 1)

            dve.wait_ge(r1_exp, 1)
            dve.tensor_reduce(sum1, expo1, AX.X, ALU.add).then_inc(r1_step, 1)
            dve.wait_ge(r1_step, 2)
            dve.reciprocal(inv1, sum1).then_inc(r1_step, 1)
            dve.wait_ge(r1_step, 3)
            dve.tensor_tensor(prob1, expo1, along(inv1, (2, E1)), ALU.mult).then_inc(r1_step, 1)
            dve.wait_ge(r1_step, 4)
            for i in range(NT):
                dve.max(top1[:, i, :], prob1[:, i, :]).then_inc(r1_step, 1)
            for i in range(NT):
                dve.wait_ge(r1_step, 5 + i)
                dve.max_index(top1_at[:, i, :], top1[:, i, :], prob1[:, i, :]).then_inc(r1_step, 1)
            dve.wait_ge(r1_step, 4 + 2 * NT)
            dve.tensor_copy(chosen1, top1_at[:, :, 0:2]).then_inc(r1_step, 1)
            dve.tensor_tensor(sum1, top1[:, :, 0], top1[:, :, 1], ALU.add).then_inc(r1_step, 1)
            dve.wait_ge(r1_step, 6 + 2 * NT)
            dve.reciprocal(inv1, sum1).then_inc(r1_step, 1)

            for k in range(2):
                for i in range(NT):
                    dve.tensor_scalar(expert_of[k][:, i, :].rearrange("p (e r) -> p e r", r=R1),
                                      along(table("iota")[:, 0:E1], (2, R1)), chosen1[:, i, k:k + 1], None,
                                      ALU.is_equal).then_inc(r1_own, 1)
            dve.wait_ge(r1_step, 7 + 2 * NT)
            dve.tensor_tensor(share, top1[:, :, 0:2], along(inv1, (2, 2)), ALU.mult).then_inc(r1_step, 1)
            dve.wait_ge(r1_step, 8 + 2 * NT)
            for k in range(2):
                dve.tensor_copy(share_rep[:, k * NT:(k + 1) * NT, :], along(share[:, :, k], (2, P))).then_inc(r1_share, NT)

            g_b = score_blk.rearrange("p (b n) m -> p b (n m)", b=B)
            for i in range(2):
                dve.wait_ge(blk_mm, 4 * i + 4)
                dve.tensor_tensor(g_b[:, 2 * i:2 * i + 2, :], bank[i][:, :].rearrange("p (b n) -> p b n", b=2),
                                  along(table("keep"), (1, 2)), ALU.mult).then_inc(blk_step, 1)
            dve.tensor_copy(rank.rearrange("p t (h n) -> p (t h) n", n=NB), along(table("later"), (1, NT * H1))).then_inc(blk_step, 1)
            dve.wait_ge(blk_step, 2)
            dve.tensor_tensor(g_b, g_b, along(table("force"), (1, B)), ALU.add).then_inc(blk_step, 1)
            dve.wait_ge(blk_step, 4)
            for d in range(1, NB):
                compare(dve, first_heads, beats_first, blk_beats, d)

            count(dve, first_heads, beats_first, blk_beats, blk_count)

            def own_queries(G, b, k, u):
                at_least(dve, bl_s, HG * (G - 1))
                dve.tensor_scalar(q_head[k][:, u, :], qkT[:, k, bass.ds(b * S, S)], table("head_scale")[:, u:u + 1], None,
                                  ALU.mult).then_inc(bl_q, 1)

            def own_bias(G, b, k):
                at_least(dve, bl_min, 2 * HG * (G - 1))
                if not (isinstance(b, int) and b == 0):
                    dve.wait_ge(rest_count, 2 * (NB - 1))
                half = slice(k * HG * NB, (k + 1) * HG * NB)
                dve.tensor_scalar(bias_g[:, k], rank[:, bass.ds(QT * b, QT), half], TOPK1 - 0.5, BIG, ALU.is_gt, ALU.mult)\
                    .then_inc(bl_bias, 1)
                dve.wait_ge(bl_bias, 2 * G + 1)
                by_head = bias_g[:, k].rearrange("p q (u n) -> p q u n", n=NB)
                dve.tensor_tensor(by_head, by_head,
                                  along(table("future", QT, NB), (2, HG)), ALU.max)\
                    .then_inc(bl_bias, 1)

            def masked_minimum(g, G, k, u, meanwhile):
                dve.wait_ge(bl_s, g + 1)
                dve.wait_ge(bl_bias, 2 * G + 2)
                at_least(dve, bl_exp, 2 * g - 6)
                meanwhile()
                for q, (a, b) in enumerate(((0, P), (P, 3 * P))):
                    n = (b - a) // CHUNK
                    dve.tensor_tensor_reduce(
                        masked[:, u % 4, a:b].rearrange("p (n c) -> p n c", c=CHUNK),
                        bank[3 + u % 2][:, a:b].rearrange("p (n c) -> p n c", c=CHUNK),
                        along(bias_g[:, k, q, u * NB:u * NB + n], (2, CHUNK)), 1.0, HUGE, ALU.add, ALU.min,
                        row_min[:, u % 4, q:q + 1]).then_inc(bl_min, 1)

            def inverse(g, u):
                dve.wait_ge(bl_exp, 2 * g + 2)
                at_least(dve, bl_o, g - 3)
                dve.reciprocal(row_inv[:, u % 4, :], row_sum[:, u % 4, :]).then_inc(bl_inv, 1)

            def head_out(g, b, k, u):
                dve.wait_ge(bl_v, g + 1)
                dve.wait_ge(bl_inv, g + 1)
                h = (k * HG + u) * D1
                dve.tensor_tensor(o_tok[:, bass.ds(QT * b, QT), h:h + D1],
                                  bank[2 + 5 * (u % 2)][:, 0:2 * P].rearrange("p (q n) -> p q n", q=QT)[:, :, u * D1:(u + 1) * D1],
                                  along(row_inv[:, u % 4, :], (2, D1)), ALU.mult).then_inc(bl_o, 1)

            def group(G, b, k, before, after):
                if after is not None:
                    own_bias(G + 1, after, 1 - k)
                for u in range(HG):
                    g = HG * G + u
                    masked_minimum(g, G, k, u, lambda: own_queries(G + 1, after, 1 - k, u) if after is not None else None)
                    if u >= 4:
                        head_out(g - 4, b, k, u - 4)
                    elif before is not None:
                        head_out(g - 4, before, 1 - k, u + 4)
                    if u >= 2 or before is not None:
                        inverse(g - 2, (u - 2) % HG)
                    if before is None and u < NB - 1:
                        compare(dve, rest_heads, beats_rest, rest_beats, u + 1)

            own_bias(0, 0, 0)
            for u in range(HG):
                own_queries(0, 0, 0, u)
            group(0, 0, 0, None, 0)
            with dve.Fori(0, GROUPS // 2 - 1) as i:
                group(2 * i + 1, i, 1, i, i + 1)
                group(2 * i + 2, i + 1, 0, i, i + 1)
            group(GROUPS - 1, B - 1, 1, B - 1, None)
            G = GROUPS * HG
            inverse(G - 2, HG - 2)
            inverse(G - 1, HG - 1)
            for g in range(G - 4, G):
                head_out(g, B - 1, 1, g % HG)

            o_heads = o_tok.rearrange("p t (h d) -> p (t h) d", d=D1)
            o_var_f, o_inv_f = o_var.rearrange("p t h -> p (t h)"), o_inv.rearrange("p t h -> p (t h)")
            dve.wait_ge(on_sq, 1)
            dve.tensor_reduce(o_var_f, squares, AX.X, ALU.add).then_inc(on_step, 1)
            dve.wait_ge(on_step, 1)
            dve.tensor_scalar(o_var, o_var, 1.0 / D1, 1e-6, ALU.mult, ALU.add).then_inc(on_step, 1)
            dve.wait_ge(on_sd, 1)
            dve.reciprocal(o_inv, o_sd).then_inc(on_step, 1)
            dve.wait_ge(on_step, 3)
            dve.tensor_tensor(o_heads, o_heads, along(o_inv_f, (2, D1)), ALU.mult).then_inc(on_step, 1)
            dve.wait_ge(on_step, 4)
            dve.tensor_tensor(o_heads, o_heads, along(row("o_norm"), (1, NT * H1)), ALU.mult).then_inc(on_done, 2)

            m = 0
            for c in range(TOK // CH):
                cols = slice(c * CH, (c + 1) * CH)
                for f, k in uses():
                    dve.wait_ge(f_silu, m + 1)
                    dve.tensor_tensor(f_act[:, m % 2, :], f_act[:, m % 2, :], bank[2 * (f % 3) + 1][:, :], ALU.mult)\
                        .then_inc(f_h, 1)
                    dve.wait_ge(f_h, m + 1)
                    if k == 0:
                        at_least(dve, f_a2, c)
                        dve.tensor_tensor(h_first[:, f, :], f_act[:, m % 2, :], shareT[:, 0, cols], ALU.mult)\
                            .then_inc(f_x, 1)
                    else:
                        at_least(dve, f_down, 4 * c)
                        dve.tensor_tensor(h_both[:, f, :], f_act[:, m % 2, :], shareT[:, 1, cols], ALU.mult)\
                            .then_inc(f_x, 1)
                        dve.wait_ge(f_x, m + 1)
                        dve.tensor_tensor(h_both[:, f, :], h_both[:, f, :], h_first[:, f, :], ALU.add).then_inc(f_x2, 1)
                    m += 1
                dve.wait_ge(f_a2, c + 1)
                at_least(dve, f_down, 4 * c)
                for h in range(2):
                    at_least(dve, f_am2, 3 * (2 * c + h))
                    dve.tensor_tensor(am2_tmp, bank[4 + h][:, :], step_maskT[:, h, cols], ALU.mult).then_inc(f_am2, 1)
                    dve.tensor_tensor(am2[:, h, :], bank[6 + h][:, :], second_maskT[:, h, cols], ALU.mult).then_inc(f_am2, 1)
                    dve.wait_ge(f_am2, 3 * (2 * c + h) + 2)
                    dve.tensor_tensor(am2[:, h, :], am2[:, h, :], am2_tmp, ALU.subtract).then_inc(f_am2, 1)
                for i in range(4):
                    dve.wait_ge(f_down, 4 * c + i + 1)
                    dve.tensor_tensor(acc[:, 4 * c + i, :], bank[i][:, 0:D], acc[:, 4 * c + i, :], ALU.add)\
                        .then_inc(y_done, 1)

        @block.tensor
        def _(pe):
            def turn(g, src, ready):
                pe.wait_ge(ready, 2 * (g % 4) + 2)
                at_least(pe, turned_out, g - 3)
                for k in range(KD):
                    for i in range(2):
                        mm = pe.transpose(bank[g % 4][:, (2 * k + i) * P:(2 * k + i + 1) * P],
                                          src[:, 2 * (g % 4) + i, k * P:(k + 1) * P], ident)
                mm.then_inc(turned, 1)

            pe.wait_ge(cf_in, 16)
            for g in range(4):
                turn(g, xn, xn_done)
            pe.wait_ge(lat_in, 16)
            for i in range(NT):
                pe.wait_ge(turned_out, i // 2 + 1)
                at_least(pe, lat_out, i - 1)
                for k in range(KD):
                    mm = pe.matmul(bank[4 + i % 2][:, 0:LATW], xnT[:, k, i * P:(i + 1) * P], w_lat[:, k, :],
                                   start=(k == 0), stop=(k == KD - 1))
                mm.then_inc(lat_mm, 1)
            for g in range(4, 8):
                turn(g, x2, x2_done)
            pe.wait_ge(route_in, 16)
            for i in range(NT):
                pe.wait_ge(turned_out, 5 + i // 2)
                for k in range(KD):
                    mm = pe.matmul(bank[6 + i // 4][:, (i % 4) * P:(i % 4 + 1) * P], x2T[:, k, i * P:(i + 1) * P],
                                   w_route[:, k, :], start=(k == 0), stop=(k == KD - 1))
                mm.then_inc(logit_mm, 1)

            def shared_up(u):
                f, c = u // 2, u % 2
                at_least(pe, sh_act, 2 * u - 2)
                for j in range(2):
                    for k in range(KD):
                        mm = pe.matmul(bank[2 * (u % 2) + j][:, :],
                                       sw_up[:, k, (j * NF + f) * P:(j * NF + f + 1) * P],
                                       x2T[:, k, c * CH:(c + 1) * CH], start=(k == 0), stop=(k == KD - 1))
                mm.then_inc(sh_mm, 1)

            def latents_turn(i):
                at_least(pe, latT_out, 5 * (i - 1))
                dst = bank[4 + i % 2][:, :].rearrange("p (a n) -> p a n", a=4)
                pe.transpose(dst[:, 0, :], lat[:, i, 0:P], ident)
                pe.transpose(dst[:, 1, :], kv_tok[:, i, 0:2 * KVL], ident)
                pe.transpose(dst[:, 2, :], kv_tok[:, i, KVL:3 * KVL], ident)
                pe.transpose(dst[:, 3, :], lat[:, i, P:QL + QL - P], ident).then_inc(latT_mm, 1)

            pe.wait_ge(up_in, 16)
            for u in range(2 * NF):
                shared_up(u)
                if u >= 2 * NF - NT:
                    pe.wait_ge(lat_done, 5)
                    latents_turn(u - (2 * NF - NT))
                if u == 7:
                    pe.wait_ge(rt_mask, 1)
                    pe.wait_ge(cb_in, 16)
                    pe.matmul(bank[6][:, 0:NT * E0], tableb("before"), maskb.rearrange("p t e -> p (t e)"),
                              start=True, stop=False, skip_group_check=True)
                    for i in range(NT - 1):
                        mm = pe.matmul(bank[6][:, (i + 1) * E0:NT * E0].rearrange("p (t e) -> p t e", e=E0),
                                       tableb("ones"), along(maskb[:, i, :], (1, NT - 1 - i)),
                                       start=False, stop=(i == NT - 2), skip_group_check=True)
                    mm.then_inc(rt_pos, 1)
            pe.wait_ge(down_in, 16)
            pe.wait_ge(sh_act, 4 * NF)
            pe.wait_ge(sh_h, 2 * NF)
            for i in range(NT):
                at_least(pe, sh_add, i - 3)
                for f in range(NF):
                    mm = pe.matmul(bank[i % 4][:, 0:D], hT[:, f, i * P:(i + 1) * P], sw_down[:, f, :],
                                   start=(f == 0), stop=(f == NF - 1))
                mm.then_inc(sh_down, 1)

            def rows_turn(s, before):
                pe.wait_ge(eb_in[s], 16 * before + 16)
                for k in range(KD):
                    mm = pe.transpose(bank[1][:, k * P:(k + 1) * P], xe[:, s, k * P:(k + 1) * P], ident)
                return mm

            def gate_up(e, s, before):
                pe.wait_ge(ex_tout, e + 1)
                pe.wait_ge(ew_in[s], 16 * before + 16)
                for j in range(4):
                    for k in range(KD):
                        mm = pe.matmul(bank[1][0:FH, j * P:(j + 1) * P], w_gu[s][:, k, j * FH:(j + 1) * FH],
                                       xeT[s][:, k, :], start=(k == 0), stop=(k == KD - 1))
                mm.then_inc(ex_g, 1)

            def down(e, s, before):
                pe.wait_ge(ed_in[s], 16 * before + 16)
                for f in range(2):
                    mm = pe.matmul(bank[1][:, KD * P:KD * P + D], e_hid[0:FH, s, f, :], w_dn[s][0:FH, f, :],
                                   start=(f == 0), stop=(f == 1))
                mm.then_inc(ex_done, 1)

            def experts_in(u, place, base, before, odd, count=EPP):
                j = TURNS.get((u, place), EPP)
                if j <= count and j < EPP:
                    pe.wait_ge(ex_h, base + j + 1)
                    if j < count:
                        rows_turn((odd + j + 1) % 2, before + (odd + j + 1) // 2)
                    down(base + j, (odd + j) % 2, before + (odd + j) // 2)
                j = GATES.get((u, place), count)
                if j < count:
                    gate_up(base + j + 1, (odd + j + 1) % 2, before + (odd + j + 1) // 2)

            def first_expert(u, place):
                if (u, place) == FIRST_ROWS:
                    rows_turn(0, 0).then_inc(ex_t, 1)
                if (u, place) == FIRST_GATE:
                    gate_up(0, 0, 0)

            def merge_qk(p, i, turn_):
                pe.wait_ge(pair_in[i], 64 * turn_ + 64)
                at_least(pe, at_qrope, 6 * p)
                for h in range(2):
                    for k in range(2):
                        mm = pe.matmul(bank[0][:, (2 * h + k) * P:(2 * h + k + 1) * P], w_q[i][:, h, k * P:(k + 1) * P],
                                       w_vk[i][:, h, KVL:3 * KVL], start=True, stop=True)
                mm.then_inc(at_m, 1)

            def merge_vo(p, i, where):
                for h in range(2):
                    mm = pe.matmul(where[:, h * D:(h + 1) * D], w_vk[i][:, h, h * KVL:h * KVL + 2 * KVL], w_o[i][:, h, :],
                                   start=True, stop=True)
                mm.then_inc(at_m, 1)

            def project(p, m, i, where):
                c, part = m // 3, (2, 0, 1)[m % 3]
                if m == 0:
                    pe.wait_ge(rope_split, 4 * p + 4)
                half, cols = slice(c * CH, (c + 1) * CH), slice(part * P, (part + 1) * P)
                terms = ((w_hi, q_hi), (w_hi, q_lo), (w_lo, q_hi), (w_rhi, q_rest), (w_rlo, q_rest))
                for n, (w, q) in enumerate(terms):
                    mm = pe.matmul(where[:, :], r(w[i][:, cols]), r(q[:, half]), start=(n == 0), stop=(n == len(terms) - 1))
                mm.then_inc(at_q, 1)

            def scores(g, p, u, i):
                b, h = u // 2, u % 2
                pe.wait_ge(at_qe, 4 * p + 2 * (b // 2) + 2)
                at_least(pe, at_exp, 2 * g - 2)
                for q in range(QT):
                    mm = pe.matmul(bank[3 + u % 2][:, q * S:(q + 1) * S],
                                   qb[i][:, h, b * S + q * P:b * S + (q + 1) * P], keys[:, h, b * S:(b + 1) * S],
                                   start=True, stop=True)
                mm.then_inc(at_s, 1)

            def probs_turn(g, u):
                pe.wait_ge(at_norm, g + 1)
                at_least(pe, at_lo, g - 1)
                dst = bank[5 + u % 2][:, :].rearrange("p (k n) -> p k n", k=QT)
                for k in range(QT):
                    for q in range(QT):
                        mm = pe.transpose(dst[:, k, q * P:(q + 1) * P], probs[:, u % 4, q, k * P:(k + 1) * P], ident)
                mm.then_inc(at_t, 1)

            def values(g, u):
                b, h = u // 2, u % 2
                pe.wait_ge(at_lo, g + 1)
                at_least(pe, at_ctx, g - 1)
                terms = [(k, part) for part in (probs_hi, probs_lo) for k in range(QT)]
                for n, (k, part) in enumerate(terms):
                    mm = pe.matmul(bank[2 + 5 * h][:, 0:S], r(v_parts[:, QT * b + k, :]), r(part[:, u % 2, k, :]),
                                   start=(n == 0), stop=(n == len(terms) - 1))
                mm.then_inc(at_pv, 1)

            def pair(p, i, turn_, first, last, experts):
                for u in range(UNITS):
                    g = UNITS * p + u
                    scores(g, p, u, i)
                    experts(u, 0)
                    if not (first and u < TURN_LAG):
                        probs_turn(g - TURN_LAG, (u - TURN_LAG) % UNITS)
                    if not (first and u < VALUE_LAG):
                        values(g - VALUE_LAG, (u - VALUE_LAG) % UNITS)
                    experts(u, 1)
                    if not last:
                        if u == 0:
                            merge_qk(p + 1, 1 - i, turn_)
                        elif u == 1:
                            pe.wait_ge(at_eff, 2 * p + 3)
                            merge_vo(p + 1, 1 - i, bank[0])
                        else:
                            if u == 2:
                                pe.wait_ge(at_eff, 2 * p + 4)
                            else:
                                pe.wait_ge(at_qrope, 6 * p + 6 + u - 2)
                            project(p + 1, u - 2, 1 - i, bank[0])
                    experts(u, 2)

            pe.wait_ge(sh_add, NT)
            pe.wait_ge(latT_out, 5 * NT)
            merge_qk(0, 0, 0)
            merge_vo(0, 0, bank[1])
            for m in range(6):
                pe.wait_ge(at_eff, min(m + 1, 2))
                at_least(pe, at_qrope, m - 1)
                project(0, m, 0, bank[m % 2])
            pe.wait_ge(at_v, 2)
            pair(0, 0, 0, True, False, first_expert)
            with pe.Fori(0, LOOPED // 2) as i:
                for k in range(2):
                    pair(2 * i + 1 + k, 1 - k, i + 1, False, False,
                         lambda u, place: experts_in(u, place, 2 * EPP * i + EPP * k, EPP * i + EPP // 2 * k, k))
            pair(PAIRS - 1, 1, 0, False, True, lambda u, place: experts_in(u, place, E0 - 2, E0 // 2 - 1, 0, 1))
            G = PAIRS * UNITS
            for g in range(G, G + VALUE_LAG):
                if g - TURN_LAG < G:
                    probs_turn(g - TURN_LAG, (g - TURN_LAG) % UNITS)
                values(g - VALUE_LAG, (g - VALUE_LAG) % UNITS)

            def turn1(g, src, ready, n):
                pe.wait_ge(ready, n)
                at_least(pe, turned_out, g - 1)
                for k in range(KD):
                    for i in range(2):
                        mm = pe.transpose(bank[turn_bank(g)][:, (2 * k + i) * P:(2 * k + i + 1) * P],
                                          src[:, 2 * (g % 4) + i, k * P:(k + 1) * P], ident)
                mm.then_inc(turned, 1)

            for i in range(NT):
                pe.wait_ge(at_ctx, G - UNITS + 2 * (i // QT) + 2)
                at_least(pe, op_add, i - 1)
                for p in range(PAIRS):
                    mm = pe.matmul(bank[i % 2][:, 0:D], ctxT[:, p, i * P:(i + 1) * P], w_vo[:, p, :],
                                   start=(p == 0), stop=(p == PAIRS - 1))
                mm.then_inc(op_mm, 1)
                if i in (3, 5, 7):
                    g = 8 + (i - 3) // 2
                    turn1(g, xn1, xn_done, NT + 2 * (g % 4) + 2)

            pe.wait_ge(op_add, NT)
            pe.wait_ge(w3_in, 64)
            for i in range(NT):
                if i == 4:
                    turn1(11, xn1, xn_done, 2 * NT)
                pe.wait_ge(turned_out, 9 + i // 2)
                at_least(pe, rope_mul, 3 * (i - 1))
                at_least(pe, v_out, i - 1)
                for part, (a, b) in enumerate(((0, 2 * D), (2 * D, 3 * D + E1))):
                    for k in range(KD):
                        mm = pe.matmul(bank[4 + 2 * (i % 2) + part][:, 0:b - a], x1T[:, k, i * P:(i + 1) * P],
                                       w_qkvg[:, k, a:b], start=(k == 0), stop=(k == KD - 1))
                mm.then_inc(qkv_mm, 1)
            for i in range(NT):
                pe.wait_ge(rope_add, i + 1)
                at_least(pe, qkT_out, i - 3)
                for j in range(4):
                    mm = pe.transpose(bank[i % 4][:, j * P:(j + 1) * P], qk_tok[:, i, j * P:(j + 1) * P], ident)
                mm.then_inc(qkT_mm, 1)
            pe.wait_ge(rope_mul, 3 * NT)
            pe.wait_ge(v_out, NT)
            for n, (what, j, h, c) in enumerate(fills()):
                if n == 4:
                    pe.wait_ge(kmean_done, 1 + KD * HG)
                    for i in range(NT):
                        for k in range(KD):
                            mm = pe.matmul(bank[i // 4][:, (i % 4) * P:(i % 4 + 1) * P], qkT[:, k, i * P:(i + 1) * P],
                                           kmean[:, k, i // QT, :], start=(k == 0), stop=(k == KD - 1))
                        mm.then_inc(blk_mm, 1)
                at_least(pe, fill_out, n - 3)
                dst = bank[4 + n % 4]
                if what == "low":
                    for k in range(KD):
                        mm = pe.matmul(dst[:, :], a13[:, k, j * ER + h * P:j * ER + (h + 1) * P],
                                       x1T[:, k, c * CH:(c + 1) * CH], start=(k == 0), stop=(k == KD - 1))
                elif what == "mask":
                    pe.wait_ge(r1_own, NT * j + 4 * c + 4)
                    for i in range(4):
                        mm = pe.matmul(dst[:, i * P:(i + 1) * P], expert_of[j][:, 4 * c + i, h * P:(h + 1) * P], identb,
                                       start=True, stop=True)
                else:
                    pe.wait_ge(r1_share, 4 * (n - 16) + 4)
                    for i in range(4):
                        mm = pe.transpose(dst[:, i * P:(i + 1) * P], share_rep[:, 4 * (n - 16) + i, :], ident)
                mm.then_inc(fill_mm, 1)

            def scores1(g, b, k, u):
                pe.wait_ge(bl_q, g + 1)
                at_least(pe, bl_min, 2 * g - 2)
                dst = bank[3 + u % 2]
                keys = qkT[:, 2 + k, bass.ds(b * S, S)]
                pe.matmul(dst[:, 0:P], q_head[k][:, u, 0:P], qkT[:, 2 + k, bass.ds(b * S, P)], start=True, stop=False,
                          skip_group_check=True)
                pe.matmul(dst[:, 0:P], identb, tableb("causal"), start=False, stop=True, skip_group_check=True)
                pe.matmul(dst[:, P:3 * P], q_head[k][:, u, P:S], keys, start=True, stop=False, skip_group_check=True)
                pe.matmul(dst[:, 2 * P:3 * P], identb, tableb("causal"), start=False, stop=True, skip_group_check=True)\
                    .then_inc(bl_s, 1)

            def probs1_turn(g, u):
                pe.wait_ge(bl_exp, 2 * g + 2)
                at_least(pe, bl_tout, g - 1)
                for j in range(3):
                    mm = pe.transpose(bank[5 + u % 2][:, j * P:(j + 1) * P], probs1[:, u % 4, j * P:(j + 1) * P], ident)
                mm.then_inc(bl_t, 1)

            def values1(g, b, k, u):
                pe.wait_ge(bl_tout, g + 1)
                at_least(pe, bl_o, g - 1)
                dst = bank[2 + 5 * (u % 2)]
                v = [v_tok[:, bass.ds(QT * b + j, 1), k * P:(k + 1) * P].rearrange("p o n -> p (o n)") for j in range(QT)]
                pe.matmul(dst[:, 0:P], probs1T[:, u % 2, 0:P], v[0], start=True, stop=True)
                pe.matmul(dst[:, P:2 * P], probs1T[:, u % 2, P:2 * P], v[0], start=True, stop=False)
                pe.matmul(dst[:, P:2 * P], probs1T[:, u % 2, 2 * P:3 * P], v[1], start=False, stop=True).then_inc(bl_v, 1)

            def group(G, b, k, before):
                for u in range(HG):
                    g = HG * G + u
                    scores1(g, b, k, u)
                    if u >= 2:
                        probs1_turn(g - 2, u - 2)
                    elif before is not None:
                        probs1_turn(g - 2, u + HG - 2)
                    if u >= 3:
                        values1(g - 3, b, k, u - 3)
                    elif before is not None:
                        values1(g - 3, before, 1 - k, u + HG - 3)

            pe.wait_ge(fill_out, len(fills()))
            group(0, 0, 0, None)
            with pe.Fori(0, GROUPS // 2 - 1) as i:
                group(2 * i + 1, i, 1, i)
                group(2 * i + 2, i + 1, 0, i)
            group(GROUPS - 1, B - 1, 1, B - 1)
            G = GROUPS * HG
            probs1_turn(G - 2, HG - 2)
            values1(G - 3, B - 1, 1, HG - 3)
            probs1_turn(G - 1, HG - 1)
            values1(G - 2, B - 1, 1, HG - 2)
            values1(G - 1, B - 1, 1, HG - 1)

            def low_rank_part(dst, f, j, c, am, am_hi, am_lo):
                tile, cols = slice(f * P, (f + 1) * P), slice(c * CH, (c + 1) * CH)
                if j == 0:
                    terms = [pair_ for h in range(2) for pair_ in ((r(b1_hi[h][:, tile]), r(am_hi[:, h, :])),
                                                                  (r(b1_hi[h][:, tile]), r(am_lo[:, h, cols])),
                                                                  (r(b1_lo[h][:, tile]), r(am_hi[:, h, :])))]
                else:
                    terms = [(b13[:, h, F1 + f * P:F1 + (f + 1) * P], am[j][:, h, cols]) for h in range(2)]
                for n, (lhs, rhs) in enumerate(terms):
                    mm = pe.matmul(dst[:, :], lhs, rhs, start=False, stop=(n == len(terms) - 1), skip_group_check=True)
                return mm

            def hidden1(f, c, m):
                at_least(pe, f_h, m)
                for j in range(2):
                    dst, a = bank[2 * (f % 3) + j], j * F1 + f * P
                    for k in range(KD):
                        pe.matmul(dst[:, :], w13[:, k, a:a + P], x1T[:, k, c * CH:(c + 1) * CH], start=(k == 0), stop=False,
                                  skip_group_check=True)
                    mm = low_rank_part(dst, f, j, c, am_first, am_first_hi, am_first_lo)
                mm.then_inc(f_mm, 1)

            def hidden2(f, c, m):
                pe.wait_ge(f_h, m)
                for j in range(2):
                    mm = low_rank_part(bank[2 * (f % 3) + j], f, j, c, am_step, am_step_hi, am_step_lo)
                mm.then_inc(f_mm, 1)

            pe.wait_ge(low_rank, 4)
            pe.wait_ge(b1_split, 4)
            pe.wait_ge(bl_o, GROUPS * HG)
            m = 0
            for c in range(TOK // CH):
                if c:
                    pe.wait_ge(y_done, 4 * c)
                pe.wait_ge(am_split, 4 * c + 4)
                done = {}
                for n, (f, k) in enumerate(uses()):
                    if k == 0:
                        hidden1(f, c, done.get((f - 3, 1), m if f == 0 else 0))
                    else:
                        hidden2(f, c, done[f, 0])
                    m += 1
                    done[f, k] = m
                    if c == 0 and n == 4:
                        for g in range(12, 16):
                            turn1(g, o_tok, on_done, 2)
                pe.wait_ge(f_x2, NF1 * (c + 1) - 1)
                pe.wait_ge(w2_in, 48)
                at_least(pe, f_am2, 6 * c)
                for j, src in enumerate((h_first, h_both)):
                    for h in range(2):
                        for f in range(NF1):
                            if f == NF1 - 1:
                                pe.wait_ge(f_x2, NF1 * (c + 1))
                            mm = pe.matmul(bank[4 + 2 * j + h][:, :], a2[:, f, h * P:(h + 1) * P], src[:, f, :],
                                           start=(f == 0), stop=(f == NF1 - 1))
                mm.then_inc(f_a2, 1)
                pe.wait_ge(turned_out, 16)
                pe.wait_ge(f_h, m)
                for i in range(4):
                    terms = [(h_both[:, f, i * P:(i + 1) * P], w2[:, f, :]) for f in range(NF1)]
                    terms += [(oT[:, k, (4 * c + i) * P:(4 * c + i + 1) * P], w_o1[:, k, :]) for k in range(KD)]
                    terms += [(am2[:, h, i * P:(i + 1) * P], b2[:, h, :]) for h in range(2)]
                    for n, (lhs, rhs) in enumerate(terms):
                        if n == NF1 + KD:
                            pe.wait_ge(f_am2, 6 * c + 6)
                        mm = pe.matmul(bank[i][:, 0:D], lhs, rhs, start=(n == 0), stop=(n == len(terms) - 1))
                    mm.then_inc(f_down, 1)


def kernel(**inputs):
    import concourse.bacc as bacc
    from concourse.bass_utils import run_bass_kernel_spmd

    arrays = lay_out(inputs)
    nc = bacc.Bacc("TRN2", target_bir_lowering=False, num_devices=1)
    t = {name: nc.dram_tensor(f"in_{name}", a.shape, mybir.dt.from_np(a.dtype), kind="ExternalInput").ap()
         for name, a in arrays.items()}
    y = nc.dram_tensor("out", (TOK, D), F32, kind="ExternalOutput").ap()
    program(nc, t, y)
    r = run_bass_kernel_spmd(nc, [{f"in_{name}": a for name, a in arrays.items()}], core_ids=[0])
    return r.results[0]["out"].reshape(B, S, D)
```
